# Optimizing a Trainium2 kernel written in Bass

```python
import numpy as np
import jax
import jax.numpy as jnp

def _softmax(x, axis=-1):
    return jax.nn.softmax(x, axis=axis)

def _gelu(x):
    return jax.nn.gelu(x, approximate=True)

def _silu(x):
    return jax.nn.silu(x)

def _sigmoid(x):
    return jax.nn.sigmoid(x)

def _layernorm(x, axis=-1, eps=1e-05):
    m = jnp.mean(x, axis=axis, keepdims=True)
    v = jnp.var(x, axis=axis, keepdims=True)
    return (x - m) / jnp.sqrt(v + eps)

def _scatter_add(tgt, idx, src, axis=0):
    return tgt.at[idx].add(src)

def _segment_sum(src, seg, n):
    return jax.ops.segment_sum(src, seg, n)
kernel_name = 'mk_vit_tower_cls_d2_tok_img1024_r4_cae09f'

def setup_inputs(seed: int=0):
    np.random.seed(seed)
    _w = jnp.asarray

    def _rec_inputs():
        import jax
        import jax.numpy as jnp
        _rk = jax.random.key(seed)
        x = -0.00011082 + 0.999858 * jax.random.normal(jax.random.fold_in(_rk, 1), (4, 5, 128, 128), jnp.float32)
        cls_tok = 0.02 * jax.random.normal(jax.random.fold_in(_rk, 5), (1, 1, 256), jnp.float32)
        return (x, cls_tok)
    x, cls_tok = _rec_inputs()

    def _L0_tok_setup():
        import jax, jax.numpy as jnp
        import numpy as np
        PATCH = 8
        EPS = 1e-05

        def _patchify(x):
            B, C, H, Wd = x.shape
            p = PATCH
            x = x.reshape(B, C, H // p, p, Wd // p, p)
            x = x.transpose(0, 2, 4, 1, 3, 5)
            return x.reshape(B, H // p * (Wd // p), C * p * p)
        key = jax.random.key(seed)
        k1, k2 = jax.random.split(key)
        B, C, H, W_ = (32, 5, 128, 128)
        in_feat, embed_dim = (C * PATCH * PATCH, 256)
        x = jax.random.normal(k1, (B, C, H, W_), dtype=jnp.float32)
        W = jax.random.normal(k2, (in_feat, embed_dim), dtype=jnp.float32) * (1.0 / np.sqrt(in_feat))
        gamma = jnp.ones((embed_dim,), dtype=jnp.float32)
        return {'x': x, 'W': W, 'gamma': gamma}
    _L0_tok_all = _L0_tok_setup()
    _L0_tok_in = {k: v for k, v in _L0_tok_all.items() if k in ('W', 'gamma')}
    del _L0_tok_all

    def _L0_attn_setup():
        import jax, jax.numpy as jnp
        import numpy as np
        DIM = 256
        NH = 16
        HD = DIM // NH
        DROPE = 16
        MAXSEQ = 512
        LAT = 64
        BATCH = 2
        SEQ = 512

        def _rope_freqs(max_seq, head_dim):
            inv = 1.0 / 10000.0 ** (jnp.arange(0, head_dim, 2, dtype=jnp.float32) / head_dim)
            ang = jnp.arange(max_seq, dtype=jnp.float32)[:, None] * inv[None, :]
            return (jnp.cos(ang), jnp.sin(ang))

        def _apply_decoupled_rope(x, cosf, sinf, d_rope):
            b, d1, d2, hd = x.shape
            half = d_rope // 2
            xr = x[..., :d_rope].astype(jnp.float32).reshape(b, d1, d2, half, 2)
            xa, xb = (xr[..., 0], xr[..., 1])
            c = cosf[:d1, :half][None, :, None, :]
            s = sinf[:d1, :half][None, :, None, :]
            rot = jnp.stack([xa * c - xb * s, xa * s + xb * c], axis=-1)
            rot = rot.reshape(b, d1, d2, d_rope)
            return jnp.concatenate([rot, x[..., d_rope:]], axis=-1)
        key = jax.random.key(seed)
        ks = jax.random.split(key, 8)

        def w(k, o, i):
            return jax.random.normal(k, (o, i), jnp.float32) / np.sqrt(i).astype(np.float32)
        return {'x': jax.random.normal(ks[0], (BATCH, SEQ, DIM), jnp.float32), 'wq': w(ks[1], NH * HD, DIM), 'wk_a': w(ks[2], LAT, DIM), 'wk_b': w(ks[3], NH * HD, LAT), 'wv_a': w(ks[4], LAT, DIM), 'wv_b': w(ks[5], NH * HD, LAT), 'wo': w(ks[6], DIM, NH * HD)}
    _L0_attn_all = _L0_attn_setup()
    _L0_attn_in = {k: v for k, v in _L0_attn_all.items() if k in ('wq', 'wk_a', 'wk_b', 'wv_a', 'wv_b', 'wo')}
    del _L0_attn_all

    def _L0_ffn_setup():
        import jax, jax.numpy as jnp
        import numpy as np
        DIM = 256

        def _reference_tuple_inner(x, W_r, W_k, W_v, mu_r, mu_k):
            B, T, C = x.shape
            x_prev = jnp.concatenate([jnp.zeros((B, 1, C), x.dtype), x[:, :-1, :]], axis=1)
            xr = mu_r * x + (1.0 - mu_r) * x_prev
            xk = mu_k * x + (1.0 - mu_k) * x_prev
            r = jax.nn.sigmoid(jnp.einsum('btc,dc->btd', xr, W_r))
            k = jnp.einsum('btc,dc->btd', xk, W_k)
            k_act = jnp.square(jax.nn.relu(k))
            out = r * jnp.einsum('btc,dc->btd', k_act, W_v)
            new_state = x[:, -1, :]
            return (out, new_state)
        key = jax.random.key(seed)
        ks = jax.random.split(key, 6)
        B, T, C = (8, 512, DIM)
        x = jax.random.normal(ks[0], (B, T, C), dtype=jnp.float32)
        s = 1.0 / np.sqrt(C)
        W_r = jax.random.uniform(ks[1], (C, C), jnp.float32, -s, s)
        W_k = jax.random.uniform(ks[2], (C, C), jnp.float32, -s, s)
        W_v = jax.random.uniform(ks[3], (C, C), jnp.float32, -s, s)
        mu_r = jax.random.uniform(ks[4], (C,), jnp.float32)
        mu_k = jax.random.uniform(ks[5], (C,), jnp.float32)
        return {'x': x, 'W_r': W_r, 'W_k': W_k, 'W_v': W_v, 'mu_r': mu_r, 'mu_k': mu_k}
    _L0_ffn_all = _L0_ffn_setup()
    _L0_ffn_in = {k: v for k, v in _L0_ffn_all.items() if k in ('W_r', 'W_k', 'W_v', 'mu_r', 'mu_k')}
    del _L0_ffn_all

    def _L1_attn_setup():
        import jax, jax.numpy as jnp
        import numpy as np
        import math
        DIM = 256
        NUM_HEADS = 16
        HEAD_DIM = DIM // NUM_HEADS
        BATCH = 4
        SEQ = 1024

        def _feature_map(x, R):
            x = x / math.sqrt(HEAD_DIM)
            proj = jnp.einsum('bhnd,dm->bhnm', x, R)
            sq_norm = jnp.sum(x * x, axis=-1, keepdims=True)
            return jnp.exp(proj - 0.5 * sq_norm)
        key = jax.random.key(seed)
        ks = jax.random.split(key, 10)
        s = 1.0 / math.sqrt(DIM)
        return {'x': jax.random.normal(ks[0], (BATCH, SEQ, DIM), dtype=jnp.float32), 'Wq': jax.random.normal(ks[1], (DIM, DIM), dtype=jnp.float32) * s, 'bq': jax.random.normal(ks[2], (DIM,), dtype=jnp.float32) * 0.01, 'Wk': jax.random.normal(ks[3], (DIM, DIM), dtype=jnp.float32) * s, 'bk': jax.random.normal(ks[4], (DIM,), dtype=jnp.float32) * 0.01, 'Wv': jax.random.normal(ks[5], (DIM, DIM), dtype=jnp.float32) * s, 'bv': jax.random.normal(ks[6], (DIM,), dtype=jnp.float32) * 0.01, 'Wo': jax.random.normal(ks[7], (DIM, DIM), dtype=jnp.float32) * s, 'bo': jax.random.normal(ks[8], (DIM,), dtype=jnp.float32) * 0.01, 'R': jax.random.normal(ks[9], (HEAD_DIM, HEAD_DIM), dtype=jnp.float32) * 0.4}
    _L1_attn_all = _L1_attn_setup()
    _L1_attn_in = {k: v for k, v in _L1_attn_all.items() if k in ('Wq', 'bq', 'Wk', 'bk', 'Wv', 'bv', 'Wo', 'bo', 'R')}
    del _L1_attn_all

    def _L1_ffn_setup():
        import jax, jax.numpy as jnp
        import numpy as np
        D_MODEL = 256
        FFN = 256
        N_EXPERTS = 8
        N_SHARED = 1
        TOP_K = 2
        B, S = (2, 512)

        def _swiglu(h):
            a, b = jnp.split(h, 2, axis=-1)
            return jax.nn.silu(a) * b
        key = jax.random.key(seed)
        ks = jax.random.split(key, 12)
        sc = 0.02
        return {'x': jax.random.normal(ks[0], (B, S, D_MODEL), dtype=jnp.float32), 'gate_w': jax.random.normal(ks[1], (D_MODEL, N_EXPERTS), dtype=jnp.float32) * sc, 'gate_b': jnp.zeros((N_EXPERTS,), dtype=jnp.float32), 'sw1': jax.random.normal(ks[2], (N_SHARED, D_MODEL, 2 * FFN), dtype=jnp.float32) * sc, 'sb1': jnp.zeros((N_SHARED, 2 * FFN), dtype=jnp.float32), 'sw2': jax.random.normal(ks[3], (N_SHARED, FFN, D_MODEL), dtype=jnp.float32) * sc, 'sb2': jnp.zeros((N_SHARED, D_MODEL), dtype=jnp.float32), 'rw1': jax.random.normal(ks[4], (N_EXPERTS, D_MODEL, 2 * FFN), dtype=jnp.float32) * sc, 'rb1': jnp.zeros((N_EXPERTS, 2 * FFN), dtype=jnp.float32), 'rw2': jax.random.normal(ks[5], (N_EXPERTS, FFN, D_MODEL), dtype=jnp.float32) * sc, 'rb2': jnp.zeros((N_EXPERTS, D_MODEL), dtype=jnp.float32)}
    _L1_ffn_all = _L1_ffn_setup()
    _L1_ffn_in = {k: v for k, v in _L1_ffn_all.items() if k in ('gate_w', 'gate_b', 'sw1', 'sb1', 'sw2', 'sb2', 'rw1', 'rb1', 'rw2', 'rb2')}
    del _L1_ffn_all
    return {'x': x, 'cls_tok': cls_tok, 'L0_tok_W': _L0_tok_in['W'], 'L0_tok_gamma': _L0_tok_in['gamma'], 'L0_attn_wq': _L0_attn_in['wq'], 'L0_attn_wk_a': _L0_attn_in['wk_a'], 'L0_attn_wk_b': _L0_attn_in['wk_b'], 'L0_attn_wv_a': _L0_attn_in['wv_a'], 'L0_attn_wv_b': _L0_attn_in['wv_b'], 'L0_attn_wo': _L0_attn_in['wo'], 'L0_ffn_W_r': _L0_ffn_in['W_r'], 'L0_ffn_W_k': _L0_ffn_in['W_k'], 'L0_ffn_W_v': _L0_ffn_in['W_v'], 'L0_ffn_mu_r': _L0_ffn_in['mu_r'], 'L0_ffn_mu_k': _L0_ffn_in['mu_k'], 'L1_attn_Wq': _L1_attn_in['Wq'], 'L1_attn_bq': _L1_attn_in['bq'], 'L1_attn_Wk': _L1_attn_in['Wk'], 'L1_attn_bk': _L1_attn_in['bk'], 'L1_attn_Wv': _L1_attn_in['Wv'], 'L1_attn_bv': _L1_attn_in['bv'], 'L1_attn_Wo': _L1_attn_in['Wo'], 'L1_attn_bo': _L1_attn_in['bo'], 'L1_attn_R': _L1_attn_in['R'], 'L1_ffn_gate_w': _L1_ffn_in['gate_w'], 'L1_ffn_gate_b': _L1_ffn_in['gate_b'], 'L1_ffn_sw1': _L1_ffn_in['sw1'], 'L1_ffn_sb1': _L1_ffn_in['sb1'], 'L1_ffn_sw2': _L1_ffn_in['sw2'], 'L1_ffn_sb2': _L1_ffn_in['sb2'], 'L1_ffn_rw1': _L1_ffn_in['rw1'], 'L1_ffn_rb1': _L1_ffn_in['rb1'], 'L1_ffn_rw2': _L1_ffn_in['rw2'], 'L1_ffn_rb2': _L1_ffn_in['rb2']}

def reference(x, cls_tok, L0_tok_W, L0_tok_gamma, L0_attn_wq, L0_attn_wk_a, L0_attn_wk_b, L0_attn_wv_a, L0_attn_wv_b, L0_attn_wo, L0_ffn_W_r, L0_ffn_W_k, L0_ffn_W_v, L0_ffn_mu_r, L0_ffn_mu_k, L1_attn_Wq, L1_attn_bq, L1_attn_Wk, L1_attn_bk, L1_attn_Wv, L1_attn_bv, L1_attn_Wo, L1_attn_bo, L1_attn_R, L1_ffn_gate_w, L1_ffn_gate_b, L1_ffn_sw1, L1_ffn_sb1, L1_ffn_sw2, L1_ffn_sb2, L1_ffn_rw1, L1_ffn_rb1, L1_ffn_rw2, L1_ffn_rb2):
    import jax
    import jax.numpy as jnp

    def _L0_tok_ref(x, W, gamma):
        import jax, jax.numpy as jnp
        import numpy as np
        PATCH = 8
        EPS = 1e-05

        def _patchify(x):
            B, C, H, Wd = x.shape
            p = PATCH
            x = x.reshape(B, C, H // p, p, Wd // p, p)
            x = x.transpose(0, 2, 4, 1, 3, 5)
            return x.reshape(B, H // p * (Wd // p), C * p * p)
        tokens = _patchify(x)
        h = jnp.einsum('bnf,fd->bnd', tokens, W)
        mu = jnp.mean(h, axis=-1, keepdims=True)
        var = jnp.mean(jnp.square(h - mu), axis=-1, keepdims=True)
        out = (h - mu) * jax.lax.rsqrt(var + EPS) * gamma
        return out

    def _L0_attn_ref(x, wq, wk_a, wk_b, wv_a, wv_b, wo):
        import jax, jax.numpy as jnp
        import numpy as np
        DIM = 256
        NH = 16
        HD = DIM // NH
        DROPE = 16
        MAXSEQ = 512
        LAT = 64
        BATCH = 2
        SEQ = 512

        def _rope_freqs(max_seq, head_dim):
            inv = 1.0 / 10000.0 ** (jnp.arange(0, head_dim, 2, dtype=jnp.float32) / head_dim)
            ang = jnp.arange(max_seq, dtype=jnp.float32)[:, None] * inv[None, :]
            return (jnp.cos(ang), jnp.sin(ang))

        def _apply_decoupled_rope(x, cosf, sinf, d_rope):
            b, d1, d2, hd = x.shape
            half = d_rope // 2
            xr = x[..., :d_rope].astype(jnp.float32).reshape(b, d1, d2, half, 2)
            xa, xb = (xr[..., 0], xr[..., 1])
            c = cosf[:d1, :half][None, :, None, :]
            s = sinf[:d1, :half][None, :, None, :]
            rot = jnp.stack([xa * c - xb * s, xa * s + xb * c], axis=-1)
            rot = rot.reshape(b, d1, d2, d_rope)
            return jnp.concatenate([rot, x[..., d_rope:]], axis=-1)
        b, s, _ = x.shape
        q = (x @ wq.T).reshape(b, s, NH, HD).transpose(0, 2, 1, 3)
        k = (x @ wk_a.T @ wk_b.T).reshape(b, s, NH, HD).transpose(0, 2, 1, 3)
        v = (x @ wv_a.T @ wv_b.T).reshape(b, s, NH, HD).transpose(0, 2, 1, 3)
        cosf, sinf = _rope_freqs(MAXSEQ, HD)
        q = _apply_decoupled_rope(q, cosf, sinf, DROPE)
        k = _apply_decoupled_rope(k, cosf, sinf, DROPE)
        scores = jnp.einsum('bhqd,bhkd->bhqk', q, k) / np.float32(np.sqrt(HD))
        attn = jax.nn.softmax(scores, axis=-1)
        out = jnp.einsum('bhqk,bhkd->bhqd', attn, v)
        out = out.transpose(0, 2, 1, 3).reshape(b, s, NH * HD)
        return out @ wo.T

    def _L0_ffn_ref(x, W_r, W_k, W_v, mu_r, mu_k):
        import jax, jax.numpy as jnp
        import numpy as np
        DIM = 256

        def _reference_tuple_inner(x, W_r, W_k, W_v, mu_r, mu_k):
            B, T, C = x.shape
            x_prev = jnp.concatenate([jnp.zeros((B, 1, C), x.dtype), x[:, :-1, :]], axis=1)
            xr = mu_r * x + (1.0 - mu_r) * x_prev
            xk = mu_k * x + (1.0 - mu_k) * x_prev
            r = jax.nn.sigmoid(jnp.einsum('btc,dc->btd', xr, W_r))
            k = jnp.einsum('btc,dc->btd', xk, W_k)
            k_act = jnp.square(jax.nn.relu(k))
            out = r * jnp.einsum('btc,dc->btd', k_act, W_v)
            new_state = x[:, -1, :]
            return (out, new_state)
        return _reference_tuple_inner(x, W_r, W_k, W_v, mu_r, mu_k)[0]

    def _L1_attn_ref(x, Wq, bq, Wk, bk, Wv, bv, Wo, bo, R):
        import jax, jax.numpy as jnp
        import numpy as np
        import math
        DIM = 256
        NUM_HEADS = 16
        HEAD_DIM = DIM // NUM_HEADS
        BATCH = 4
        SEQ = 1024

        def _feature_map(x, R):
            x = x / math.sqrt(HEAD_DIM)
            proj = jnp.einsum('bhnd,dm->bhnm', x, R)
            sq_norm = jnp.sum(x * x, axis=-1, keepdims=True)
            return jnp.exp(proj - 0.5 * sq_norm)
        b, n, _ = x.shape
        h, d = (NUM_HEADS, HEAD_DIM)

        def split_heads(t):
            return t.reshape(b, n, h, d).transpose(0, 2, 1, 3)
        q = split_heads(x @ Wq.T + bq)
        k = split_heads(x @ Wk.T + bk)
        v = split_heads(x @ Wv.T + bv)
        q_prime = _feature_map(q, R)
        k_prime = _feature_map(k, R)
        kv = jnp.einsum('bhnd,bhne->bhde', k_prime, v)
        z = 1.0 / (jnp.sum(q_prime, axis=-1) + 1e-08)
        out = jnp.einsum('bhnd,bhde,bhn->bhne', q_prime, kv, z)
        out = out.transpose(0, 2, 1, 3).reshape(b, n, DIM)
        return out @ Wo.T + bo

    def _L1_ffn_ref(x, gate_w, gate_b, sw1, sb1, sw2, sb2, rw1, rb1, rw2, rb2):
        import jax, jax.numpy as jnp
        import numpy as np
        D_MODEL = 256
        FFN = 256
        N_EXPERTS = 8
        N_SHARED = 1
        TOP_K = 2
        B, S = (2, 512)

        def _swiglu(h):
            a, b = jnp.split(h, 2, axis=-1)
            return jax.nn.silu(a) * b
        hs = jnp.einsum('bsd,ndf->nbsf', x, sw1) + sb1[:, None, None, :]
        shared_out = jnp.einsum('nbsf,nfd->bsd', _swiglu(hs), sw2) + sb2.sum(0)
        probs = jax.nn.softmax(x @ gate_w + gate_b, axis=-1)
        topk_probs, topk_idx = jax.lax.top_k(probs, TOP_K)
        cw = jnp.sum(jax.nn.one_hot(topk_idx, N_EXPERTS, dtype=x.dtype) * topk_probs[..., None], axis=2)
        hr = jnp.einsum('bsd,edf->ebsf', x, rw1) + rb1[:, None, None, :]
        out_e = jnp.einsum('ebsf,efd->ebsd', _swiglu(hr), rw2) + rb2[:, None, None, :]
        routed_out = jnp.einsum('ebsd,bse->bsd', out_e, cw)
        return shared_out + routed_out
    h = _L0_tok_ref(x, L0_tok_W, L0_tok_gamma)
    h = jnp.concatenate([jnp.broadcast_to(cls_tok, (h.shape[0], 1, h.shape[2])), h], axis=1)
    h = h + _L0_attn_ref(_layernorm(h, axis=-1), L0_attn_wq, L0_attn_wk_a, L0_attn_wk_b, L0_attn_wv_a, L0_attn_wv_b, L0_attn_wo)
    h = h + _L0_ffn_ref(_layernorm(h, axis=-1), L0_ffn_W_r, L0_ffn_W_k, L0_ffn_W_v, L0_ffn_mu_r, L0_ffn_mu_k)
    h = h + _L1_attn_ref(_layernorm(h, axis=-1), L1_attn_Wq, L1_attn_bq, L1_attn_Wk, L1_attn_bk, L1_attn_Wv, L1_attn_bv, L1_attn_Wo, L1_attn_bo, L1_attn_R)
    h = h + _L1_ffn_ref(_layernorm(h, axis=-1), L1_ffn_gate_w, L1_ffn_gate_b, L1_ffn_sw1, L1_ffn_sb1, L1_ffn_sw2, L1_ffn_sb2, L1_ffn_rw1, L1_ffn_rb1, L1_ffn_rw2, L1_ffn_rb2)
    return h

_drawn_inputs = setup_inputs


def setup_inputs(seed=0):
    import zlib

    import numpy as np

    out = dict(_drawn_inputs(seed))
    spreads = {'L0_tok_gamma': (1.0, 0.2),
     'L1_ffn_gate_b': (0.0, 0.8),
     'L1_ffn_sb1': (0.0, 0.8),
     'L1_ffn_sb2': (0.0, 0.8),
     'L1_ffn_rb1': (0.0, 0.8),
     'L1_ffn_rb2': (0.0, 2.0)}
    factors = {'L0_ffn_W_r': 2.999,
     'L0_ffn_mu_r': 8.0,
     'L1_attn_bq': 52.135,
     'L1_attn_bk': 8.0,
     'L1_attn_bo': 46.09,
     'L1_ffn_gate_w': 8.0,
     'L1_ffn_sw1': 8.0,
     'L1_ffn_sw2': 8.0,
     'L1_ffn_rw1': 8.0,
     'L1_ffn_rw2': 8.0}
    for name, (base, spread) in spreads.items():
        noise = np.random.default_rng([zlib.crc32(name.encode()), seed]).standard_normal(out[name].shape)
        drawn = base * np.exp(spread * noise) if base else spread * noise
        out[name] = jnp.asarray(drawn.astype(out[name].dtype))
    for name, factor in factors.items():
        out[name] = (out[name] * factor).astype(out[name].dtype)
    return out
```

```python
from contextlib import ExitStack

import numpy as np

import concourse.bass as bass
from concourse import mybir

B = 4
T = 257
TP = 258
TC = 86
NC = 3
D = 256
NH = 16
HD = 16
KP = 107
NE = 8
EPS = 1e-5
F32 = mybir.dt.float32
F32R = mybir.dt.float32r
ALU = mybir.AluOpType
ACT = mybir.ActivationFunctionType
AX = mybir.AxisListType.X

W_COLS = {}
_at = 0
for _name, _n in (("lat", 2 * 128), ("q0", 2 * D), ("k0", D), ("v0", D), ("o0", 4 * D),
                  ("r", 2 * D), ("fk", 2 * D), ("fv", 2 * D),
                  ("q1", 2 * D), ("k1", 2 * D), ("v1", 2 * D), ("o1", 2 * D),
                  ("eb", D), ("gate", 2 * NE), ("sel", NE * 128)):
    W_COLS[_name] = (_at, _n)
    _at += _n
W_TOTAL = _at
EXPERT = 2 * 2 * D + 2 * D
PIECES = [("lat", "v0"), ("o0", "o0"), ("r", "fv"), ("q1", "k1"), ("v1", "o1"), ("eb", "sel")]
EARLY = 3

C_COLS = {}
_at = 0
for _name, _n in (("cos", D), ("sin", D), ("mask", 128), ("rbd", 128), ("ident", 128),
                  ("mu_r", 2), ("mu_k", 2), ("bq", 2), ("bk", 2), ("b1", 4 * (NE + 1))):
    C_COLS[_name] = (_at, _n)
    _at += _n
C_TOTAL = _at
R_COLS = {}
_at = 0
for _name, _n in (("gamma", D), ("bv", D), ("bo", D), ("gate_b", NE), ("before", NE * NE)):
    R_COLS[_name] = (_at, _n)
    _at += _n
R_TOTAL = _at


def walk():
    for b in range(B):
        yield ("tok", b)
        if b:
            yield ("tokn", b - 1)
            yield ("st", 0, b - 1)
    yield ("tokn", B - 1)
    yield ("st", 0, B - 1)

    def proj(b):
        yield ("ln", 0, b)
        yield ("xt", 0, b)
        yield ("lat", b)
        yield ("q", b)
        yield ("k", b)
        if b == 0:
            yield ("v", b)
        yield ("qsplit", 2 * b)
        yield ("qsplit", 2 * b + 1)

    yield ("split", 0)
    yield ("split", 1)
    yield from proj(0)
    for i in range(2 * B + 1):
        if i % 2 == 0 and i // 2 + 1 < B:
            yield from proj(i // 2 + 1)
        for u in range(12):
            if i < 2 * B:
                yield ("p1", i, u)
            if i > 0:
                yield ("p2", i - 1, u)
            if u == 8 and i > 0:
                yield ("pv", i - 1, 0)
                yield ("osplit", i - 1, 0)
            if u == 2 and i > 1:
                yield ("pv", i - 2, 1)
                yield ("osplit", i - 2, 1)
            if u == 4 and i > 2 and i % 2 == 1:
                yield ("wo", (i - 3) // 2)
                yield ("st", 1, (i - 3) // 2)
            if u == 5 and i % 2 == 1 and (i + 1) // 2 < B:
                yield ("v", (i + 1) // 2)
            if u == 6 and i == 2 * B - 2:
                yield ("split", 2)
            if u in (3, 9) and i == 2 * B - 1:
                yield ("split", 3 + u // 9)
        if i < 2 * B:
            yield ("mT", i)
    yield ("pv", 2 * B - 1, 1)
    yield ("osplit", 2 * B - 1, 1)
    yield ("wo", B - 1)
    yield ("st", 1, B - 1)

    for t in range(B + 1):
        if t < B:
            yield ("ln", 1, t)
            yield ("xt", 1, t)
            yield ("mix", t)
            yield ("split", 5 + t)
            yield ("r", t)
            yield ("fk", t)
        if t > 0:
            yield ("kv", t - 1)
            yield ("st", 2, t - 1)

    for t in range(B + 3):
        if 0 <= t - 3 < B:
            yield ("wo1", t - 3)
            yield ("st", 3, t - 3)
        if 0 <= t - 2 < B:
            yield ("kvm", t - 2)
        if t < B:
            yield ("ln", 2, t)
            yield ("xt", 2, t)
            yield ("q1", t)
            yield ("k1", t)
            yield ("v1", t)
            yield ("sq", t)
        if 0 <= t - 1 < B:
            yield ("ke", t - 1)
            yield ("qe", t - 1)
        if 0 <= t - 1 < B:
            yield ("kT", t - 1)
        if 0 <= t - 2 < B:
            yield ("z", t - 2)
            yield ("o", t - 2)
            yield ("o1split", t - 2)
    for t in range(B + 1):
        if t < B:
            yield ("ln", 3, t)
            yield ("xt", 3, t)
            yield ("xx", t)
            yield ("gate", t)
        if t > 0:
            yield ("cwT", t - 1)
        if t < 2:
            yield ("split", 9 + t)
    for b in range(B):
        for e in range(NE + 1):
            yield ("expert", b, e)
            if b == 0 and e < 4:
                yield ("split", 11 + e)


V_STEPS = {"tok", "xt", "lat", "p1", "mT", "pv", "wo", "kv", "v1", "kT", "kvm", "z", "o", "wo1", "gate", "cwT"}
A_STEPS = {"q", "k", "v", "p2", "r", "fk", "q1", "k1", "qe", "ke", "xx"}
V_NO = {s: n for n, s in enumerate(s for s in walk() if s[0] in V_STEPS)}
A_NO = {s: n for n, s in enumerate(s for s in walk() if s[0] in A_STEPS)}
ST_NO = {s: n for n, s in enumerate(s for s in walk() if s[0] in ("tok", "st"))}
LN_NO = {s: n for n, s in enumerate(s for s in walk() if s[0] == "ln")}


def tower(nc, xp, w_tok, rows, cls_rows, consts, weights, experts, out):
    ctx = ExitStack()

    def sb(where, name, shape, dt=F32):
        return where.enter_context(nc.sbuf_tensor(name, shape, dt))

    stage = sb(ctx, "stage", [128, 2, EXPERT])
    cst = sb(ctx, "cst", [128, C_TOTAL])
    row = sb(ctx, "row", [TC, R_TOTAL])
    cls = sb(ctx, "cls", [TC, D])
    neg = sb(ctx, "neg", [128, 128])
    rbd = sb(ctx, "rbd", [128, 128])
    eps = sb(ctx, "eps", [128, 1])
    st = sb(ctx, "st", [TC, NC, 6])
    mv = sb(ctx, "mv", [TC, len(ST_NO), NC, 2])
    lnv = sb(ctx, "lnv", [TC, len(ST_NO), NC])
    rstd = sb(ctx, "rstd", [TC, len(ST_NO), NC])
    g0 = ExitStack()
    X = sb(g0, "X", [TC, B, NC, D])
    xn = sb(g0, "xn", [TC, 2, NC, D])
    XTh = sb(g0, "XTh", [128, 2, 2, TP], F32R)
    XTl = sb(g0, "XTl", [128, 2, 2, TP], F32R)
    size0 = B * NC * D + 2 * NC * D + 8 * TP
    g0.close()
    g0 = ExitStack()
    es = sb(g0, "es", [128, 2, 2, TP])
    eg = sb(g0, "eg", [128, 2, TP])
    ehf = sb(g0, "ehf", [128, 2, TP])
    ehh = sb(g0, "ehh", [128, 2, 2, TP], F32R)
    ehl = sb(g0, "ehl", [128, 2, 2, TP], F32R)
    outb = sb(g0, "outb", [128, 2, 2, TP])
    g0.close()
    assert size0 >= 20 * TP
    sb(ctx, "room0", [128, size0])

    g1 = ExitStack()
    n_w0 = W_COLS["o0"][0]
    W0h = sb(g1, "W0h", [128, n_w0], F32R)
    W0l = sb(g1, "W0l", [128, n_w0], F32R)
    lath = sb(g1, "lath", [128, 2, TP], F32R)
    latl = sb(g1, "latl", [128, 2, TP], F32R)
    qf = sb(g1, "qf", [128, 2, 2, TP])
    wcos = sb(g1, "wcos", [128, 3, D])
    wsin = sb(g1, "wsin", [128, 3, D])
    mid0 = W_COLS["r"][0]
    n_mid = W_COLS["eb"][0] - mid0
    size1 = 2 * n_w0 + 8 * TP + 6 * D
    if size1 < 2 * n_mid:
        sb(g1, "room_mid", [128, 2 * n_mid - size1])
        size1 = 2 * n_mid
    g2 = ExitStack()
    Woh = sb(g2, "Woh", [128, 4 * D], F32R)
    Wol = sb(g2, "Wol", [128, 4 * D], F32R)
    qh = sb(g2, "qh", [128, 2, 2, TP], F32R)
    ql = sb(g2, "ql", [128, 2, 2, TP], F32R)
    Qst = sb(g2, "Qst", [68, 3, 8, TP], F32R)
    Kst = sb(g2, "Kst", [68, 3, 8, TP], F32R)
    Vt = sb(g2, "Vt", [TC, 2, NC, NH, 32])
    mx = sb(g2, "mx", [TC, 2, NC, 8])
    nm = sb(g2, "nm", [8, 2, 2, TP], F32R)
    den = sb(g2, "den", [128, TP])
    rec = sb(g2, "rec", [128, TP])
    of = sb(g2, "of", [128, 2, TP])
    oh = sb(g2, "oh", [128, 4, TP], F32R)
    ol = sb(g2, "ol", [128, 4, TP], F32R)
    gp_ = ExitStack()
    P = sb(gp_, "P", [TC, 2, 12, TP])
    gp_.close()
    xps = sb(gp_, "xps", [KP, NC, B, TP])
    wts = sb(gp_, "wts", [KP, NC, D])
    gp_.close()
    g2.close()
    g1.close()

    gm_ = ExitStack()
    Wmh = sb(gm_, "Wmh", [128, n_mid], F32R)
    Wml = sb(gm_, "Wml", [128, n_mid], F32R)
    if size1 > 2 * n_mid:
        sb(gm_, "room1", [128, size1 - 2 * n_mid])
    g3 = ExitStack()
    xf = sb(g3, "xf", [128, 2, TP + 1])
    dx = sb(g3, "dx", [128, 2, TP])
    xm = sb(g3, "xm", [128, 2, 2, TP])
    xmh = sb(g3, "xmh", [128, 2, 2, 2, TP], F32R)
    xml = sb(g3, "xml", [128, 2, 2, 2, TP], F32R)
    er = sb(g3, "er", [TC, 2, NC, D])
    sig = sb(g3, "sig", [TC, NC, D])
    kr = sb(g3, "kr", [128, 2, TP])
    ka = sb(g3, "ka", [128, 2, TP])
    kah = sb(g3, "kah", [128, 2, 2, TP], F32R)
    kal = sb(g3, "kal", [128, 2, 2, TP], F32R)
    g3.close()
    g4 = ExitStack()
    q1f = sb(g4, "q1f", [128, 2, 2, 2, TP])
    q1s = sb(g4, "q1s", [128, 2, 2, TP])
    q1e = sb(g4, "q1e", [128, 2, 2, 2, TP])
    v1t = sb(g4, "v1t", [TC, 2, NC, D])
    k1t = sb(g4, "k1t", [TC, 2, NC, D])
    kvb = sb(g4, "kvb", [128, 2, 128])
    zz = sb(g4, "zz", [128, 2, TP])
    zr = sb(g4, "zr", [128, 2, TP])
    o1f = sb(g4, "o1f", [128, 2, TP])
    o1h = sb(g4, "o1h", [128, 2, 2, TP], F32R)
    o1l = sb(g4, "o1l", [128, 2, 2, TP], F32R)
    size4 = 40 * TP + 4 * NC * D + 256
    g4.close()
    gm_.close()
    late_cols = 2 * (NE + 1 - EARLY) * EXPERT
    Wlh = sb(ctx, "Wlh", [128, NE + 1 - EARLY, EXPERT], F32R)
    Wll = sb(ctx, "Wll", [128, NE + 1 - EARLY, EXPERT], F32R)
    assert late_cols <= size1 + size4
    sb(ctx, "room2", [128, size1 + size4 - late_cols])
    Weh = sb(ctx, "Weh", [128, EARLY, EXPERT], F32R)
    Wel = sb(ctx, "Wel", [128, EARLY, EXPERT], F32R)
    n_eb = W_COLS["sel"][0] - W_COLS["eb"][0]
    Ebh = sb(ctx, "Ebh", [128, W_TOTAL - W_COLS["eb"][0]], F32R)
    Ebl = sb(ctx, "Ebl", [128, n_eb], F32R)
    XMh = sb(ctx, "XMh", [128, B, 2, TP], F32R)
    XMl = sb(ctx, "XMl", [128, B, 2, TP], F32R)
    XF = sb(ctx, "XF", [128, B, 2, TP])
    cwx = sb(ctx, "cwx", [128, B, TP], F32R)
    glog = sb(ctx, "glog", [TC, NC, NE])
    gm = sb(ctx, "gm", [TC, NC])
    gs = sb(ctx, "gs", [TC, NC])
    gr = sb(ctx, "gr", [TC, NC])
    rank = sb(ctx, "rank", [TC, NC, NE])
    ge = sb(ctx, "ge", [TC, 2, NC, NE])
    gp = sb(ctx, "gp", [TC, NC, NE])
    gt = sb(ctx, "gt", [TC, NC, NE * NE])
    gq = sb(ctx, "gq", [TC, NC, NE * NE])
    cw = sb(ctx, "cw", [TC, 2, NC, NE])

    psum = [ctx.enter_context(nc.psum_tensor(f"unit{n}", [128, 2, 512], F32)) for n in range(4)]
    V_UNIT, A_UNIT = psum[0:2], psum[2:4]
    ACC, UP_A, UP_B, CWB = psum

    scratch = nc.dram_tensor("qk_scratch", [B, 2, 2, D, TP], F32, kind="Internal").ap()
    scratch_m = nc.dram_tensor("max_scratch", [2 * B, 8, 2, TP], F32, kind="Internal").ap()

    def sem(name):
        return ctx.enter_context(nc.semaphore(name))

    s_xp = [sem(f"patches_in{b}") for b in range(B)]
    s_cst, s_wt = sem("constants_in"), sem("token_weights_in")
    s_stage = [sem(f"stage_in{n}") for n in range(2)]
    s_set = sem("constants_made")
    v_full, v_free = sem("v_full"), sem("v_free")
    a_full, a_free = sem("a_full"), sem("a_free")
    w_hi, w_lo = sem("weights_high"), sem("weights_low")
    stats, rstd_ok, xn_ok = sem("stats_ready"), sem("rstd_ready"), sem("normalised")
    lnv_ok = sem("log_var_ready")
    rot_ok, q_hi, q_lo = sem("weights_rotated"), sem("qk_high"), sem("qk_low")
    s_scr = [sem(f"qk_in_scratch{n}") for n in range(2)]
    s_stk = [sem(f"stack_in{n}") for n in range(3)]
    s_nmw = [sem(f"max_in_scratch{n}") for n in range(2)]
    s_mrow = [sem(f"max_rows_in{n}") for n in range(3)]
    o_hi, o_lo = sem("heads_high"), sem("heads_low")
    mix_ok, mix_hi, mix_lo = sem("mixed"), sem("mixed_high"), sem("mixed_low")
    kr_ok, ka_ok, ka_hi, ka_lo = sem("relu_ready"), sem("square_ready"), sem("square_high"), sem("square_low")
    sq_ok, bo_ok = sem("qk_squared"), sem("out_bias_added")
    o1_hi, o1_lo = sem("heads1_high"), sem("heads1_low")
    ge_ok, cw_ok = sem("gate_exp"), sem("expert_weights")
    dve_step = sem("vector_step")
    ma_full, ma_free = sem("up_a_full"), sem("up_a_free")
    mb_full, mb_free = sem("up_b_full"), sem("up_b_free")
    mc_full, mc_free = sem("token_weights_full"), sem("token_weights_free")
    h_ok, down_done, acc_free = sem("hidden_ready"), sem("down_done"), sem("out_ready")
    s_out = [sem(f"out_written{n}") for n in range(2)]
    block = ctx.enter_context(nc.Block())

    def cc(name):
        a, n = C_COLS[name]
        return cst[:, a:a + n]

    def rr(name):
        a, n = R_COLS[name]
        return row[:, a:a + n]

    def piece(p):
        if p < len(PIECES):
            a, (z, n) = W_COLS[PIECES[p][0]][0], W_COLS[PIECES[p][1]]
            n = z + n - a
            if p == 0:
                return n, W0h[:, a:a + n], W0l[:, a:a + n], n
            if p == 1:
                return n, Woh[:, :], Wol[:, :], n
            if p < 5:
                return n, Wmh[:, a - mid0:a - mid0 + n], Wml[:, a - mid0:a - mid0 + n], n
            return n, Ebh[:, :], Ebl[:, :], n_eb
        e = p - len(PIECES)
        h, l, e = (Weh, Wel, e) if e < EARLY else (Wlh, Wll, e - EARLY)
        return EXPERT, h[:, e, :], l[:, e, :], EXPERT

    LAST_PROJ = ("v", B - 1)
    GRAM = ("wo1", B - 1)

    @block.sync
    def _(sp):
        def load_piece(p):
            if p >= 2:
                sp.wait_ge(w_lo, p - 1)
            n = piece(p)[0]
            if p < len(PIECES):
                a = W_COLS[PIECES[p][0]][0]
                src = weights[:, a:a + n]
            else:
                src = experts[p - len(PIECES)]
            sp.dma_start(stage[:, p % 2, 0:n], src).then_inc(s_stage[p % 2], 16)

        def store_qk(r):
            b, k = r // 2, r % 2
            sp.wait_ge(q_lo, r + 1)
            for part, src in ((0, qh), (1, ql)):
                sp.dma_start(scratch[b, k, part].rearrange("(c p) t -> p c t", p=128),
                             src[:, r % 2].bitcast(F32)).then_inc(s_scr[k], 16)

        def load_stacks(i):
            b, c, s = i // 2, i % 2, i % 3
            for k in range(2):
                sp.wait_ge(s_scr[k], 32 * (b + 1))
            if i >= 3:
                sp.wait_ge(a_full, A_NO["p2", i - 3, 11] + 1)
            for k, dst, parts in ((0, Qst, (0, 1, 0, 1)), (1, Kst, (0, 0, 1, 1))):
                for g, part in enumerate(parts):
                    src = scratch[b, k, part, 128 * c:128 * c + 128].rearrange("(h d) t -> d h t", d=HD)
                    sp.dma_start(dst[HD * g:HD * g + HD, s].bitcast(F32), src).then_inc(s_stk[s], 16)

        def move_max(i):
            sp.wait_ge(v_free, V_NO["mT", i] + 1)
            sp.dma_start(scratch_m[i], nm[:, i % 2].bitcast(F32)).then_inc(s_nmw[i % 2], 16)
            sp.wait_ge(s_nmw[i % 2], 16 * (i // 2 + 1))
            sp.dma_start(Qst[66:68, i % 3].bitcast(F32),
                         scratch_m[i].rearrange("h r t -> r h t")).then_inc(s_mrow[i % 3], 16)

        sp.dma_start(wts[:, :, :], w_tok).then_inc(s_wt, 16)
        sp.dma_start(xps[:, :, 0, :], xp[:, :, 0, :]).then_inc(s_xp[0], 16)
        sp.dma_start(cst[:, :], consts).then_inc(s_cst, 16)
        sp.dma_start(row[:, :], rows.partition_broadcast(TC)).then_inc(s_cst, 16)
        sp.dma_start(cls[:, :], cls_rows).then_inc(s_cst, 16)
        load_piece(0)
        for b in range(1, B):
            sp.dma_start(xps[:, :, b, :], xp[:, :, b, :]).then_inc(s_xp[b], 16)
        load_piece(1)
        n_pieces = len(PIECES) + NE + 1
        loaded = 2
        for step in walk():
            kind = step[0]
            if kind == "qsplit":
                store_qk(step[1])
                if step[1] == 1:
                    load_stacks(0)
                    load_stacks(1)
                if step[1] == 3:
                    load_stacks(2)
            elif kind == "mT":
                move_max(step[1])
                if step[1] >= 1 and step[1] + 2 < 2 * B:
                    load_stacks(step[1] + 2)
            elif kind == "split" and loaded < n_pieces:
                load_piece(loaded)
                loaded += 1
        for b in range(B):
            sp.wait_ge(acc_free, b + 1)
            sp.dma_start(out[b].rearrange("(c p) t -> p c t", p=128), outb[:, b % 2]).then_inc(s_out[b % 2], 16)
        for n in range(2):
            sp.wait_ge(s_out[n], 16 * (B // 2))

    @block.tensor
    def _(pe):
        units = {"V": 0, "A": 0}

        def unit(step):
            ring = "V" if step[0] in V_STEPS else "A"
            n = units[ring]
            assert n == (V_NO if ring == "V" else A_NO)[step]
            if n >= 2:
                pe.wait_ge(v_free if ring == "V" else a_free, n - 1)
            units[ring] = n + 1
            return (V_UNIT if ring == "V" else A_UNIT)[n % 2]

        def exact(dst, lh, ll, rh, rl, first, last):
            pe.matmul(dst, lh, rh, start=first, stop=False)
            pe.matmul(dst, lh, rl, start=False, stop=False)
            return pe.matmul(dst, ll, rh, start=False, stop=last)

        def w(name, c, m=None):
            a, n = W_COLS[name]
            h, l = (W0h, W0l) if a < n_w0 else (Woh, Wol) if name == "o0" else (Wmh, Wml) if a < W_COLS["eb"][0] else (Ebh, Ebl)
            a -= 0 if a < n_w0 else n_w0 if name == "o0" else mid0 if a < W_COLS["eb"][0] else W_COLS["eb"][0]
            width = {"lat": 128, "gate": NE}.get(name, D)
            a += c * width
            if m is not None:
                a, width = a + 128 * m, 128
            return h[:, a:a + width], l[:, a:a + width]

        def tok(t):
            return slice(TC * t, TC * t + TC)

        def flat(u):
            return u[:, :, :].rearrange("p b n -> p (b n)")

        def transposes(u, src, step=None):
            for c in range(2):
                for t in range(NC):
                    ins = pe.transpose(u[:, c, tok(t)], src[:, t, 128 * c:128 * c + 128], cc("ident")[0:TC, 0:TC])
            return ins

        def token_major(u, lh, ll, name, halves=2):
            for t in range(NC):
                for c in range(halves):
                    ins = exact(flat(u)[0:TC, D * t:D * t + D], lh[:, c, tok(t)], ll[:, c, tok(t)],
                                *w(name, c), c == 0, c == halves - 1)
            return ins

        def feature_major(u, name, xh, xl, halves=2):
            for m in range(2):
                for c in range(halves):
                    ins = exact(u[:, m, 0:TP], *w(name, c, m), xh[:, c], xl[:, c], c == 0, c == halves - 1)
            return ins

        pe.wait_ge(s_wt, 16)
        for step in walk():
            kind = step[0]
            if kind == "tok":
                b = step[1]
                pe.wait_ge(s_xp[b], 16)
                u = unit(step)
                for t in range(NC):
                    for k in range(NC):
                        ins = pe.matmul(flat(u)[0:TC, D * t:D * t + D], xps[:, k, b, tok(t)], wts[:, k, :],
                                        start=k == 0, stop=k == NC - 1)
                ins.then_inc(v_full, 1)
            elif kind == "xt":
                _, s, b = step
                if LN_NO["ln", s, b] == 0:
                    pe.wait_ge(s_cst, 48)
                pe.wait_ge(xn_ok, LN_NO["ln", s, b] + 1)
                u = unit(step)
                transposes(u, xn[:, b % 2]).then_inc(v_full, 1)
            elif kind == "lat":
                b = step[1]
                if b == 0:
                    pe.wait_ge(w_lo, 1)
                pe.wait_ge(v_free, V_NO["xt", 0, b] + 1)
                u = unit(step)
                for c in range(2):
                    ins = exact(u[:, 0, 0:TP], *w("lat", c, 0), XTh[:, b % 2, c], XTl[:, b % 2, c], c == 0, c == 1)
                ins.then_inc(v_full, 1)
            elif kind == "q":
                b = step[1]
                u = unit(step)
                feature_major(u, "q0", XTh[:, b % 2], XTl[:, b % 2]).then_inc(a_full, 1)
            elif kind == "k":
                b = step[1]
                pe.wait_ge(v_free, V_NO["lat", b] + 1)
                u = unit(step)
                feature_major(u, "k0", lath[:, b % 2:b % 2 + 1], latl[:, b % 2:b % 2 + 1], 1).then_inc(a_full, 1)
            elif kind == "v":
                b = step[1]
                u = unit(step)
                token_major(u, lath[:, b % 2:b % 2 + 1], latl[:, b % 2:b % 2 + 1], "v0", 1).then_inc(a_full, 1)
            elif kind == "p1":
                _, i, n = step
                if n == 0:
                    pe.wait_ge(s_stk[i % 3], 128 * (i // 3 + 1))
                    if i < 3:
                        pe.wait_ge(s_set, 6)
                u = unit(step)
                for j in range(2):
                    h = 2 * (n % 4) + j
                    ins = pe.matmul(u[0:TC, j, 0:TP], Qst[0:66, i % 3, h, tok(n // 4)], Kst[0:66, i % 3, h, :],
                                    start=True, stop=True)
                ins.then_inc(v_full, 1)
            elif kind == "mT":
                i = step[1]
                pe.wait_ge(v_free, V_NO["p1", i, 11] + 1)
                u = unit(step)
                for t in range(NC):
                    ins = pe.transpose(u[0:8, 0, tok(t)], mx[:, i % 2, t, :], cc("ident")[0:TC, 0:TC])
                ins.then_inc(v_full, 1)
            elif kind == "p2":
                _, i, n = step
                if n == 0:
                    pe.wait_ge(s_mrow[i % 3], 16 * (i // 3 + 1))
                u = unit(step)
                for j in range(2):
                    h, t = divmod(2 * n + j, NC)
                    ins = pe.matmul(u[0:TC, j, 0:TP], Kst[0:68, i % 3, h, tok(t)], Qst[0:68, i % 3, h, :],
                                    start=True, stop=True)
                ins.then_inc(a_full, 1)
            elif kind == "pv":
                _, i, g = step
                b = i // 2
                pe.wait_ge(a_free, A_NO["p2", i, 6 * g + 5] + 1)
                u = unit(step)
                for t in range(NC):
                    kn = TC - (t == NC - 1)
                    for j in range(4):
                        ins = pe.matmul(u[32 * j:32 * j + 32, 0, 0:TP], Vt[0:kn, b % 2, t, 8 * (i % 2) + 4 * g + j, :],
                                        P[0:kn, g, NC * j + t, :], start=t == 0, stop=t == NC - 1,
                                        tile_position=(0, 32 * j))
                ins.then_inc(v_full, 1)
            elif kind == "wo":
                b = step[1]
                pe.wait_ge(o_lo, 4 * b + 4)
                u = unit(step)
                token_major(u, oh, ol, "o0", 4).then_inc(v_full, 1)
            elif kind in ("r", "fk"):
                b = step[1]
                if kind == "r":
                    if b == 0:
                        pe.wait_ge(w_lo, 3)
                    pe.wait_ge(mix_lo, b + 1)
                u = unit(step)
                if kind == "r":
                    ins = token_major(u, xmh[:, b % 2, 0], xml[:, b % 2, 0], "r")
                else:
                    ins = feature_major(u, "fk", xmh[:, b % 2, 1], xml[:, b % 2, 1])
                ins.then_inc(a_full, 1)
            elif kind == "kv":
                b = step[1]
                pe.wait_ge(ka_lo, b + 1)
                u = unit(step)
                token_major(u, kah[:, b % 2], kal[:, b % 2], "fv").then_inc(v_full, 1)
            elif kind in ("q1", "k1", "v1"):
                b = step[1]
                if kind == "q1":
                    if b == 0:
                        pe.wait_ge(w_lo, 5)
                    pe.wait_ge(v_free, V_NO["xt", 2, b] + 1)
                u = unit(step)
                if kind == "v1":
                    token_major(u, XTh[:, b % 2], XTl[:, b % 2], kind).then_inc(v_full, 1)
                else:
                    feature_major(u, kind, XTh[:, b % 2], XTl[:, b % 2]).then_inc(a_full, 1)
            elif kind in ("qe", "ke"):
                b, n = step[1], int(kind == "ke")
                if kind == "ke":
                    pe.wait_ge(sq_ok, b + 1)
                    pe.wait_ge(a_free, A_NO["k1", b] + 1)
                u = unit(step)
                for c in range(2):
                    pe.matmul(u[:, c, 0:TP], rbd[:, :], q1f[:, b % 2, n, c], start=True, stop=False)
                    ins = pe.matmul(u[:, c, 0:TP], neg[:, :], q1s[:, n, c], start=False, stop=True)
                ins.then_inc(a_full, 1)
            elif kind == "kT":
                b = step[1]
                pe.wait_ge(a_free, A_NO["ke", b] + 1)
                u = unit(step)
                for t in range(NC):
                    for c in range(2):
                        ins = pe.transpose(flat(u)[0:TC, D * t + 128 * c:D * t + 128 * c + 128],
                                           q1e[:, b % 2, 1, c, tok(t)], cc("ident"))
                ins.then_inc(v_full, 1)
            elif kind == "kvm":
                b = step[1]
                pe.wait_ge(v_free, V_NO["kT", b] + 1)
                u = unit(step)
                for c in range(2):
                    for t in range(NC):
                        kn = TC - (t == NC - 1)
                        ins = pe.matmul(u[:, c, 0:128], k1t[0:kn, b % 2, t, 128 * c:128 * c + 128],
                                        v1t[0:kn, b % 2, t, 128 * c:128 * c + 128], start=t == 0, stop=t == NC - 1)
                ins.then_inc(v_full, 1)
            elif kind == "z":
                b = step[1]
                pe.wait_ge(a_free, A_NO["qe", b] + 1)
                u = unit(step)
                for c in range(2):
                    ins = pe.matmul(u[:, c, 0:TP], cc("mask"), q1e[:, b % 2, 0, c], start=True, stop=True)
                ins.then_inc(v_full, 1)
            elif kind == "o":
                b = step[1]
                pe.wait_ge(v_free, V_NO["kvm", b] + 1)
                u = unit(step)
                for c in range(2):
                    ins = pe.matmul(u[:, c, 0:TP], kvb[:, c], q1e[:, b % 2, 0, c], start=True, stop=True)
                ins.then_inc(v_full, 1)
            elif kind == "wo1":
                b = step[1]
                pe.wait_ge(o1_lo, b + 1)
                u = unit(step)
                token_major(u, o1h[:, b % 2], o1l[:, b % 2], "o1").then_inc(v_full, 1)
            elif kind == "xx":
                b = step[1]
                pe.wait_ge(v_free, V_NO["wo1", b] + 1)
                u = unit(step)
                transposes(u, X[:, b]).then_inc(a_full, 1)
            elif kind == "gate":
                b = step[1]
                if b == 0:
                    pe.wait_ge(w_lo, 6)
                pe.wait_ge(v_free, V_NO["xt", 3, b] + 1)
                u = unit(step)
                for t in range(NC):
                    for c in range(2):
                        ins = exact(u[0:TC, 0, NE * t:NE * t + NE], XMh[:, b, c, tok(t)], XMl[:, b, c, tok(t)],
                                    *w("gate", c), c == 0, c == 1)
                ins.then_inc(v_full, 1)
            elif kind == "cwT":
                b = step[1]
                pe.wait_ge(cw_ok, b + 1)
                u = unit(step)
                for t in range(NC):
                    ins = pe.transpose(u[0:NE, 0, tok(t)], cw[:, b % 2, t, :], cc("ident")[0:TC, 0:TC])
                ins.then_inc(v_full, 1)
            elif kind == "expert":
                _, b, e = step
                n = (NE + 1) * b + e

                def down(b, e):
                    n = (NE + 1) * b + e
                    wh, wl = (Weh[:, e], Wel[:, e]) if e < EARLY else (Wlh[:, e - EARLY], Wll[:, e - EARLY])
                    if e == 0:
                        if b:
                            pe.wait_ge(acc_free, b)
                        for m in range(2):
                            bias_h, bias_l = w("eb", 0, m)
                            pe.matmul(ACC[:, m, 0:TP], bias_h, cwx[:, b, :], start=True, stop=False)
                            pe.matmul(ACC[:, m, 0:TP], bias_l, cwx[:, b, :], start=False, stop=False)
                    pe.wait_ge(h_ok, n + 1)
                    for m in range(2):
                        for c in range(2):
                            a = 4 * D + D * c + 128 * m
                            ins = exact(ACC[:, m, 0:TP], wh[:, a:a + 128], wl[:, a:a + 128],
                                        ehh[:, n % 2, c], ehl[:, n % 2, c], False, e == NE and c == 1)
                    ins.then_inc(down_done, 1)

                wh, wl = (Weh[:, e], Wel[:, e]) if e < EARLY else (Wlh[:, e - EARLY], Wll[:, e - EARLY])
                if n == 0:
                    pe.wait_ge(v_free, len(V_NO))
                    pe.wait_ge(a_free, len(A_NO))
                if b == 0:
                    pe.wait_ge(w_lo, len(PIECES) + e + 1)
                for up, full, free, at in ((UP_A, ma_full, ma_free, 0), (UP_B, mb_full, mb_free, D)):
                    if n:
                        pe.wait_ge(free, n)
                    for m in range(2):
                        for c in range(2):
                            a = 2 * D * c + at + 128 * m
                            ins = exact(up[:, m, 0:TP], wh[:, a:a + 128], wl[:, a:a + 128],
                                        XMh[:, b, c], XMl[:, b, c], c == 0, c == 1)
                    ins.then_inc(full, 1)
                if e:
                    nc_ = NE * b + e - 1
                    if nc_:
                        pe.wait_ge(mc_free, nc_)
                    a = W_COLS["sel"][0] - W_COLS["eb"][0] + 128 * (e - 1)
                    pe.matmul(CWB[:, 0, 0:TP], Ebh[:, a:a + 128], cwx[:, b, :], start=True, stop=True).then_inc(mc_full, 1)
                if n:
                    down((n - 1) // (NE + 1), (n - 1) % (NE + 1))
                if n == B * (NE + 1) - 1:
                    down(b, e)

    @block.scalar
    def _(act):
        def full(step):
            act.wait_ge(a_full, A_NO[step] + 1)
            return A_UNIT[A_NO[step] % 2]

        def flat(u):
            return u[:, :, :].rearrange("p b n -> p (b n)")

        act.preload_act_table_set("natural_log_exp_and_others")
        act.wait_ge(s_set, 1)
        for step in walk():
            kind = step[0]
            if kind == "split":
                p = step[1]
                n, hi, _, _ = piece(p)
                act.wait_ge(s_stage[p % 2], 16 * (p // 2 + 1))
                if p == 0:
                    act.wait_ge(rot_ok, 1)
                if p == 2:
                    act.wait_ge(a_full, A_NO["v", B - 1] + 1)
                    act.wait_ge(q_lo, 2 * B)
                if p == 5:
                    act.wait_ge(v_free, V_NO["wo", B - 1] + 1)
                if p == len(PIECES) + EARLY:
                    act.wait_ge(v_free, V_NO["wo1", B - 1] + 1)
                act.activation(hi, stage[:, p % 2, 0:n], ACT.Copy).then_inc(w_hi, 1)
            elif kind in ("tok", "st"):
                n = ST_NO[step]
                act.wait_ge(stats, n + 1)
                act.activation(lnv[:, n, :], mv[:, n, :, 1], ACT.Ln, bias=eps[0:TC, :]).then_inc(lnv_ok, 1)
                act.wait_ge(lnv_ok, n + 1)
                act.activation(rstd[:, n, :], lnv[:, n, :], ACT.Exp, scale=-0.5).then_inc(rstd_ok, 1)
            elif kind in ("q", "k"):
                b, r = step[1], 2 * step[1] + (kind == "k")
                u = full(step)
                if r >= 2:
                    act.wait_ge(q_lo, r - 1)
                act.activation(qf[:, r % 2], u[:, :, 0:TP], ACT.Copy).then_inc(a_free, 1)
            elif kind == "v":
                b = step[1]
                u = full(step)
                if b == 0:
                    act.wait_ge(s_set, 6)
                if b >= 2:
                    act.wait_ge(v_full, V_NO["pv", 2 * b - 3, 1] + 1)
                for t in range(NC):
                    ins = act.activation(Vt[:, b % 2, t, :, 0:HD],
                                         flat(u)[0:TC, D * t:D * t + D].rearrange("p (h d) -> p h d", d=HD), ACT.Copy)
                ins.then_inc(a_free, 1)
            elif kind == "qsplit":
                r = step[1]
                act.wait_ge(a_free, A_NO["qk"[r % 2], r // 2] + 1)
                if r >= 2:
                    act.wait_ge(s_scr[r % 2], 32 * (r // 2))
                act.activation(qh[:, r % 2], qf[:, r % 2], ACT.Copy).then_inc(q_hi, 1)
            elif kind == "p2":
                _, i, n = step
                g = n // 6
                u = full(step)
                if i == 0 and n == 0:
                    act.wait_ge(v_full, V_NO["tok", B - 1] + 1)
                if i and n % 6 == 0:
                    act.wait_ge(v_full, V_NO["pv", i - 1, g] + 1)
                k = 2 * n - 12 * g
                act.activation(P[:, g, k:k + 2, :], u[0:TC, :, 0:TP], ACT.Exp, scale=HD ** -0.5).then_inc(a_free, 1)
            elif kind == "osplit":
                _, i, g = step
                q = 2 * i + g
                act.wait_ge(v_free, V_NO["pv", i, g] + 1)
                if q % 4 == 0 and q:
                    act.wait_ge(v_full, V_NO["wo", i // 2 - 1] + 1)
                act.activation(oh[:, q % 4, :], of[:, q % 2, :], ACT.Copy).then_inc(o_hi, 1)
            elif kind == "mix":
                b = step[1]
                act.wait_ge(mix_ok, b + 1)
                if b >= 2:
                    act.wait_ge(a_full, A_NO["fk", b - 2] + 1)
                act.activation(xmh[:, b % 2].rearrange("p a c t -> p (a c t)"),
                               xm[:, :, :, :].rearrange("p a c t -> p (a c t)"), ACT.Copy).then_inc(mix_hi, 1)
            elif kind == "r":
                b = step[1]
                u = full(step)
                if b >= 2:
                    act.wait_ge(v_free, V_NO["kv", b - 2] + 1)
                act.activation(er[:, b % 2].rearrange("p t d -> p (t d)"), flat(u)[0:TC, 0:NC * D], ACT.Exp,
                               scale=-1.0).then_inc(a_free, 1)
            elif kind == "fk":
                b = step[1]
                u = full(step)
                if b:
                    act.wait_ge(ka_ok, b)
                act.activation(kr[:, :, :], u[:, :, 0:TP], ACT.Relu).then_inc(a_free, 1)
                act.wait_ge(a_free, A_NO[step] + 1)
                if b:
                    act.wait_ge(ka_lo, b)
                act.activation(ka[:, :, :], kr[:, :, :], ACT.Square).then_inc(ka_ok, 1)
                act.wait_ge(ka_ok, b + 1)
                if b >= 2:
                    act.wait_ge(v_full, V_NO["kv", b - 2] + 1)
                act.activation(kah[:, b % 2], ka[:, :, :], ACT.Copy).then_inc(ka_hi, 1)
            elif kind in ("q1", "k1"):
                b, n = step[1], int(kind == "k1")
                if b == 0 and n == 0:
                    act.wait_ge(v_free, V_NO["kv", B - 1] + 1)
                u = full(step)
                if b >= 2:
                    act.wait_ge(a_full, A_NO["qe", b - 2] + 1)
                for c in range(2):
                    bias = cc("bk" if n else "bq")[:, c:c + 1]
                    ins = act.activation(q1f[:, b % 2, n, c], u[:, c, 0:TP], ACT.Identity, bias=bias)
                ins.then_inc(a_free, 1)
            elif kind in ("qe", "ke"):
                b, n = step[1], int(kind == "ke")
                u = full(step)
                if b >= 2:
                    act.wait_ge(v_full, V_NO["o" if n == 0 else "kT", b - 2] + 1)
                act.activation(q1e[:, b % 2, n], u[:, :, 0:TP], ACT.Exp).then_inc(a_free, 1)
            elif kind == "o1split":
                b = step[1]
                act.wait_ge(v_free, V_NO["o", b] + 1)
                if b >= 2:
                    act.wait_ge(v_full, V_NO["wo1", b - 2] + 1)
                act.activation(o1h[:, b % 2], o1f[:, :, :], ACT.Copy).then_inc(o1_hi, 1)
            elif kind == "xx":
                b = step[1]
                u = full(step)
                act.activation(XF[:, b], u[:, :, 0:TP], ACT.Copy).then_inc(a_free, 1)
            elif kind == "gate":
                b = step[1]
                act.wait_ge(v_free, V_NO[step] + 1)
                act.activation(ge[:, b % 2], glog[:, :, :], ACT.Exp).then_inc(ge_ok, 1)
            elif kind == "expert":
                _, b, e = step
                n = (NE + 1) * b + e
                if n == 0:
                    act.wait_ge(v_full, len(V_NO))
                    act.wait_ge(a_full, len(A_NO))
                act.wait_ge(ma_full, n + 1)
                if n >= 2:
                    act.wait_ge(mb_free, n - 1)
                for m in range(2):
                    a = C_COLS["b1"][0] + 4 * e + m
                    ins = act.activation(es[:, n % 2, m], UP_A[:, m, 0:TP], ACT.Silu, bias=cst[:, a:a + 1])
                ins.then_inc(ma_free, 1)

    @block.gpsimd
    def _(pool):
        pool.memset(eps[:, :], EPS).then_inc(s_set, 1)
        pool.memset(Vt[:, :, :, :, HD:32], 0.0).then_inc(s_set, 1)
        pool.wait_ge(s_set, 2)
        pool.memset(Vt[:, :, :, :, HD:HD + 1], 1.0).then_inc(s_set, 1)
        pool.wait_ge(s_set, 3)
        pool.memset(Qst[64:68, :, :, :].bitcast(F32), 0.0).then_inc(s_set, 1)
        pool.wait_ge(s_set, 4)
        pool.memset(Kst[64:68, :, :, :].bitcast(F32), 1.0).then_inc(s_set, 1)
        pool.wait_ge(s_set, 5)
        pool.wait_ge(s_cst, 48)
        pool.tensor_scalar(neg[:, :], cc("mask"), -0.5 / HD, None, ALU.mult)
        pool.tensor_scalar(rbd[:, :], cc("rbd"), HD ** -0.5, None, ALU.mult).then_inc(s_set, 1)
        for step in walk():
            kind = step[0]
            if kind == "split":
                p = step[1]
                _, hi, lo, n = piece(p)
                pool.wait_ge(w_hi, p + 1)
                pool.tensor_tensor(lo, stage[:, p % 2, 0:n], hi[:, 0:n].bitcast(F32), ALU.subtract).then_inc(w_lo, 1)
                if p == 5:
                    pool.memset(cwx[:, :, :].bitcast(F32), 0.0).then_inc(s_set, 1)
                    pool.wait_ge(s_set, 7)
                    pool.memset(cwx[32:33, :, :].bitcast(F32), 1.0).then_inc(s_set, 1)
                    pool.wait_ge(s_set, 8)
            elif kind == "qsplit":
                r = step[1]
                pool.wait_ge(q_hi, r + 1)
                pool.tensor_tensor(ql[:, r % 2], qf[:, r % 2], qh[:, r % 2].bitcast(F32),
                                   ALU.subtract).then_inc(q_lo, 1)
            elif kind == "osplit":
                _, i, g = step
                q = 2 * i + g
                pool.wait_ge(o_hi, q + 1)
                pool.tensor_tensor(ol[:, q % 4, :], of[:, q % 2, :], oh[:, q % 4, :].bitcast(F32),
                                   ALU.subtract).then_inc(o_lo, 1)
            elif kind == "mix":
                b = step[1]
                pool.wait_ge(mix_hi, b + 1)
                pool.tensor_tensor(xml[:, b % 2].rearrange("p a c t -> p (a c t)"),
                                   xm[:, :, :, :].rearrange("p a c t -> p (a c t)"),
                                   xmh[:, b % 2].bitcast(F32).rearrange("p a c t -> p (a c t)"),
                                   ALU.subtract).then_inc(mix_lo, 1)
            elif kind == "fk":
                b = step[1]
                pool.wait_ge(ka_hi, b + 1)
                pool.tensor_tensor(kal[:, b % 2], ka[:, :, :], kah[:, b % 2].bitcast(F32), ALU.subtract).then_inc(ka_lo, 1)
            elif kind == "sq":
                b = step[1]
                pool.wait_ge(a_free, A_NO["k1", b] + 1)
                if b:
                    pool.wait_ge(a_full, A_NO["qe", b - 1] + 1)
                pool.tensor_tensor(q1s[:, :, :, :], q1f[:, b % 2], q1f[:, b % 2], ALU.mult).then_inc(sq_ok, 1)
                pool.wait_ge(xn_ok, LN_NO["ln", 2, b] + 1)
                pool.tensor_tensor(X[:, b], X[:, b], rr("bo").unsqueeze(1).broadcast_to([TC, NC, D]),
                                   ALU.add).then_inc(bo_ok, 1)
            elif kind == "o1split":
                b = step[1]
                pool.wait_ge(o1_hi, b + 1)
                pool.tensor_tensor(o1l[:, b % 2], o1f[:, :, :], o1h[:, b % 2].bitcast(F32), ALU.subtract).then_inc(o1_lo, 1)

    @block.vector
    def _(dve):
        steps = [0]

        def link(ins):
            steps[0] += 1
            ins.then_inc(dve_step, 1)
            dve.wait_ge(dve_step, steps[0])

        def full(step):
            dve.wait_ge(v_full, V_NO[step] + 1)
            return V_UNIT[V_NO[step] % 2]

        def flat(u):
            return u[:, :, :].rearrange("p b n -> p (b n)")

        def statistics(src, n):
            for t in range(NC):
                ins = dve.bn_stats(st[:, t, :], src[:, t])
            link(ins)
            for t in range(NC):
                ins = dve.bn_aggr(mv[:, n, t, :], st[:, t, :])
            ins.then_inc(stats, 1)
            dve.wait_ge(stats, n + 1)

        def split(hi, lo, src, semaphore):
            link(dve.tensor_copy(hi, src))
            dve.tensor_tensor(lo, src, hi.bitcast(F32), ALU.subtract).then_inc(semaphore, 1)

        def finish(b):
            dve.wait_ge(down_done, (NE + 1) * (b + 1))
            if b >= 2:
                dve.wait_ge(s_out[b % 2], 16 * (b // 2))
            dve.tensor_tensor(outb[:, b % 2], ACC[:, :, 0:TP], XF[:, b], ALU.add).then_inc(acc_free, 1)

        dve.wait_ge(s_cst, 48)
        dve.wait_ge(s_stage[0], 16)
        a = W_COLS["q0"][0]
        wqk = stage[:, 0, a:a + 3 * D].rearrange("p (n d) -> p n d", d=D)
        cos3, sin3 = (cc(name).unsqueeze(1).broadcast_to([128, 3, D]) for name in ("cos", "sin"))
        dve.tensor_tensor(wcos[:, :, :], wqk, cos3, ALU.mult)
        for even in range(2):
            ins = dve.tensor_tensor(wsin[:, :, even::2], wqk[:, :, 1 - even::2], sin3[:, :, even::2], ALU.mult)
        link(ins)
        dve.tensor_tensor(wqk, wcos[:, :, :], wsin[:, :, :], ALU.add).then_inc(rot_ok, 1)
        for step in walk():
            kind = step[0]
            if kind == "tok":
                b, n = step[1], ST_NO[step]
                u = full(step)
                uu = flat(u)[0:TC, 0:NC * D].rearrange("p (t d) -> p t d", d=D)
                statistics(uu, n)
                for t in range(NC):
                    ins = dve.scalar_tensor_tensor(X[:, b, t, :], uu[:, t, :], mv[:, n, t, 0:1], rr("gamma"),
                                                   ALU.subtract, ALU.mult)
                ins.then_inc(v_free, 1)
                dve.wait_ge(v_free, V_NO[step] + 1)
            elif kind == "tokn":
                b, n = step[1], ST_NO["tok", step[1]]
                dve.wait_ge(rstd_ok, n + 1)
                dve.scalar_tensor_tensor(X[:, b, 0, :], X[:, b, 0, :], rstd[:, n, 0:1], cls[:, :], ALU.mult, ALU.add)
                for t in range(1, NC):
                    ins = dve.tensor_scalar(X[:, b, t, :], X[:, b, t, :], rstd[:, n, t:t + 1], None, ALU.mult)
                link(ins)
            elif kind == "st":
                _, s, b = step
                statistics(X[:, b], ST_NO[step])
            elif kind == "ln":
                _, s, b = step
                n = ST_NO["st", s, b]
                dve.wait_ge(rstd_ok, n + 1)
                for t in range(NC):
                    ins = dve.tensor_scalar(xn[:, b % 2, t, :], X[:, b, t, :], mv[:, n, t, 0:1], rstd[:, n, t:t + 1],
                                            ALU.subtract, ALU.mult)
                ins.then_inc(xn_ok, 1)
            elif kind == "xt":
                _, s, b = step
                if s in (0, 2) and b >= 2:
                    if s == 0:
                        dve.wait_ge(a_full, A_NO["q", b - 2] + 1)
                    else:
                        dve.wait_ge(v_full, V_NO["v1", b - 2] + 1)
                        dve.wait_ge(a_full, A_NO["k1", b - 2] + 1)
                u = full(step)
                if s == 1:
                    if b == 0:
                        dve.wait_ge(v_free, V_NO["wo", B - 1] + 1)
                        dve.memset(xf[:, :, 0:1], 0.0)
                    dve.tensor_copy(xf[:, :, 1:TP + 1], u[:, :, 0:TP]).then_inc(v_free, 1)
                    dve.wait_ge(v_free, V_NO[step] + 1)
                elif s == 3:
                    split(XMh[:, b], XMl[:, b], u[:, :, 0:TP], v_free)
                else:
                    split(XTh[:, b % 2], XTl[:, b % 2], u[:, :, 0:TP], v_free)
            elif kind == "lat":
                b = step[1]
                if b >= 2:
                    dve.wait_ge(a_full, A_NO["v", b - 2] + 1)
                u = full(step)
                split(lath[:, b % 2], latl[:, b % 2], u[:, 0, 0:TP], v_free)
            elif kind == "p1":
                _, i, n = step
                u = full(step)
                if n == 0 and i >= 2:
                    dve.wait_ge(v_full, V_NO["mT", i - 2] + 1)
                a = 2 * (n % 4)
                dve.tensor_reduce(mx[:, i % 2, n // 4, a:a + 2], u[0:TC, :, 0:T], AX, ALU.max).then_inc(v_free, 1)
            elif kind == "mT":
                i = step[1]
                u = full(step)
                if i >= 2:
                    dve.wait_ge(s_nmw[i % 2], 16 * (i // 2))
                link(dve.tensor_scalar(nm[:, i % 2, 0, :], u[0:8, 0, 0:TP], -1.0, None, ALU.mult))
                dve.scalar_tensor_tensor(nm[:, i % 2, 1, :], u[0:8, 0, 0:TP], -1.0, nm[:, i % 2, 0, :].bitcast(F32),
                                         ALU.mult, ALU.subtract).then_inc(v_free, 1)
            elif kind == "pv":
                _, i, g = step
                q = 2 * i + g
                u = full(step)
                link(dve.stream_shuffle(den[:, :], u[:, 0, 0:TP], [HD] * 32))
                if q:
                    last = ("pv", i, 0) if g else ("pv", i - 1, 1)
                    dve.wait_ge(v_free, V_NO[last] + 1)
                link(dve.reciprocal(rec[:, :], den[:, :]))
                if q >= 2:
                    dve.wait_ge(o_lo, q - 1)
                dve.tensor_tensor(of[:, q % 2, :], u[:, 0, 0:TP], rec[:, :], ALU.mult).then_inc(v_free, 1)
            elif kind in ("wo", "wo1"):
                b = step[1]
                if kind == "wo1":
                    dve.wait_ge(bo_ok, b + 1)
                u = full(step)
                xb = X[:, b].rearrange("p t d -> p (t d)")
                dve.tensor_tensor(xb, xb, flat(u)[0:TC, 0:NC * D], ALU.add).then_inc(v_free, 1)
                dve.wait_ge(v_free, V_NO[step] + 1)
            elif kind == "mix":
                b = step[1]
                link(dve.tensor_tensor(dx[:, :, :], xf[:, :, 1:TP + 1], xf[:, :, 0:TP], ALU.subtract))
                if b:
                    dve.wait_ge(mix_lo, b)
                for k, name in enumerate(("mu_r", "mu_k")):
                    for c in range(2):
                        ins = dve.scalar_tensor_tensor(xm[:, k, c], dx[:, c], cc(name)[:, c:c + 1], xf[:, c, 0:TP],
                                                       ALU.mult, ALU.add)
                ins.then_inc(mix_ok, 1)
                dve.wait_ge(mix_ok, b + 1)
            elif kind == "kv":
                b = step[1]
                dve.wait_ge(a_free, A_NO["r", b] + 1)
                link(dve.tensor_scalar(sig[:, :, :], er[:, b % 2], 1.0, None, ALU.add))
                link(dve.reciprocal(er[:, b % 2], sig[:, :, :]))
                u = full(step)
                ee = er[:, b % 2].rearrange("p t d -> p (t d)")
                dve.tensor_tensor(sig[:, :, :].rearrange("p t d -> p (t d)"), flat(u)[0:TC, 0:NC * D], ee,
                                  ALU.mult).then_inc(v_free, 1)
                dve.wait_ge(v_free, V_NO[step] + 1)
                link(dve.tensor_tensor(X[:, b], X[:, b], sig[:, :, :], ALU.add))
            elif kind == "v1":
                b = step[1]
                u = full(step)
                if b >= 2:
                    dve.wait_ge(v_full, V_NO["kvm", b - 2] + 1)
                dve.tensor_tensor(v1t[:, b % 2], flat(u)[0:TC, 0:NC * D].rearrange("p (t d) -> p t d", d=D),
                                  rr("bv").unsqueeze(1).broadcast_to([TC, NC, D]), ALU.add).then_inc(v_free, 1)
            elif kind == "kT":
                b = step[1]
                u = full(step)
                if b >= 2:
                    dve.wait_ge(v_full, V_NO["kvm", b - 2] + 1)
                dve.tensor_copy(k1t[:, b % 2].rearrange("p t d -> p (t d)"), flat(u)[0:TC, 0:NC * D]).then_inc(v_free, 1)
            elif kind == "kvm":
                b = step[1]
                u = full(step)
                if b:
                    dve.wait_ge(v_full, V_NO["o", b - 1] + 1)
                dve.tensor_tensor(kvb[:, :, :], u[:, :, 0:128], cc("mask").unsqueeze(1).broadcast_to([128, 2, 128]),
                                  ALU.mult).then_inc(v_free, 1)
            elif kind == "z":
                if step[1]:
                    dve.wait_ge(v_free, V_NO["o", step[1] - 1] + 1)
                u = full(step)
                dve.tensor_scalar(zz[:, :, :], u[:, :, 0:TP], 1e-8, None, ALU.add).then_inc(v_free, 1)
                dve.wait_ge(v_free, V_NO[step] + 1)
                link(dve.reciprocal(zr[:, :, :], zz[:, :, :]))
            elif kind == "o":
                b = step[1]
                u = full(step)
                if b:
                    dve.wait_ge(o1_lo, b)
                dve.tensor_tensor(o1f[:, :, :], u[:, :, 0:TP], zr[:, :, :], ALU.mult).then_inc(v_free, 1)
            elif kind == "gate":
                b = step[1]
                u = full(step)
                lg = u[0:TC, 0, 0:NC * NE].rearrange("p (t e) -> p t e", e=NE)
                bc = [TC, NC, NE]
                if b >= 2:
                    dve.wait_ge(cw_ok, b - 1)
                if b:
                    dve.wait_ge(v_free, V_NO["gate", b - 1] + 1)
                link(dve.tensor_tensor(gp[:, :, :], lg, rr("gate_b").unsqueeze(1).broadcast_to(bc), ALU.add))
                link(dve.tensor_reduce(gm[:, :], gp[:, :, :], AX, ALU.max))
                if b:
                    dve.wait_ge(ge_ok, b)
                dve.tensor_tensor(glog[:, :, :], gp[:, :, :], gm[:, :].unsqueeze(2).broadcast_to(bc),
                                  ALU.subtract).then_inc(v_free, 1)
            elif kind == "cwT":
                b = step[1]
                bc, b4 = [TC, NC, NE], [TC, NC, NE, NE]
                dve.wait_ge(ge_ok, b + 1)
                dve.wait_ge(v_free, V_NO["gate", min(b + 1, B - 1)] + 1)
                link(dve.tensor_reduce(gs[:, :], ge[:, b % 2], AX, ALU.add))
                link(dve.reciprocal(gr[:, :], gs[:, :]))
                link(dve.tensor_tensor(gp[:, :, :], ge[:, b % 2], gr[:, :].unsqueeze(2).broadcast_to(bc), ALU.mult))
                p_j, p_e = gp[:, :, :].unsqueeze(2).broadcast_to(b4), gp[:, :, :].unsqueeze(3).broadcast_to(b4)
                before = rr("before").rearrange("p (e j) -> p e j", j=NE).unsqueeze(1).broadcast_to(b4)
                gt4, gq4 = (x[:, :, :].rearrange("p t (e j) -> p t e j", j=NE) for x in (gt, gq))
                link(dve.tensor_tensor(gq4, p_j, p_e, ALU.is_equal))
                link(dve.tensor_tensor(gq4, gq4, before, ALU.mult))
                link(dve.tensor_tensor(gt4, p_j, p_e, ALU.is_gt))
                link(dve.tensor_tensor(gt4, gt4, gq4, ALU.add))
                link(dve.tensor_reduce(rank[:, :, :], gt4, AX, ALU.add))
                dve.scalar_tensor_tensor(cw[:, b % 2], rank[:, :, :], 2.0, gp[:, :, :], ALU.is_lt, ALU.mult).then_inc(cw_ok, 1)
                if b == 0:
                    dve.wait_ge(s_set, 8)
                u = full(step)
                link(dve.tensor_copy(cwx[0:NE, b, :], u[0:NE, 0, 0:TP]))
                dve.tensor_tensor(cwx[64:64 + NE, b, :], u[0:NE, 0, 0:TP], cwx[0:NE, b, :].bitcast(F32),
                                  ALU.subtract).then_inc(v_free, 1)
            elif kind == "expert":
                _, b, e = step
                n = (NE + 1) * b + e
                dve.wait_ge(ma_free, n + 1)
                dve.wait_ge(mb_full, n + 1)
                g = eg if e else ehf
                if n:
                    dve.wait_ge(h_ok, n)
                for m in range(2):
                    a = C_COLS["b1"][0] + 4 * e + 2 + m
                    ins = dve.scalar_tensor_tensor(g[:, m], UP_B[:, m, 0:TP], cst[:, a:a + 1], es[:, n % 2, m],
                                                   ALU.add, ALU.mult)
                ins.then_inc(mb_free, 1)
                dve.wait_ge(mb_free, n + 1)
                if e:
                    k = NE * b + e - 1
                    dve.wait_ge(mc_full, k + 1)
                    dve.tensor_tensor(ehf[:, :, :], eg[:, :, :], CWB[:, 0:1, 0:TP].broadcast_to([128, 2, TP]),
                                      ALU.mult).then_inc(mc_free, 1)
                    dve.wait_ge(mc_free, k + 1)
                if n >= 2:
                    dve.wait_ge(down_done, n - 1)
                split(ehh[:, n % 2], ehl[:, n % 2], ehf[:, :, :], h_ok)
                if e == 0 and b:
                    finish(b - 1)
                if n == B * (NE + 1) - 1:
                    finish(b)

    ctx.close()


def _layout(x, cls_tok, w):
    f = np.float32

    def halves(a):
        a = np.asarray(a)
        return np.concatenate([a[0:128], a[128:256]], axis=1)

    patches = np.asarray(x).reshape(B, 5, 16, 8, 16, 8).transpose(1, 3, 5, 0, 2, 4).reshape(320, B, D)
    xp = np.zeros((NC * KP, B, TP), f)
    xp[0:320, :, 1:T] = patches
    xp = np.ascontiguousarray(xp.reshape(NC, KP, B, TP).transpose(1, 0, 2, 3))
    wt = np.zeros((NC * KP, D), f)
    wt[0:320] = w["L0_tok_W"]
    wt = np.ascontiguousarray(wt.reshape(NC, KP, D).transpose(1, 0, 2))

    pack = np.zeros((128, W_TOTAL), f)

    def put(name, a):
        at, n = W_COLS[name]
        assert a.shape[1] == n
        pack[0:a.shape[0], at:at + n] = a

    w = {k: np.asarray(v) for k, v in w.items()}
    put("lat", halves(np.concatenate([w["L0_attn_wk_a"].T, w["L0_attn_wv_a"].T], axis=1)))
    put("q0", halves(w["L0_attn_wq"].T))
    put("k0", w["L0_attn_wk_b"].T)
    put("v0", np.concatenate([np.zeros((64, D), f), w["L0_attn_wv_b"].T]))
    o0 = np.zeros((4, 4, 32, D), f)
    o0[:, :, 0:HD] = w["L0_attn_wo"].T.reshape(4, 4, HD, D)
    put("o0", o0.reshape(4, 128, D).transpose(1, 0, 2).reshape(128, 4 * D))
    for name, key in (("r", "L0_ffn_W_r"), ("fk", "L0_ffn_W_k"), ("fv", "L0_ffn_W_v"), ("q1", "L1_attn_Wq"),
                      ("k1", "L1_attn_Wk"), ("v1", "L1_attn_Wv"), ("o1", "L1_attn_Wo")):
        put(name, halves(w[key].T))
    eb = np.zeros((128, D), f)
    eb[0:NE] = eb[64:64 + NE] = w["L1_ffn_rb2"]
    eb[32] = w["L1_ffn_sb2"][0]
    put("eb", eb)
    put("gate", halves(w["L1_ffn_gate_w"]))
    sel = np.zeros((128, NE, 128), f)
    for e in range(NE):
        sel[e, e] = sel[64 + e, e] = 1.0
    put("sel", sel.reshape(128, NE * 128))

    experts = np.zeros((NE + 1, 128, EXPERT), f)
    w1 = np.concatenate([w["L1_ffn_sw1"], w["L1_ffn_rw1"]])
    w2 = np.concatenate([w["L1_ffn_sw2"], w["L1_ffn_rw2"]])
    b1 = np.concatenate([w["L1_ffn_sb1"], w["L1_ffn_rb1"]])
    for e in range(NE + 1):
        experts[e, :, 0:4 * D] = halves(w1[e])
        experts[e, :, 4 * D:] = halves(w2[e])

    con = np.zeros((128, C_TOTAL), f)

    def const(name, a):
        at, n = C_COLS[name]
        con[:, at:at + n] = np.asarray(a).reshape(128, n)

    inv = (1.0 / 10000.0 ** (np.arange(0, HD, 2, dtype=f) / f(HD))).astype(f)
    angle = np.repeat(np.arange(NH, dtype=f)[:, None] * inv[None, :], 2, axis=1).reshape(1, D)
    sign = np.where(np.arange(D) % 2 == 0, f(-1), f(1))
    const("cos", np.repeat(np.cos(angle), 128, axis=0))
    const("sin", np.repeat(np.sin(angle) * sign, 128, axis=0))
    block = np.arange(128) // HD
    const("mask", (block[:, None] == block[None, :]).astype(f))
    rbd = np.zeros((128, 128), f)
    for h in range(8):
        rbd[HD * h:HD * h + HD, HD * h:HD * h + HD] = w["L1_attn_R"]
    const("rbd", rbd)
    const("ident", np.eye(128, dtype=f))
    for name, key in (("mu_r", "L0_ffn_mu_r"), ("mu_k", "L0_ffn_mu_k"), ("bq", "L1_attn_bq"), ("bk", "L1_attn_bk")):
        const(name, w[key].reshape(2, 128).T)
    const("b1", b1.reshape(NE + 1, 4, 128).transpose(2, 0, 1).reshape(128, -1))

    rows = np.zeros((1, R_TOTAL), f)
    before = (np.arange(NE)[None, :] < np.arange(NE)[:, None]).astype(f)
    for name, a in (("gamma", w["L0_tok_gamma"]), ("bv", w["L1_attn_bv"]), ("bo", w["L1_attn_bo"]),
                    ("gate_b", w["L1_ffn_gate_b"]), ("before", before)):
        at, n = R_COLS[name]
        rows[0, at:at + n] = a.reshape(n)
    cls_rows = np.zeros((TC, D), f)
    cls_rows[0] = np.asarray(cls_tok).reshape(D)
    return {"patches": xp, "w_tok": wt, "rows": rows, "cls_rows": cls_rows, "consts": con,
            "weights": pack, "experts": experts}


def kernel(x, cls_tok, **w):
    import concourse.bacc as bacc
    from concourse.bass_utils import run_bass_kernel_spmd

    nc = bacc.Bacc("TRN2", target_bir_lowering=False, num_devices=1)
    arrays = _layout(x, cls_tok, w)
    args = [nc.dram_tensor(name, a.shape, F32, kind="ExternalInput").ap() for name, a in arrays.items()]
    out = nc.dram_tensor("tower_out", (B, D, TP), F32, kind="ExternalOutput").ap()
    tower(nc, *args, out)
    got = run_bass_kernel_spmd(nc, [arrays], core_ids=[0]).results[0]["tower_out"]
    return np.ascontiguousarray(got.transpose(0, 2, 1)[:, 0:T, :])
```

```python
from contextlib import ExitStack

import numpy as np

import concourse.bass as bass
from concourse import mybir

B = 4
T = 257
TP = 258
TC = 86
NC = 3
D = 256
NH = 16
HD = 16
KP = 107
NE = 8
EPS = 1e-5
F32 = mybir.dt.float32
F32R = mybir.dt.float32r
ALU = mybir.AluOpType
ACT = mybir.ActivationFunctionType
AX = mybir.AxisListType.X

W_COLS = {}
_at = 0
for _name, _n in (("lat", 2 * 128), ("q0", 2 * D), ("k0", D), ("v0", D), ("o0", 4 * D),
                  ("r", 2 * D), ("fk", 2 * D), ("fv", 2 * D),
                  ("q1", 2 * D), ("k1", 2 * D), ("v1", 2 * D), ("o1", 2 * D),
                  ("eb", D), ("gate", 2 * NE), ("sel", NE * 128)):
    W_COLS[_name] = (_at, _n)
    _at += _n
W_TOTAL = _at
EXPERT = 2 * 2 * D + 2 * D
PIECES = [("lat", "v0"), ("o0", "o0"), ("r", "fv"), ("q1", "k1"), ("v1", "o1"), ("eb", "sel")]
EARLY = 1

C_COLS = {}
_at = 0
for _name, _n in (("cos", D), ("sin", D), ("mask", 128), ("rbd", 128), ("ident", 128),
                  ("mu_r", 2), ("mu_k", 2), ("bq", 2), ("bk", 2), ("b1", 4 * (NE + 1))):
    C_COLS[_name] = (_at, _n)
    _at += _n
C_TOTAL = _at
R_COLS = {}
_at = 0
for _name, _n in (("gamma", D), ("bv", D), ("bo", D), ("gate_b", NE), ("before", NE * NE)):
    R_COLS[_name] = (_at, _n)
    _at += _n
R_TOTAL = _at


STAGGER = 8
LAG = 18


def walk():
    yield ("tok", 0)
    yield ("split", 0)
    yield ("tokn", 0)
    yield ("st", 0, 0)
    yield ("tok", 1)
    yield ("ln", 0, 0)
    yield ("xt", 0, 0)
    yield ("tokn", 1)
    yield ("st", 0, 1)
    yield ("tok", 2)
    yield ("q", 0)
    yield ("qsplit", 0)
    yield ("lat", 0)
    yield ("tokn", 2)
    yield ("st", 0, 2)
    yield ("k", 0)
    yield ("qsplit", 1)
    yield ("stk", 0)
    yield ("stk", 1)
    yield ("v", 0)
    yield ("tok", 3)
    yield ("tokn", 3)
    yield ("st", 0, 3)
    yield ("split", 1)

    for m in range(12 * 2 * B + LAG + 14):
        b = m // 24 + 1
        if b < B:
            for at, step in ((0, ("ln", 0, b)), (1, ("xt", 0, b)), (3, ("q", b)), (3, ("qsplit", 2 * b)),
                             (4, ("lat", b)), (6, ("k", b)), (6, ("qsplit", 2 * b + 1)), (22, ("v", b))):
                if m % 24 == at:
                    yield step
        if m < 12 * 2 * B:
            yield ("p1", m // 12, m % 12)
        if m >= 13 and (m - 13) % 12 == 0 and (m - 13) // 12 < 2 * B:
            yield ("mT", (m - 13) // 12)
        k = m - LAG
        if m == 8:
            yield ("stk", 2)
        if 0 <= k < 12 * 2 * B:
            yield ("p2", k // 12, k % 12)
            if k % 12 == 11 and k // 12 + 3 < 2 * B:
                yield ("stk", k // 12 + 3)
        for t in range(NC):
            g, at = divmod(k - 5 - t, 6)
            if at == 0 and 0 <= g < 4 * B:
                yield ("pv", g // 2, g % 2, t)
                if t == NC - 1:
                    yield ("osplit", g // 2, g % 2)
        if k >= 28 and (k - 28) % 24 == 0:
            yield ("wo", (k - 28) // 24)
            yield ("st", 1, (k - 28) // 24)
        if m in (80, 88, 96):
            yield ("split", 2 + (m - 80) // 8)

    def rows(b):
        return ((("ln", 1, b),), (("xt", 1, b),), (("mix", b),), (), (("r", b), ("fk", b)), (), (),
                (("kv", b), ("st", 2, b)), (), (("ln", 2, b),), (("xt", 2, b),), (("q1", b), ("k1", b)),
                (("v1", b), ("sq", b)), (), (("ke", b), ("qe", b)), (), (("kT", b), ("z", b)),
                (("kvm", b),), (("o", b), ("o1split", b)), (), (("wo1", b), ("st", 3, b)), (),
                (("ln", 3, b),), (("xt", 3, b), ("xx", b)), (("gate", b),), (), (("cwT", b),))

    for t in range(len(rows(0)) + (B - 1) * STAGGER):
        for b in range(B):
            if 0 <= t - STAGGER * b < len(rows(0)):
                yield from rows(b)[t - STAGGER * b]
        if t == 5:
            yield ("split", 5)
    for n in range(3):
        yield ("split", 6 + n)
    for b in range(B):
        for e in range(NE + 1):
            yield ("expert", b, e)
            if b == 0 and e + 3 <= NE:
                yield ("split", 9 + e)


V_STEPS = {"tok", "xt", "lat", "p1", "mT", "pv", "wo", "kv", "v1", "kT", "kvm", "z", "o", "wo1", "gate", "cwT"}
A_STEPS = {"q", "k", "v", "p2", "r", "fk", "q1", "k1", "qe", "ke", "xx"}
LAST = {s for s in walk() if s[0] != "pv" or s[3] == NC - 1}
V_NO = {s: n for n, s in enumerate(s for s in walk() if s[0] in V_STEPS and s in LAST)}
A_NO = {s: n for n, s in enumerate(s for s in walk() if s[0] in A_STEPS)}
SMALL = {"lat", "mT", "pv", "gate", "cwT"}
RINGS = ([s for s in walk() if s[0] in V_STEPS | A_STEPS and s[0] not in SMALL],
         [s[0:3] for s in walk() if s[0] in SMALL and (s[0] != "pv" or s[3] == 0)])
RING_NO = {s: (ring, n) for ring in range(2) for n, s in enumerate(RINGS[ring])}


def no_last(step):
    return V_NO[step + (NC - 1,) if step[0] == "pv" else step]


ST_NO = {s: n for n, s in enumerate(s for s in walk() if s[0] in ("tok", "st"))}
LN_NO = {s: n for n, s in enumerate(s for s in walk() if s[0] == "ln")}


def tower(nc, xp, w_tok, rows, cls_rows, consts, weights, experts, out):
    ctx = ExitStack()

    def sb(where, name, shape, dt=F32):
        return where.enter_context(nc.sbuf_tensor(name, shape, dt))

    stage = sb(ctx, "stage", [128, 2, EXPERT])
    cst = sb(ctx, "cst", [128, C_TOTAL])
    row = sb(ctx, "row", [TC, R_TOTAL])
    cls = sb(ctx, "cls", [TC, D])
    neg = sb(ctx, "neg", [128, 128])
    rbd = sb(ctx, "rbd", [128, 128])
    eps = sb(ctx, "eps", [128, 1])
    st = sb(ctx, "st", [TC, NC, 6])
    mv = sb(ctx, "mv", [TC, len(ST_NO), NC, 2])
    lnv = sb(ctx, "lnv", [TC, len(ST_NO), NC])
    rst0 = sb(ctx, "rst0", [TC, len(ST_NO), NC])
    nwt = sb(ctx, "nwt", [TC, len(ST_NO), NC])
    rstd = sb(ctx, "rstd", [TC, len(ST_NO), NC])
    g0 = ExitStack()
    X = sb(g0, "X", [TC, B, NC, D])
    xn = sb(g0, "xn", [TC, 2, NC, D])
    XTh = sb(g0, "XTh", [128, 2, 2, TP], F32R)
    XTl = sb(g0, "XTl", [128, 2, 2, TP], F32R)
    size0 = B * NC * D + 2 * NC * D + 8 * TP
    g0.close()
    g0 = ExitStack()
    es = sb(g0, "es", [128, 2, 2, TP])
    eg = sb(g0, "eg", [128, 2, TP])
    ehf = sb(g0, "ehf", [128, 2, TP])
    ehh = sb(g0, "ehh", [128, 2, 2, TP], F32R)
    ehl = sb(g0, "ehl", [128, 2, 2, TP], F32R)
    outb = sb(g0, "outb", [128, 2, 2, TP])
    g0.close()
    assert size0 >= 20 * TP
    sb(ctx, "room0", [128, size0])

    g1 = ExitStack()
    n_w0 = W_COLS["o0"][0]
    W0h = sb(g1, "W0h", [128, n_w0], F32R)
    W0l = sb(g1, "W0l", [128, n_w0], F32R)
    lath = sb(g1, "lath", [128, 2, TP], F32R)
    latl = sb(g1, "latl", [128, 2, TP], F32R)
    qf = sb(g1, "qf", [128, 2, 2, TP])
    wcos = sb(g1, "wcos", [128, 3, D])
    wsin = sb(g1, "wsin", [128, 3, D])
    mid0 = W_COLS["r"][0]
    n_mid = W_COLS["eb"][0] - mid0
    size1 = 2 * n_w0 + 8 * TP + 6 * D
    if size1 < 2 * n_mid:
        sb(g1, "room_mid", [128, 2 * n_mid - size1])
        size1 = 2 * n_mid
    g2 = ExitStack()
    Woh = sb(g2, "Woh", [128, 4 * D], F32R)
    Wol = sb(g2, "Wol", [128, 4 * D], F32R)
    qh = sb(g2, "qh", [128, 2, 2, TP], F32R)
    ql = sb(g2, "ql", [128, 2, 2, TP], F32R)
    Qst = sb(g2, "Qst", [128, 3, 8, TP], F32R)
    Kst = sb(g2, "Kst", [128, 3, 8, TP], F32R)
    Vt = sb(g2, "Vt", [TC, 2, NC, NH, 32])
    mx = sb(g2, "mx", [TC, 2, NC, 8])
    nm = sb(g2, "nm", [8, 2, 2, TP], F32R)
    den = sb(g2, "den", [128, TP])
    rec = sb(g2, "rec", [128, TP])
    of = sb(g2, "of", [128, 2, TP])
    oh = sb(g2, "oh", [128, 4, TP], F32R)
    ol = sb(g2, "ol", [128, 4, TP], F32R)
    gp_ = ExitStack()
    P = sb(gp_, "P", [TC, 2, 12, TP])
    gp_.close()
    xps = sb(gp_, "xps", [KP, NC, B, TP])
    wts = sb(gp_, "wts", [KP, NC, D])
    gp_.close()
    g2.close()
    g1.close()

    gm_ = ExitStack()
    Wmh = sb(gm_, "Wmh", [128, n_mid], F32R)
    Wml = sb(gm_, "Wml", [128, n_mid], F32R)
    if size1 > 2 * n_mid:
        sb(gm_, "room1", [128, size1 - 2 * n_mid])
    g3 = ExitStack()
    xf = sb(g3, "xf", [128, 2, TP + 1])
    dx = sb(g3, "dx", [128, 2, TP])
    xm = sb(g3, "xm", [128, 2, 2, TP])
    xmh = sb(g3, "xmh", [128, 2, 2, TP], F32R)
    xml = sb(g3, "xml", [128, 2, 2, TP], F32R)
    er = sb(g3, "er", [TC, NC, D])
    sig = sb(g3, "sig", [TC, NC, D])
    kr = sb(g3, "kr", [128, 2, TP])
    ka = sb(g3, "ka", [128, 2, TP])
    kah = sb(g3, "kah", [128, 2, TP], F32R)
    kal = sb(g3, "kal", [128, 2, TP], F32R)
    q1f = sb(g3, "q1f", [128, 2, 2, 2, TP])
    q1s = sb(g3, "q1s", [128, 2, 2, TP])
    q1e = sb(g3, "q1e", [128, 2, 2, 2, TP])
    v1t = sb(g3, "v1t", [TC, NC, D])
    k1t = sb(g3, "k1t", [TC, NC, D])
    kvb = sb(g3, "kvb", [128, 2, 128])
    zz = sb(g3, "zz", [128, 2, TP])
    zr = sb(g3, "zr", [128, 2, TP])
    o1f = sb(g3, "o1f", [128, 2, TP])
    o1h = sb(g3, "o1h", [128, 2, 2, TP], F32R)
    o1l = sb(g3, "o1l", [128, 2, 2, TP], F32R)
    size3 = 2 * TP + 1 + (2 + 4 + 8 + 2 + 2 + 4 + 8 + 4 + 8 + 2 + 2 + 2 + 8) * TP + 4 * NC * D + 256
    g3.close()
    gm_.close()
    late_cols = 2 * (NE + 1 - EARLY) * EXPERT
    Wlh = sb(ctx, "Wlh", [128, NE + 1 - EARLY, EXPERT], F32R)
    Wll = sb(ctx, "Wll", [128, NE + 1 - EARLY, EXPERT], F32R)
    assert late_cols <= size1 + size3
    sb(ctx, "room2", [128, size1 + size3 - late_cols])
    Weh = sb(ctx, "Weh", [128, EARLY, EXPERT], F32R)
    Wel = sb(ctx, "Wel", [128, EARLY, EXPERT], F32R)
    n_eb = W_COLS["sel"][0] - W_COLS["eb"][0]
    Ebh = sb(ctx, "Ebh", [128, W_TOTAL - W_COLS["eb"][0]], F32R)
    Ebl = sb(ctx, "Ebl", [128, n_eb], F32R)
    XMh = sb(ctx, "XMh", [128, B, 2, TP], F32R)
    XMl = sb(ctx, "XMl", [128, B, 2, TP], F32R)
    XF = sb(ctx, "XF", [128, B, 2, TP])
    cwx = sb(ctx, "cwx", [128, B, TP], F32R)
    glog = sb(ctx, "glog", [TC, NC, NE])
    gm = sb(ctx, "gm", [TC, NC])
    gs = sb(ctx, "gs", [TC, NC])
    gr = sb(ctx, "gr", [TC, NC])
    rank = sb(ctx, "rank", [TC, NC, NE])
    ge = sb(ctx, "ge", [TC, 2, NC, NE])
    gp = sb(ctx, "gp", [TC, NC, NE])
    gt = sb(ctx, "gt", [TC, NC, NE * NE])
    gq = sb(ctx, "gq", [TC, NC, NE * NE])
    cw = sb(ctx, "cw", [TC, 2, NC, NE])

    psum = [ctx.enter_context(nc.psum_tensor(f"unit{n}", [128, 2, 512], F32)) for n in range(4)]

    def unit_of(step):
        ring, n = RING_NO[step[0:3] if step[0] == "pv" else step]
        return psum[3][:, n % 2:n % 2 + 1, :] if ring else psum[n % 3]

    ACC, UP_A, UP_B, CWB = psum

    scratch = nc.dram_tensor("qk_scratch", [B, 2, 2, D, TP], F32, kind="Internal").ap()

    def sem(name):
        return ctx.enter_context(nc.semaphore(name))

    s_xp = [sem(f"patches_in{b}") for b in range(B)]
    s_cst, s_wt = sem("constants_in"), sem("token_weights_in")
    s_stage = [sem(f"stage_in{n}") for n in range(2)]
    s_set = sem("constants_made")
    v_full, v_free = sem("v_full"), sem("v_free")
    a_full, a_free = sem("a_full"), sem("a_free")
    w_hi, w_lo = sem("weights_high"), sem("weights_low")
    stats, rstd_ok, xn_ok = sem("stats_ready"), sem("rstd_ready"), sem("normalised")
    lnv_ok, rst0_ok, newton = sem("log_var_ready"), sem("rstd_estimate"), sem("newton_step")
    rot_ok, q_hi, q_lo = sem("weights_rotated"), sem("qk_high"), sem("qk_low")
    s_scr = [sem(f"qk_in_scratch{n}") for n in range(2)]
    s_stk = [sem(f"stack_in{n}") for n in range(3)]
    s_mrow = [sem(f"max_rows_in{n}") for n in range(3)]
    o_hi, o_lo = sem("heads_high"), sem("heads_low")
    mix_ok, mix_hi, mix_lo = sem("mixed"), sem("mixed_high"), sem("mixed_low")
    kr_ok, ka_ok, ka_hi, ka_lo = sem("relu_ready"), sem("square_ready"), sem("square_high"), sem("square_low")
    sq_ok, bo_ok = sem("qk_squared"), sem("out_bias_added")
    o1_hi, o1_lo = sem("heads1_high"), sem("heads1_low")
    ge_ok, cw_ok = sem("gate_exp"), sem("expert_weights")
    dve_step = sem("vector_step")
    ma_full, ma_free = sem("up_a_full"), sem("up_a_free")
    mb_full, mb_free = sem("up_b_full"), sem("up_b_free")
    mc_full, mc_free = sem("token_weights_full"), sem("token_weights_free")
    h_ok, down_done, acc_free = sem("hidden_ready"), sem("down_done"), sem("out_ready")
    s_out = [sem(f"out_written{n}") for n in range(2)]
    block = ctx.enter_context(nc.Block())

    def cc(name):
        a, n = C_COLS[name]
        return cst[:, a:a + n]

    def rr(name):
        a, n = R_COLS[name]
        return row[:, a:a + n]

    def piece(p):
        if p < len(PIECES):
            a, (z, n) = W_COLS[PIECES[p][0]][0], W_COLS[PIECES[p][1]]
            n = z + n - a
            if p == 0:
                return n, W0h[:, a:a + n], W0l[:, a:a + n], n
            if p == 1:
                return n, Woh[:, :], Wol[:, :], n
            if p < 5:
                return n, Wmh[:, a - mid0:a - mid0 + n], Wml[:, a - mid0:a - mid0 + n], n
            return n, Ebh[:, :], Ebl[:, :], n_eb
        e = p - len(PIECES)
        h, l, e = (Weh, Wel, e) if e < EARLY else (Wlh, Wll, e - EARLY)
        return EXPERT, h[:, e, :], l[:, e, :], EXPERT

    LAST_PROJ = ("v", B - 1)
    GRAM = ("wo1", B - 1)

    @block.sync
    def _(sp):
        def load_piece(p):
            if p >= 2:
                sp.wait_ge(w_lo, p - 1)
            n = piece(p)[0]
            if p < len(PIECES):
                a = W_COLS[PIECES[p][0]][0]
                src = weights[:, a:a + n]
            else:
                src = experts[p - len(PIECES)]
            sp.dma_start(stage[:, p % 2, 0:n], src).then_inc(s_stage[p % 2], 16)

        def store_qk(r):
            b, k = r // 2, r % 2
            sp.wait_ge(q_lo, r + 1)
            for part, src in ((0, qh), (1, ql)):
                sp.dma_start(scratch[b, k, part].rearrange("(c p) t -> p c t", p=128),
                             src[:, r % 2].bitcast(F32)).then_inc(s_scr[k], 16)

        def load_stacks(i):
            b, c, s = i // 2, i % 2, i % 3
            for k in range(2):
                sp.wait_ge(s_scr[k], 32 * (b + 1))
            if i >= 3:
                sp.wait_ge(a_full, A_NO["p2", i - 3, 11] + 1)
                sp.dma_start(Qst[96:98, s].bitcast(F32), Qst[64:66, s].bitcast(F32)).then_inc(s_stk[s], 16)
            for k, dst, parts in ((0, Qst, (0, 1, 0, 1)), (1, Kst, (0, 0, 1, 1))):
                for g, part in enumerate(parts):
                    src = scratch[b, k, part, 128 * c:128 * c + 128].rearrange("(h d) t -> d h t", d=HD)
                    sp.dma_start(dst[HD * g:HD * g + HD, s].bitcast(F32), src).then_inc(s_stk[s], 16)

        def move_max(i):
            sp.wait_ge(v_free, V_NO["mT", i] + 1)
            for part in range(2):
                sp.dma_start(Qst[96 + part:97 + part, i % 3].bitcast(F32),
                             nm[:, i % 2, part].bitcast(F32)).then_inc(s_mrow[i % 3], 16)

        sp.dma_start(wts[:, :, :], w_tok).then_inc(s_wt, 16)
        sp.dma_start(xps[:, :, 0, :], xp[:, :, 0, :]).then_inc(s_xp[0], 16)
        sp.dma_start(cst[:, :], consts).then_inc(s_cst, 16)
        sp.dma_start(row[:, :], rows.partition_broadcast(TC)).then_inc(s_cst, 16)
        sp.dma_start(cls[:, :], cls_rows).then_inc(s_cst, 16)
        load_piece(0)
        for b in range(1, B):
            sp.dma_start(xps[:, :, b, :], xp[:, :, b, :]).then_inc(s_xp[b], 16)
        load_piece(1)
        n_pieces = len(PIECES) + NE + 1
        loaded = 2
        for step in walk():
            kind = step[0]
            if kind == "qsplit":
                store_qk(step[1])
            elif kind == "stk":
                load_stacks(step[1])
            elif kind == "mT":
                move_max(step[1])
            elif kind == "split" and loaded < n_pieces:
                load_piece(loaded)
                loaded += 1
        for b in range(B):
            sp.wait_ge(acc_free, b + 1)
            sp.dma_start(out[b].rearrange("(c p) t -> p c t", p=128), outb[:, b % 2]).then_inc(s_out[b % 2], 16)
        for n in range(2):
            sp.wait_ge(s_out[n], 16 * (B // 2))

    @block.tensor
    def _(pe):
        def unit(step):
            ring, n = RING_NO[step[0:3] if step[0] == "pv" else step]
            before = n - (2 if ring else 3)
            if before >= 0:
                last = RINGS[ring][before]
                if last[0] in V_STEPS:
                    pe.wait_ge(v_free, no_last(last) + 1)
                else:
                    pe.wait_ge(a_free, A_NO[last] + 1)
            return unit_of(step)

        def exact(dst, lh, ll, rh, rl, first, last):
            pe.matmul(dst, lh, rh, start=first, stop=False)
            pe.matmul(dst, lh, rl, start=False, stop=False)
            return pe.matmul(dst, ll, rh, start=False, stop=last)

        def w(name, c, m=None):
            a, n = W_COLS[name]
            h, l = (W0h, W0l) if a < n_w0 else (Woh, Wol) if name == "o0" else (Wmh, Wml) if a < W_COLS["eb"][0] else (Ebh, Ebl)
            a -= 0 if a < n_w0 else n_w0 if name == "o0" else mid0 if a < W_COLS["eb"][0] else W_COLS["eb"][0]
            width = {"lat": 128, "gate": NE}.get(name, D)
            a += c * width
            if m is not None:
                a, width = a + 128 * m, 128
            return h[:, a:a + width], l[:, a:a + width]

        def tok(t):
            return slice(TC * t, TC * t + TC)

        def flat(u):
            return u[:, :, :].rearrange("p b n -> p (b n)")

        def transposes(u, src, step=None):
            for c in range(2):
                for t in range(NC):
                    ins = pe.transpose(u[:, c, tok(t)], src[:, t, 128 * c:128 * c + 128], cc("ident")[0:TC, 0:TC])
            return ins

        def token_major(u, lh, ll, name, halves=2):
            for t in range(NC):
                for c in range(halves):
                    ins = exact(flat(u)[0:TC, D * t:D * t + D], lh[:, c, tok(t)], ll[:, c, tok(t)],
                                *w(name, c), c == 0, c == halves - 1)
            return ins

        def feature_major(u, name, xh, xl, halves=2):
            for m in range(2):
                for c in range(halves):
                    ins = exact(u[:, m, 0:TP], *w(name, c, m), xh[:, c], xl[:, c], c == 0, c == halves - 1)
            return ins

        pe.wait_ge(s_wt, 16)
        for step in walk():
            kind = step[0]
            if kind == "tok":
                b = step[1]
                pe.wait_ge(s_xp[b], 16)
                u = unit(step)
                for t in range(NC):
                    for k in range(NC):
                        ins = pe.matmul(flat(u)[0:TC, D * t:D * t + D], xps[:, k, b, tok(t)], wts[:, k, :],
                                        start=k == 0, stop=k == NC - 1)
                ins.then_inc(v_full, 1)
            elif kind == "xt":
                _, s, b = step
                if LN_NO["ln", s, b] == 0:
                    pe.wait_ge(s_cst, 48)
                pe.wait_ge(xn_ok, LN_NO["ln", s, b] + 1)
                u = unit(step)
                transposes(u, xn[:, b % 2]).then_inc(v_full, 1)
            elif kind == "lat":
                b = step[1]
                u = unit(step)
                for c in range(2):
                    ins = exact(u[:, 0, 0:TP], *w("lat", c, 0), XTh[:, b % 2, c], XTl[:, b % 2, c], c == 0, c == 1)
                ins.then_inc(v_full, 1)
            elif kind == "q":
                b = step[1]
                if b == 0:
                    pe.wait_ge(w_lo, 1)
                pe.wait_ge(v_free, V_NO["xt", 0, b] + 1)
                u = unit(step)
                feature_major(u, "q0", XTh[:, b % 2], XTl[:, b % 2]).then_inc(a_full, 1)
            elif kind == "k":
                b = step[1]
                pe.wait_ge(v_free, V_NO["lat", b] + 1)
                u = unit(step)
                feature_major(u, "k0", lath[:, b % 2:b % 2 + 1], latl[:, b % 2:b % 2 + 1], 1).then_inc(a_full, 1)
            elif kind == "v":
                b = step[1]
                u = unit(step)
                token_major(u, lath[:, b % 2:b % 2 + 1], latl[:, b % 2:b % 2 + 1], "v0", 1).then_inc(a_full, 1)
            elif kind == "p1":
                _, i, n = step
                if n == 0:
                    pe.wait_ge(s_stk[i % 3], 128 * (i // 3 + 1) + 16 * (i // 3))
                    if i < 3:
                        pe.wait_ge(s_set, 6)
                u = unit(step)
                for j in range(2):
                    h = 2 * (n % 4) + j
                    ins = pe.matmul(u[0:TC, j, 0:TP], Qst[:, i % 3, h, tok(n // 4)], Kst[:, i % 3, h, :],
                                    start=True, stop=True)
                ins.then_inc(v_full, 1)
            elif kind == "mT":
                i = step[1]
                pe.wait_ge(v_free, V_NO["p1", i, 11] + 1)
                u = unit(step)
                for t in range(NC):
                    ins = pe.transpose(u[0:8, 0, tok(t)], mx[:, i % 2, t, :], cc("ident")[0:TC, 0:TC])
                ins.then_inc(v_full, 1)
            elif kind == "p2":
                _, i, n = step
                if n == 0:
                    pe.wait_ge(s_mrow[i % 3], 32 * (i // 3 + 1))
                u = unit(step)
                for j in range(2):
                    t, h = n % 6 // 2, 4 * (n // 6) + 2 * (n % 2) + j
                    ins = pe.matmul(u[0:TC, j, 0:TP], Kst[:, i % 3, h, tok(t)], Qst[:, i % 3, h, :],
                                    start=True, stop=True)
                ins.then_inc(a_full, 1)
            elif kind == "pv":
                _, i, g, t = step
                b = i // 2
                pe.wait_ge(a_free, A_NO["p2", i, 6 * g + 2 * t + 1] + 1)
                u = unit(step) if t == 0 else unit_of(step)
                kn = TC - (t == NC - 1)
                for j in range(4):
                    ins = pe.matmul(u[32 * j:32 * j + 32, 0, 0:TP], Vt[0:kn, b % 2, t, 8 * (i % 2) + 4 * g + j, :],
                                    P[0:kn, g, 4 * t + j, :], start=t == 0, stop=t == NC - 1,
                                    tile_position=(0, 32 * j))
                if t == NC - 1:
                    ins.then_inc(v_full, 1)
            elif kind == "wo":
                b = step[1]
                pe.wait_ge(o_lo, 4 * b + 4)
                u = unit(step)
                token_major(u, oh, ol, "o0", 4).then_inc(v_full, 1)
            elif kind in ("r", "fk"):
                b = step[1]
                if kind == "r":
                    if b == 0:
                        pe.wait_ge(w_lo, 3)
                    pe.wait_ge(mix_lo, b + 1)
                u = unit(step)
                if kind == "r":
                    ins = token_major(u, xmh[:, 0], xml[:, 0], "r")
                else:
                    ins = feature_major(u, "fk", xmh[:, 1], xml[:, 1])
                ins.then_inc(a_full, 1)
            elif kind == "kv":
                b = step[1]
                pe.wait_ge(ka_lo, b + 1)
                u = unit(step)
                token_major(u, kah, kal, "fv").then_inc(v_full, 1)
            elif kind in ("q1", "k1", "v1"):
                b = step[1]
                if kind == "q1":
                    if b == 0:
                        pe.wait_ge(w_lo, 5)
                    pe.wait_ge(v_free, V_NO["xt", 2, b] + 1)
                u = unit(step)
                if kind == "v1":
                    token_major(u, XTh[:, b % 2], XTl[:, b % 2], kind).then_inc(v_full, 1)
                else:
                    feature_major(u, kind, XTh[:, b % 2], XTl[:, b % 2]).then_inc(a_full, 1)
            elif kind in ("qe", "ke"):
                b, n = step[1], int(kind == "ke")
                if kind == "ke":
                    pe.wait_ge(sq_ok, b + 1)
                    pe.wait_ge(a_free, A_NO["k1", b] + 1)
                u = unit(step)
                for c in range(2):
                    pe.matmul(u[:, c, 0:TP], rbd[:, :], q1f[:, b % 2, n, c], start=True, stop=False)
                    ins = pe.matmul(u[:, c, 0:TP], neg[:, :], q1s[:, n, c], start=False, stop=True)
                ins.then_inc(a_full, 1)
            elif kind == "kT":
                b = step[1]
                pe.wait_ge(a_free, A_NO["ke", b] + 1)
                u = unit(step)
                for t in range(NC):
                    for c in range(2):
                        ins = pe.transpose(flat(u)[0:TC, D * t + 128 * c:D * t + 128 * c + 128],
                                           q1e[:, b % 2, 1, c, tok(t)], cc("ident"))
                ins.then_inc(v_full, 1)
            elif kind == "kvm":
                b = step[1]
                pe.wait_ge(v_free, V_NO["kT", b] + 1)
                u = unit(step)
                for c in range(2):
                    for t in range(NC):
                        kn = TC - (t == NC - 1)
                        ins = pe.matmul(u[:, c, 0:128], k1t[0:kn, t, 128 * c:128 * c + 128],
                                        v1t[0:kn, t, 128 * c:128 * c + 128], start=t == 0, stop=t == NC - 1)
                ins.then_inc(v_full, 1)
            elif kind == "z":
                b = step[1]
                pe.wait_ge(a_free, A_NO["qe", b] + 1)
                u = unit(step)
                for c in range(2):
                    ins = pe.matmul(u[:, c, 0:TP], cc("mask"), q1e[:, b % 2, 0, c], start=True, stop=True)
                ins.then_inc(v_full, 1)
            elif kind == "o":
                b = step[1]
                pe.wait_ge(v_free, V_NO["kvm", b] + 1)
                u = unit(step)
                for c in range(2):
                    ins = pe.matmul(u[:, c, 0:TP], kvb[:, c], q1e[:, b % 2, 0, c], start=True, stop=True)
                ins.then_inc(v_full, 1)
            elif kind == "wo1":
                b = step[1]
                pe.wait_ge(o1_lo, b + 1)
                u = unit(step)
                token_major(u, o1h[:, b % 2], o1l[:, b % 2], "o1").then_inc(v_full, 1)
            elif kind == "xx":
                b = step[1]
                pe.wait_ge(v_free, V_NO["wo1", b] + 1)
                u = unit(step)
                transposes(u, X[:, b]).then_inc(a_full, 1)
            elif kind == "gate":
                b = step[1]
                if b == 0:
                    pe.wait_ge(w_lo, 6)
                pe.wait_ge(v_free, V_NO["xt", 3, b] + 1)
                u = unit(step)
                for t in range(NC):
                    for c in range(2):
                        ins = exact(u[0:TC, 0, NE * t:NE * t + NE], XMh[:, b, c, tok(t)], XMl[:, b, c, tok(t)],
                                    *w("gate", c), c == 0, c == 1)
                ins.then_inc(v_full, 1)
            elif kind == "cwT":
                b = step[1]
                pe.wait_ge(cw_ok, b + 1)
                u = unit(step)
                for t in range(NC):
                    ins = pe.transpose(u[0:NE, 0, tok(t)], cw[:, b % 2, t, :], cc("ident")[0:TC, 0:TC])
                ins.then_inc(v_full, 1)
            elif kind == "expert":
                _, b, e = step
                n = (NE + 1) * b + e

                def down(b, e):
                    n = (NE + 1) * b + e
                    wh, wl = (Weh[:, e], Wel[:, e]) if e < EARLY else (Wlh[:, e - EARLY], Wll[:, e - EARLY])
                    if e == 0:
                        if b:
                            pe.wait_ge(acc_free, b)
                        for m in range(2):
                            bias_h, bias_l = w("eb", 0, m)
                            pe.matmul(ACC[:, m, 0:TP], bias_h, cwx[:, b, :], start=True, stop=False)
                            pe.matmul(ACC[:, m, 0:TP], bias_l, cwx[:, b, :], start=False, stop=False)
                    pe.wait_ge(h_ok, n + 1)
                    for m in range(2):
                        for c in range(2):
                            a = 4 * D + D * c + 128 * m
                            ins = exact(ACC[:, m, 0:TP], wh[:, a:a + 128], wl[:, a:a + 128],
                                        ehh[:, n % 2, c], ehl[:, n % 2, c], False, e == NE and c == 1)
                    ins.then_inc(down_done, 1)

                wh, wl = (Weh[:, e], Wel[:, e]) if e < EARLY else (Wlh[:, e - EARLY], Wll[:, e - EARLY])
                if n == 0:
                    pe.wait_ge(v_free, len(V_NO))
                    pe.wait_ge(a_free, len(A_NO))
                if b == 0:
                    pe.wait_ge(w_lo, len(PIECES) + e + 1)
                for up, full, free, at in ((UP_A, ma_full, ma_free, 0), (UP_B, mb_full, mb_free, D)):
                    if n:
                        pe.wait_ge(free, n)
                    for m in range(2):
                        for c in range(2):
                            a = 2 * D * c + at + 128 * m
                            ins = exact(up[:, m, 0:TP], wh[:, a:a + 128], wl[:, a:a + 128],
                                        XMh[:, b, c], XMl[:, b, c], c == 0, c == 1)
                    ins.then_inc(full, 1)
                if e:
                    nc_ = NE * b + e - 1
                    if nc_:
                        pe.wait_ge(mc_free, nc_)
                    a = W_COLS["sel"][0] - W_COLS["eb"][0] + 128 * (e - 1)
                    pe.matmul(CWB[:, 0, 0:TP], Ebh[:, a:a + 128], cwx[:, b, :], start=True, stop=True).then_inc(mc_full, 1)
                if n:
                    down((n - 1) // (NE + 1), (n - 1) % (NE + 1))
                if n == B * (NE + 1) - 1:
                    down(b, e)

    @block.scalar
    def _(act):
        def full(step):
            act.wait_ge(a_full, A_NO[step] + 1)
            return unit_of(step)

        def flat(u):
            return u[:, :, :].rearrange("p b n -> p (b n)")

        act.preload_act_table_set("natural_log_exp_and_others")
        act.wait_ge(s_set, 1)
        for step in walk():
            kind = step[0]
            if kind == "split":
                p = step[1]
                n, hi, _, _ = piece(p)
                act.wait_ge(s_stage[p % 2], 16 * (p // 2 + 1))
                if p == 0:
                    act.wait_ge(rot_ok, 1)
                if p == 2:
                    act.wait_ge(a_full, A_NO["v", B - 1] + 1)
                    act.wait_ge(q_lo, 2 * B)
                if p == 5:
                    act.wait_ge(v_free, V_NO["wo", B - 1] + 1)
                if p == len(PIECES) + EARLY:
                    act.wait_ge(v_free, V_NO["wo1", B - 1] + 1)
                act.activation(hi, stage[:, p % 2, 0:n], ACT.Copy).then_inc(w_hi, 1)
            elif kind in ("tok", "st"):
                n = ST_NO[step]
                act.wait_ge(stats, n + 1)
                act.activation(lnv[:, n, :], mv[:, n, :, 1], ACT.Ln, bias=eps[0:TC, :]).then_inc(lnv_ok, 1)
                act.wait_ge(lnv_ok, n + 1)
                act.activation(rst0[:, n, :], lnv[:, n, :], ACT.Exp, scale=-0.5).then_inc(rst0_ok, 1)
            elif kind in ("q", "k"):
                b, r = step[1], 2 * step[1] + (kind == "k")
                u = full(step)
                if r >= 2:
                    act.wait_ge(q_lo, r - 1)
                act.activation(qf[:, r % 2], u[:, :, 0:TP], ACT.Copy).then_inc(a_free, 1)
            elif kind == "v":
                b = step[1]
                u = full(step)
                if b == 0:
                    act.wait_ge(s_set, 6)
                if b >= 2:
                    act.wait_ge(v_full, V_NO["pv", 2 * b - 3, 1, NC - 1] + 1)
                for t in range(NC):
                    ins = act.activation(Vt[:, b % 2, t, :, 0:HD],
                                         flat(u)[0:TC, D * t:D * t + D].rearrange("p (h d) -> p h d", d=HD), ACT.Copy)
                ins.then_inc(a_free, 1)
            elif kind == "qsplit":
                r = step[1]
                act.wait_ge(a_free, A_NO["qk"[r % 2], r // 2] + 1)
                if r >= 2:
                    act.wait_ge(s_scr[r % 2], 32 * (r // 2))
                act.activation(qh[:, r % 2], qf[:, r % 2], ACT.Copy).then_inc(q_hi, 1)
            elif kind == "p2":
                _, i, n = step
                g = n // 6
                u = full(step)
                if i == 0 and n == 0:
                    act.wait_ge(v_full, V_NO["tok", B - 1] + 1)
                if i and n % 6 == 0:
                    act.wait_ge(v_full, V_NO["pv", i - 1, g, NC - 1] + 1)
                k = 2 * n - 12 * g
                act.activation(P[:, g, k:k + 2, :], u[0:TC, :, 0:TP], ACT.Exp, scale=HD ** -0.5).then_inc(a_free, 1)
            elif kind == "osplit":
                _, i, g = step
                q = 2 * i + g
                act.wait_ge(v_free, V_NO["pv", i, g, NC - 1] + 1)
                if q % 4 == 0 and q:
                    act.wait_ge(v_full, V_NO["wo", i // 2 - 1] + 1)
                act.activation(oh[:, q % 4, :], of[:, q % 2, :], ACT.Copy).then_inc(o_hi, 1)
            elif kind == "mix":
                b = step[1]
                act.wait_ge(mix_ok, b + 1)
                if b:
                    act.wait_ge(a_full, A_NO["fk", b - 1] + 1)
                act.activation(xmh[:, :, :, :].rearrange("p a c t -> p (a c t)"),
                               xm[:, :, :, :].rearrange("p a c t -> p (a c t)"), ACT.Copy).then_inc(mix_hi, 1)
            elif kind == "r":
                b = step[1]
                u = full(step)
                if b:
                    act.wait_ge(v_free, V_NO["kv", b - 1] + 1)
                act.activation(er[:, :, :].rearrange("p t d -> p (t d)"), flat(u)[0:TC, 0:NC * D], ACT.Exp,
                               scale=-1.0).then_inc(a_free, 1)
            elif kind == "fk":
                b = step[1]
                u = full(step)
                if b:
                    act.wait_ge(ka_ok, b)
                act.activation(kr[:, :, :], u[:, :, 0:TP], ACT.Relu).then_inc(a_free, 1)
                act.wait_ge(a_free, A_NO[step] + 1)
                if b:
                    act.wait_ge(ka_lo, b)
                act.activation(ka[:, :, :], kr[:, :, :], ACT.Square).then_inc(ka_ok, 1)
                act.wait_ge(ka_ok, b + 1)
                if b:
                    act.wait_ge(v_full, V_NO["kv", b - 1] + 1)
                act.activation(kah[:, :, :], ka[:, :, :], ACT.Copy).then_inc(ka_hi, 1)
            elif kind in ("q1", "k1"):
                b, n = step[1], int(kind == "k1")
                u = full(step)
                if b >= 2:
                    act.wait_ge(a_full, A_NO["qe", b - 2] + 1)
                for c in range(2):
                    bias = cc("bk" if n else "bq")[:, c:c + 1]
                    ins = act.activation(q1f[:, b % 2, n, c], u[:, c, 0:TP], ACT.Identity, bias=bias)
                ins.then_inc(a_free, 1)
            elif kind in ("qe", "ke"):
                b, n = step[1], int(kind == "ke")
                u = full(step)
                if b >= 2:
                    act.wait_ge(v_full, V_NO["o" if n == 0 else "kT", b - 2] + 1)
                act.activation(q1e[:, b % 2, n], u[:, :, 0:TP], ACT.Exp).then_inc(a_free, 1)
            elif kind == "o1split":
                b = step[1]
                act.wait_ge(v_free, V_NO["o", b] + 1)
                if b >= 2:
                    act.wait_ge(v_full, V_NO["wo1", b - 2] + 1)
                act.activation(o1h[:, b % 2], o1f[:, :, :], ACT.Copy).then_inc(o1_hi, 1)
            elif kind == "xx":
                b = step[1]
                u = full(step)
                act.activation(XF[:, b], u[:, :, 0:TP], ACT.Copy).then_inc(a_free, 1)
            elif kind == "gate":
                b = step[1]
                act.wait_ge(v_free, V_NO[step] + 1)
                act.activation(ge[:, b % 2], glog[:, :, :], ACT.Exp).then_inc(ge_ok, 1)
            elif kind == "expert":
                _, b, e = step
                n = (NE + 1) * b + e
                if n == 0:
                    act.wait_ge(v_full, len(V_NO))
                    act.wait_ge(a_full, len(A_NO))
                act.wait_ge(ma_full, n + 1)
                if n >= 2:
                    act.wait_ge(mb_free, n - 1)
                for m in range(2):
                    a = C_COLS["b1"][0] + 4 * e + m
                    ins = act.activation(es[:, n % 2, m], UP_A[:, m, 0:TP], ACT.Silu, bias=cst[:, a:a + 1])
                ins.then_inc(ma_free, 1)

    @block.gpsimd
    def _(pool):
        pool.memset(eps[:, :], EPS).then_inc(s_set, 1)
        pool.memset(Vt[:, :, :, :, HD:32], 0.0).then_inc(s_set, 1)
        pool.wait_ge(s_set, 2)
        pool.memset(Vt[:, :, :, :, HD:HD + 1], 1.0).then_inc(s_set, 1)
        pool.wait_ge(s_set, 3)
        pool.memset(Qst[64:128, :, :, :].bitcast(F32), 0.0)
        pool.memset(Kst[64:128, :, :, :].bitcast(F32), 0.0).then_inc(s_set, 1)
        pool.wait_ge(s_set, 4)
        pool.memset(Kst[96:98, :, :, :].bitcast(F32), 1.0).then_inc(s_set, 1)
        pool.wait_ge(s_set, 5)
        pool.wait_ge(s_cst, 48)
        pool.tensor_scalar(neg[:, :], cc("mask"), -0.5 / HD, None, ALU.mult)
        pool.tensor_scalar(rbd[:, :], cc("rbd"), HD ** -0.5, None, ALU.mult).then_inc(s_set, 1)
        for step in walk():
            kind = step[0]
            if kind in ("tok", "st"):
                n = ST_NO[step]
                pool.wait_ge(rst0_ok, n + 1)
                r0, t = rst0[:, n, :], nwt[:, n, :]
                pool.tensor_tensor(t, r0, r0, ALU.mult).then_inc(newton, 1)
                pool.wait_ge(newton, 4 * n + 1)
                pool.tensor_scalar(lnv[:, n, :], mv[:, n, :, 1], EPS, -0.5, ALU.add, ALU.mult).then_inc(newton, 1)
                pool.wait_ge(newton, 4 * n + 2)
                pool.tensor_tensor(t, t, lnv[:, n, :], ALU.mult).then_inc(newton, 1)
                pool.wait_ge(newton, 4 * n + 3)
                pool.tensor_scalar(t, t, 1.5, None, ALU.add).then_inc(newton, 1)
                pool.wait_ge(newton, 4 * n + 4)
                pool.tensor_tensor(rstd[:, n, :], t, r0, ALU.mult).then_inc(rstd_ok, 1)
            elif kind == "split":
                p = step[1]
                _, hi, lo, n = piece(p)
                pool.wait_ge(w_hi, p + 1)
                pool.tensor_tensor(lo, stage[:, p % 2, 0:n], hi[:, 0:n].bitcast(F32), ALU.subtract).then_inc(w_lo, 1)
                if p == 5:
                    pool.memset(cwx[:, :, :].bitcast(F32), 0.0).then_inc(s_set, 1)
                    pool.wait_ge(s_set, 7)
                    pool.memset(cwx[32:33, :, :].bitcast(F32), 1.0).then_inc(s_set, 1)
                    pool.wait_ge(s_set, 8)
            elif kind == "qsplit":
                r = step[1]
                pool.wait_ge(q_hi, r + 1)
                pool.tensor_tensor(ql[:, r % 2], qf[:, r % 2], qh[:, r % 2].bitcast(F32),
                                   ALU.subtract).then_inc(q_lo, 1)
            elif kind == "osplit":
                _, i, g = step
                q = 2 * i + g
                pool.wait_ge(o_hi, q + 1)
                pool.tensor_tensor(ol[:, q % 4, :], of[:, q % 2, :], oh[:, q % 4, :].bitcast(F32),
                                   ALU.subtract).then_inc(o_lo, 1)
            elif kind == "mix":
                b = step[1]
                pool.wait_ge(mix_hi, b + 1)
                pool.tensor_tensor(xml[:, :, :, :].rearrange("p a c t -> p (a c t)"),
                                   xm[:, :, :, :].rearrange("p a c t -> p (a c t)"),
                                   xmh[:, :, :, :].bitcast(F32).rearrange("p a c t -> p (a c t)"),
                                   ALU.subtract).then_inc(mix_lo, 1)
            elif kind == "fk":
                b = step[1]
                pool.wait_ge(ka_hi, b + 1)
                pool.tensor_tensor(kal[:, :, :], ka[:, :, :], kah[:, :, :].bitcast(F32), ALU.subtract).then_inc(ka_lo, 1)
            elif kind == "sq":
                b = step[1]
                pool.wait_ge(a_free, A_NO["k1", b] + 1)
                if b:
                    pool.wait_ge(a_full, A_NO["qe", b - 1] + 1)
                pool.tensor_tensor(q1s[:, :, :, :], q1f[:, b % 2], q1f[:, b % 2], ALU.mult).then_inc(sq_ok, 1)
                pool.wait_ge(xn_ok, LN_NO["ln", 2, b] + 1)
                pool.tensor_tensor(X[:, b], X[:, b], rr("bo").unsqueeze(1).broadcast_to([TC, NC, D]),
                                   ALU.add).then_inc(bo_ok, 1)
            elif kind == "o1split":
                b = step[1]
                pool.wait_ge(o1_hi, b + 1)
                pool.tensor_tensor(o1l[:, b % 2], o1f[:, :, :], o1h[:, b % 2].bitcast(F32), ALU.subtract).then_inc(o1_lo, 1)

    @block.vector
    def _(dve):
        steps = [0]

        def link(ins):
            steps[0] += 1
            ins.then_inc(dve_step, 1)
            dve.wait_ge(dve_step, steps[0])

        def full(step):
            dve.wait_ge(v_full, V_NO[step] + 1)
            return unit_of(step)

        def flat(u):
            return u[:, :, :].rearrange("p b n -> p (b n)")

        def statistics(src, n):
            for t in range(NC):
                ins = dve.bn_stats(st[:, t, :], src[:, t])
            link(ins)
            for t in range(NC):
                ins = dve.bn_aggr(mv[:, n, t, :], st[:, t, :])
            ins.then_inc(stats, 1)
            dve.wait_ge(stats, n + 1)

        def split(hi, lo, src, semaphore):
            link(dve.tensor_copy(hi, src))
            dve.tensor_tensor(lo, src, hi.bitcast(F32), ALU.subtract).then_inc(semaphore, 1)

        def finish(b):
            dve.wait_ge(down_done, (NE + 1) * (b + 1))
            if b >= 2:
                dve.wait_ge(s_out[b % 2], 16 * (b // 2))
            dve.tensor_tensor(outb[:, b % 2], ACC[:, :, 0:TP], XF[:, b], ALU.add).then_inc(acc_free, 1)

        dve.wait_ge(s_cst, 48)
        dve.wait_ge(s_stage[0], 16)
        a = W_COLS["q0"][0]
        wqk = stage[:, 0, a:a + 3 * D].rearrange("p (n d) -> p n d", d=D)
        cos3, sin3 = (cc(name).unsqueeze(1).broadcast_to([128, 3, D]) for name in ("cos", "sin"))
        dve.tensor_tensor(wcos[:, :, :], wqk, cos3, ALU.mult)
        for even in range(2):
            ins = dve.tensor_tensor(wsin[:, :, even::2], wqk[:, :, 1 - even::2], sin3[:, :, even::2], ALU.mult)
        link(ins)
        dve.tensor_tensor(wqk, wcos[:, :, :], wsin[:, :, :], ALU.add).then_inc(rot_ok, 1)
        for step in walk():
            kind = step[0]
            if kind == "tok":
                b, n = step[1], ST_NO[step]
                u = full(step)
                uu = flat(u)[0:TC, 0:NC * D].rearrange("p (t d) -> p t d", d=D)
                statistics(uu, n)
                for t in range(NC):
                    ins = dve.scalar_tensor_tensor(X[:, b, t, :], uu[:, t, :], mv[:, n, t, 0:1], rr("gamma"),
                                                   ALU.subtract, ALU.mult)
                ins.then_inc(v_free, 1)
                dve.wait_ge(v_free, V_NO[step] + 1)
            elif kind == "tokn":
                b, n = step[1], ST_NO["tok", step[1]]
                dve.wait_ge(rstd_ok, n + 1)
                dve.scalar_tensor_tensor(X[:, b, 0, :], X[:, b, 0, :], rstd[:, n, 0:1], cls[:, :], ALU.mult, ALU.add)
                for t in range(1, NC):
                    ins = dve.tensor_scalar(X[:, b, t, :], X[:, b, t, :], rstd[:, n, t:t + 1], None, ALU.mult)
                link(ins)
            elif kind == "st":
                _, s, b = step
                statistics(X[:, b], ST_NO[step])
            elif kind == "ln":
                _, s, b = step
                n = ST_NO["st", s, b]
                dve.wait_ge(rstd_ok, n + 1)
                for t in range(NC):
                    ins = dve.tensor_scalar(xn[:, b % 2, t, :], X[:, b, t, :], mv[:, n, t, 0:1], rstd[:, n, t:t + 1],
                                            ALU.subtract, ALU.mult)
                ins.then_inc(xn_ok, 1)
            elif kind == "xt":
                _, s, b = step
                if s in (0, 2) and b >= 2:
                    if s == 0:
                        dve.wait_ge(a_full, A_NO["q", b - 2] + 1)
                        dve.wait_ge(v_full, V_NO["lat", b - 2] + 1)
                    else:
                        dve.wait_ge(v_full, V_NO["v1", b - 2] + 1)
                        dve.wait_ge(a_full, A_NO["k1", b - 2] + 1)
                u = full(step)
                if s == 1:
                    if b == 0:
                        dve.wait_ge(v_free, V_NO["wo", B - 1] + 1)
                        dve.memset(xf[:, :, 0:1], 0.0)
                    dve.tensor_copy(xf[:, :, 1:TP + 1], u[:, :, 0:TP]).then_inc(v_free, 1)
                    dve.wait_ge(v_free, V_NO[step] + 1)
                elif s == 3:
                    split(XMh[:, b], XMl[:, b], u[:, :, 0:TP], v_free)
                else:
                    split(XTh[:, b % 2], XTl[:, b % 2], u[:, :, 0:TP], v_free)
            elif kind == "lat":
                b = step[1]
                if b >= 2:
                    dve.wait_ge(a_full, A_NO["v", b - 2] + 1)
                u = full(step)
                split(lath[:, b % 2], latl[:, b % 2], u[:, 0, 0:TP], v_free)
            elif kind == "p1":
                _, i, n = step
                u = full(step)
                if n == 0 and i >= 2:
                    dve.wait_ge(v_full, V_NO["mT", i - 2] + 1)
                a = 2 * (n % 4)
                dve.tensor_reduce(mx[:, i % 2, n // 4, a:a + 2], u[0:TC, :, 0:T], AX, ALU.max).then_inc(v_free, 1)
            elif kind == "mT":
                i = step[1]
                u = full(step)
                if i >= 2:
                    dve.wait_ge(s_mrow[(i - 2) % 3], 32 * ((i - 2) // 3 + 1))
                link(dve.tensor_scalar(nm[:, i % 2, 0, :], u[0:8, 0, 0:TP], -1.0, None, ALU.mult))
                dve.scalar_tensor_tensor(nm[:, i % 2, 1, :], u[0:8, 0, 0:TP], -1.0, nm[:, i % 2, 0, :].bitcast(F32),
                                         ALU.mult, ALU.subtract).then_inc(v_free, 1)
            elif kind == "pv" and step in LAST:
                _, i, g, _ = step
                q = 2 * i + g
                u = full(step)
                link(dve.stream_shuffle(den[:, :], u[:, 0, 0:TP], [HD] * 32))
                if q:
                    last = ("pv", i, 0) if g else ("pv", i - 1, 1)
                    dve.wait_ge(v_free, no_last(last) + 1)
                link(dve.reciprocal(rec[:, :], den[:, :]))
                if q >= 2:
                    dve.wait_ge(o_lo, q - 1)
                dve.tensor_tensor(of[:, q % 2, :], u[:, 0, 0:TP], rec[:, :], ALU.mult).then_inc(v_free, 1)
            elif kind in ("wo", "wo1"):
                b = step[1]
                if kind == "wo1":
                    dve.wait_ge(bo_ok, b + 1)
                u = full(step)
                xb = X[:, b].rearrange("p t d -> p (t d)")
                dve.tensor_tensor(xb, xb, flat(u)[0:TC, 0:NC * D], ALU.add).then_inc(v_free, 1)
                dve.wait_ge(v_free, V_NO[step] + 1)
            elif kind == "mix":
                b = step[1]
                link(dve.tensor_tensor(dx[:, :, :], xf[:, :, 1:TP + 1], xf[:, :, 0:TP], ALU.subtract))
                if b:
                    dve.wait_ge(mix_lo, b)
                for k, name in enumerate(("mu_r", "mu_k")):
                    for c in range(2):
                        ins = dve.scalar_tensor_tensor(xm[:, k, c], dx[:, c], cc(name)[:, c:c + 1], xf[:, c, 0:TP],
                                                       ALU.mult, ALU.add)
                ins.then_inc(mix_ok, 1)
                dve.wait_ge(mix_ok, b + 1)
            elif kind == "kv":
                b = step[1]
                dve.wait_ge(a_free, A_NO["r", b] + 1)
                link(dve.tensor_scalar(sig[:, :, :], er[:, :, :], 1.0, None, ALU.add))
                link(dve.reciprocal(er[:, :, :], sig[:, :, :]))
                u = full(step)
                ee = er[:, :, :].rearrange("p t d -> p (t d)")
                dve.tensor_tensor(sig[:, :, :].rearrange("p t d -> p (t d)"), flat(u)[0:TC, 0:NC * D], ee,
                                  ALU.mult).then_inc(v_free, 1)
                dve.wait_ge(v_free, V_NO[step] + 1)
                link(dve.tensor_tensor(X[:, b], X[:, b], sig[:, :, :], ALU.add))
            elif kind == "v1":
                b = step[1]
                u = full(step)
                if b:
                    dve.wait_ge(v_full, V_NO["kvm", b - 1] + 1)
                dve.tensor_tensor(v1t[:, :, :], flat(u)[0:TC, 0:NC * D].rearrange("p (t d) -> p t d", d=D),
                                  rr("bv").unsqueeze(1).broadcast_to([TC, NC, D]), ALU.add).then_inc(v_free, 1)
            elif kind == "kT":
                b = step[1]
                u = full(step)
                if b:
                    dve.wait_ge(v_full, V_NO["kvm", b - 1] + 1)
                dve.tensor_copy(k1t[:, :, :].rearrange("p t d -> p (t d)"), flat(u)[0:TC, 0:NC * D]).then_inc(v_free, 1)
            elif kind == "kvm":
                b = step[1]
                u = full(step)
                if b:
                    dve.wait_ge(v_full, V_NO["o", b - 1] + 1)
                dve.tensor_tensor(kvb[:, :, :], u[:, :, 0:128], cc("mask").unsqueeze(1).broadcast_to([128, 2, 128]),
                                  ALU.mult).then_inc(v_free, 1)
            elif kind == "z":
                if step[1]:
                    dve.wait_ge(v_free, V_NO["o", step[1] - 1] + 1)
                u = full(step)
                dve.tensor_scalar(zz[:, :, :], u[:, :, 0:TP], 1e-8, None, ALU.add).then_inc(v_free, 1)
                dve.wait_ge(v_free, V_NO[step] + 1)
                link(dve.reciprocal(zr[:, :, :], zz[:, :, :]))
            elif kind == "o":
                b = step[1]
                u = full(step)
                if b:
                    dve.wait_ge(o1_lo, b)
                dve.tensor_tensor(o1f[:, :, :], u[:, :, 0:TP], zr[:, :, :], ALU.mult).then_inc(v_free, 1)
            elif kind == "gate":
                b = step[1]
                u = full(step)
                lg = u[0:TC, 0, 0:NC * NE].rearrange("p (t e) -> p t e", e=NE)
                bc = [TC, NC, NE]
                if b:
                    dve.wait_ge(cw_ok, b)
                if b:
                    dve.wait_ge(v_free, V_NO["gate", b - 1] + 1)
                link(dve.tensor_tensor(gp[:, :, :], lg, rr("gate_b").unsqueeze(1).broadcast_to(bc), ALU.add))
                link(dve.tensor_reduce(gm[:, :], gp[:, :, :], AX, ALU.max))
                if b:
                    dve.wait_ge(ge_ok, b)
                dve.tensor_tensor(glog[:, :, :], gp[:, :, :], gm[:, :].unsqueeze(2).broadcast_to(bc),
                                  ALU.subtract).then_inc(v_free, 1)
            elif kind == "cwT":
                b = step[1]
                bc, b4 = [TC, NC, NE], [TC, NC, NE, NE]
                dve.wait_ge(ge_ok, b + 1)
                dve.wait_ge(v_free, V_NO["gate", b] + 1)
                link(dve.tensor_reduce(gs[:, :], ge[:, b % 2], AX, ALU.add))
                link(dve.reciprocal(gr[:, :], gs[:, :]))
                link(dve.tensor_tensor(gp[:, :, :], ge[:, b % 2], gr[:, :].unsqueeze(2).broadcast_to(bc), ALU.mult))
                p_j, p_e = gp[:, :, :].unsqueeze(2).broadcast_to(b4), gp[:, :, :].unsqueeze(3).broadcast_to(b4)
                before = rr("before").rearrange("p (e j) -> p e j", j=NE).unsqueeze(1).broadcast_to(b4)
                gt4, gq4 = (x[:, :, :].rearrange("p t (e j) -> p t e j", j=NE) for x in (gt, gq))
                link(dve.tensor_tensor(gq4, p_j, p_e, ALU.is_equal))
                link(dve.tensor_tensor(gq4, gq4, before, ALU.mult))
                link(dve.tensor_tensor(gt4, p_j, p_e, ALU.is_gt))
                link(dve.tensor_tensor(gt4, gt4, gq4, ALU.add))
                link(dve.tensor_reduce(rank[:, :, :], gt4, AX, ALU.add))
                dve.scalar_tensor_tensor(cw[:, b % 2], rank[:, :, :], 2.0, gp[:, :, :], ALU.is_lt, ALU.mult).then_inc(cw_ok, 1)
                if b == 0:
                    dve.wait_ge(s_set, 8)
                u = full(step)
                link(dve.tensor_copy(cwx[0:NE, b, :], u[0:NE, 0, 0:TP]))
                dve.tensor_tensor(cwx[64:64 + NE, b, :], u[0:NE, 0, 0:TP], cwx[0:NE, b, :].bitcast(F32),
                                  ALU.subtract).then_inc(v_free, 1)
            elif kind == "expert":
                _, b, e = step
                n = (NE + 1) * b + e
                dve.wait_ge(ma_free, n + 1)
                dve.wait_ge(mb_full, n + 1)
                g = eg if e else ehf
                if n:
                    dve.wait_ge(h_ok, n)
                for m in range(2):
                    a = C_COLS["b1"][0] + 4 * e + 2 + m
                    ins = dve.scalar_tensor_tensor(g[:, m], UP_B[:, m, 0:TP], cst[:, a:a + 1], es[:, n % 2, m],
                                                   ALU.add, ALU.mult)
                ins.then_inc(mb_free, 1)
                dve.wait_ge(mb_free, n + 1)
                if e:
                    k = NE * b + e - 1
                    dve.wait_ge(mc_full, k + 1)
                    dve.tensor_tensor(ehf[:, :, :], eg[:, :, :], CWB[:, 0:1, 0:TP].broadcast_to([128, 2, TP]),
                                      ALU.mult).then_inc(mc_free, 1)
                    dve.wait_ge(mc_free, k + 1)
                if n >= 2:
                    dve.wait_ge(down_done, n - 1)
                split(ehh[:, n % 2], ehl[:, n % 2], ehf[:, :, :], h_ok)
                if e == 0 and b:
                    finish(b - 1)
                if n == B * (NE + 1) - 1:
                    finish(b)

    ctx.close()


def _layout(x, cls_tok, w):
    f = np.float32

    def halves(a):
        a = np.asarray(a)
        return np.concatenate([a[0:128], a[128:256]], axis=1)

    patches = np.asarray(x).reshape(B, 5, 16, 8, 16, 8).transpose(1, 3, 5, 0, 2, 4).reshape(320, B, D)
    xp = np.zeros((NC * KP, B, TP), f)
    xp[0:320, :, 1:T] = patches
    xp = np.ascontiguousarray(xp.reshape(NC, KP, B, TP).transpose(1, 0, 2, 3))
    wt = np.zeros((NC * KP, D), f)
    wt[0:320] = w["L0_tok_W"]
    wt = np.ascontiguousarray(wt.reshape(NC, KP, D).transpose(1, 0, 2))

    pack = np.zeros((128, W_TOTAL), f)

    def put(name, a):
        at, n = W_COLS[name]
        assert a.shape[1] == n
        pack[0:a.shape[0], at:at + n] = a

    w = {k: np.asarray(v) for k, v in w.items()}
    put("lat", halves(np.concatenate([w["L0_attn_wk_a"].T, w["L0_attn_wv_a"].T], axis=1)))
    put("q0", halves(w["L0_attn_wq"].T))
    put("k0", w["L0_attn_wk_b"].T)
    put("v0", np.concatenate([np.zeros((64, D), f), w["L0_attn_wv_b"].T]))
    o0 = np.zeros((4, 4, 32, D), f)
    o0[:, :, 0:HD] = w["L0_attn_wo"].T.reshape(4, 4, HD, D)
    put("o0", o0.reshape(4, 128, D).transpose(1, 0, 2).reshape(128, 4 * D))
    for name, key in (("r", "L0_ffn_W_r"), ("fk", "L0_ffn_W_k"), ("fv", "L0_ffn_W_v"), ("q1", "L1_attn_Wq"),
                      ("k1", "L1_attn_Wk"), ("v1", "L1_attn_Wv"), ("o1", "L1_attn_Wo")):
        put(name, halves(w[key].T))
    eb = np.zeros((128, D), f)
    eb[0:NE] = eb[64:64 + NE] = w["L1_ffn_rb2"]
    eb[32] = w["L1_ffn_sb2"][0]
    put("eb", eb)
    put("gate", halves(w["L1_ffn_gate_w"]))
    sel = np.zeros((128, NE, 128), f)
    for e in range(NE):
        sel[e, e] = sel[64 + e, e] = 1.0
    put("sel", sel.reshape(128, NE * 128))

    experts = np.zeros((NE + 1, 128, EXPERT), f)
    w1 = np.concatenate([w["L1_ffn_sw1"], w["L1_ffn_rw1"]])
    w2 = np.concatenate([w["L1_ffn_sw2"], w["L1_ffn_rw2"]])
    b1 = np.concatenate([w["L1_ffn_sb1"], w["L1_ffn_rb1"]])
    for e in range(NE + 1):
        experts[e, :, 0:4 * D] = halves(w1[e])
        experts[e, :, 4 * D:] = halves(w2[e])

    con = np.zeros((128, C_TOTAL), f)

    def const(name, a):
        at, n = C_COLS[name]
        con[:, at:at + n] = np.asarray(a).reshape(128, n)

    inv = (1.0 / 10000.0 ** (np.arange(0, HD, 2, dtype=f) / f(HD))).astype(f)
    angle = np.repeat(np.arange(NH, dtype=f)[:, None] * inv[None, :], 2, axis=1).reshape(1, D)
    sign = np.where(np.arange(D) % 2 == 0, f(-1), f(1))
    const("cos", np.repeat(np.cos(angle), 128, axis=0))
    const("sin", np.repeat(np.sin(angle) * sign, 128, axis=0))
    block = np.arange(128) // HD
    const("mask", (block[:, None] == block[None, :]).astype(f))
    rbd = np.zeros((128, 128), f)
    for h in range(8):
        rbd[HD * h:HD * h + HD, HD * h:HD * h + HD] = w["L1_attn_R"]
    const("rbd", rbd)
    const("ident", np.eye(128, dtype=f))
    for name, key in (("mu_r", "L0_ffn_mu_r"), ("mu_k", "L0_ffn_mu_k"), ("bq", "L1_attn_bq"), ("bk", "L1_attn_bk")):
        const(name, w[key].reshape(2, 128).T)
    const("b1", b1.reshape(NE + 1, 4, 128).transpose(2, 0, 1).reshape(128, -1))

    rows = np.zeros((1, R_TOTAL), f)
    before = (np.arange(NE)[None, :] < np.arange(NE)[:, None]).astype(f)
    for name, a in (("gamma", w["L0_tok_gamma"]), ("bv", w["L1_attn_bv"]), ("bo", w["L1_attn_bo"]),
                    ("gate_b", w["L1_ffn_gate_b"]), ("before", before)):
        at, n = R_COLS[name]
        rows[0, at:at + n] = a.reshape(n)
    cls_rows = np.zeros((TC, D), f)
    cls_rows[0] = np.asarray(cls_tok).reshape(D)
    return {"patches": xp, "w_tok": wt, "rows": rows, "cls_rows": cls_rows, "consts": con,
            "weights": pack, "experts": experts}


def kernel(x, cls_tok, **w):
    import concourse.bacc as bacc
    from concourse.bass_utils import run_bass_kernel_spmd

    nc = bacc.Bacc("TRN2", target_bir_lowering=False, num_devices=1)
    arrays = _layout(x, cls_tok, w)
    args = [nc.dram_tensor(name, a.shape, F32, kind="ExternalInput").ap() for name, a in arrays.items()]
    out = nc.dram_tensor("tower_out", (B, D, TP), F32, kind="ExternalOutput").ap()
    tower(nc, *args, out)
    got = run_bass_kernel_spmd(nc, [arrays], core_ids=[0]).results[0]["tower_out"]
    return np.ascontiguousarray(got.transpose(0, 2, 1)[:, 0:T, :])
```

```python
from contextlib import ExitStack

import numpy as np

import concourse.bass as bass
from concourse import mybir

B = 4
T = 257
TP = 258
TC = 86
NC = 3
D = 256
NH = 16
HD = 16
KP = 107
NE = 8
EPS = 1e-5
F32 = mybir.dt.float32
F32R = mybir.dt.float32r
ALU = mybir.AluOpType
ACT = mybir.ActivationFunctionType
AX = mybir.AxisListType.X

W_COLS = {}
_at = 0
for _name, _n in (("lat", 2 * 128), ("q0", 2 * D), ("k0", D), ("v0", D), ("o0", 4 * D),
                  ("r", 2 * D), ("fk", 2 * D), ("fv", 2 * D),
                  ("q1", 2 * D), ("k1", 2 * D), ("v1", 2 * D), ("o1", 2 * D),
                  ("eb", D), ("gate", 2 * NE), ("sel", NE * 128)):
    W_COLS[_name] = (_at, _n)
    _at += _n
W_TOTAL = _at
EXPERT = 2 * 2 * D + 2 * D
PIECES = [("lat", "v0"), ("o0", "o0"), ("r", "fv"), ("q1", "k1"), ("v1", "o1"), ("eb", "sel")]

C_COLS = {}
_at = 0
for _name, _n in (("cos", D), ("sin", D), ("mask", 128), ("rbd", 128), ("ident", 128),
                  ("mu_r", 2), ("mu_k", 2), ("bq", 2), ("bk", 2), ("b1", 4 * (NE + 1))):
    C_COLS[_name] = (_at, _n)
    _at += _n
C_TOTAL = _at
R_COLS = {}
_at = 0
for _name, _n in (("gamma", D), ("bv", D), ("bo", D), ("gate_b", NE), ("before", NE * NE)):
    R_COLS[_name] = (_at, _n)
    _at += _n
R_TOTAL = _at


AT = {
    "s_split0": -34.0, "s_tok0": -32.0, "s_tokn0": -29.0, "s_st0": -28.0, "s_tok1": -29.25,
    "s_ln0": -27.0, "s_xt0": -25.0, "s_tokn1": -21.0, "s_st1": -20.0, "s_tok2": -26.0, "s_q0": -24.0,
    "s_qs0": -22.25, "s_lat0": -22.0, "s_tokn2": -12.5, "s_st2": -11.0, "s_k0": -19.25, "s_qs1": -17.75,
    "s_stk0": -15.25, "s_stk1": -16.0, "s_v0": 10.5, "s_tok3": -15.0, "s_ln1": -7.0, "s_xt1": -5.25,
    "s_tokn3": -5.5, "s_q1": -4.5, "s_qs2": -4.4, "s_lat1": -0.5, "s_st3": -5.4, "s_k1": 2.55,
    "s_qs3": 4.06, "s_v1": 14.25, "s_stk2": 5.0, "s_split1": 8.0,
    "ln0": 0.0, "xt0": 1.0, "q": 3.0, "qs": 3.1, "lat": 4.75, "k": 6.0, "ks": 10.1, "v": 21.0,
    "mT": 12.05, "LAG": 18.0, "pv0": 5.2, "pv1": 6.7, "pv2": 7.2, "norm": 9.55,
    "wo": 31.9,
    "FFN": 86.5, "FFN_STEP": 11.5, "FFN_LAST": 130.25,
    "ln1": 0.0, "xf": 2.0, "mix": 4.0, "mixl": 5.5, "r": 8.5, "fk": 9.0, "fkl": 10.25, "kv": 13.0,
    "LAYER1": 129.5, "LAYER1_STEP": 5.0,
    "ln2": 0.25, "xt2": 2.75, "q1": 4.25, "v1": 5.25, "ke": 7.25, "kT": 8.75, "z": 9.1, "kvm": 9.25, "zn": 11.75,
    "o": 12.85, "o1l": 13.25, "wo1": 14.25, "ln3": 16.75, "xt3": 17.75, "gl": 18.25, "gate": 20.25, "cwT": 22.5,
    "W2": 72.25, "W3": 74.25, "W4": 85.0, "W5": 128.5, "E0": 146.0, "E1": 148.5, "E2": 154.0, "E3": 160.25,
}


def timetable():
    lag = AT["LAG"]
    for name, step in (
            ("s_split0", ("split", 0)), ("s_tok0", ("tok", 0)), ("s_tokn0", ("tokn", 0)),
            ("s_st0", ("st", 0, 0)), ("s_tok1", ("tok", 1)), ("s_ln0", ("ln", 0, 0)), ("s_xt0", ("xt", 0, 0)),
            ("s_tokn1", ("tokn", 1)), ("s_st1", ("st", 0, 1)), ("s_tok2", ("tok", 2)), ("s_q0", ("q", 0)),
            ("s_qs0", ("qsplit", 0)), ("s_lat0", ("lat", 0)), ("s_tokn2", ("tokn", 2)), ("s_st2", ("st", 0, 2)),
            ("s_k0", ("k", 0)), ("s_qs1", ("qsplit", 1)), ("s_stk0", ("stk", 0)), ("s_stk1", ("stk", 1)),
            ("s_v0", ("v", 0)), ("s_tok3", ("tok", 3)), ("s_ln1", ("ln", 0, 1)), ("s_xt1", ("xt", 0, 1)),
            ("s_tokn3", ("tokn", 3)), ("s_q1", ("q", 1)), ("s_qs2", ("qsplit", 2)), ("s_lat1", ("lat", 1)),
            ("s_st3", ("st", 0, 3)), ("s_k1", ("k", 1)), ("s_qs3", ("qsplit", 3)), ("s_v1", ("v", 1)),
            ("s_stk2", ("stk", 2)), ("s_split1", ("split", 1))):
        yield AT[name], step
    for i in range(2 * B):
        for n in range(12):
            yield 12 * i + n, ("p1", i, n)
            yield 12 * i + n + lag + 0.1, ("p2", i, n)
        yield 12 * i + AT["mT"], ("mT", i)
        if i >= 3:
            yield 12 * i - 25 + lag + 0.15, ("stk", i)
        for g in range(2):
            at = 12 * i + 6 * g + lag
            for t in range(NC):
                yield at + AT[f"pv{t}"], ("pv", i, g, t)
            yield at + AT["norm"], ("pvn", i, g)
            yield at + AT["norm"], ("osplit", i, g)
    for b in range(2, B):
        for name, step in (("ln0", ("ln", 0, b)), ("xt0", ("xt", 0, b)), ("q", ("q", b)), ("qs", ("qsplit", 2 * b)),
                           ("lat", ("lat", b)), ("k", ("k", b)), ("ks", ("qsplit", 2 * b + 1)), ("v", ("v", b))):
            yield 24 * (b - 1) + AT[name] - 0.05, step
    for b in range(B):
        at = 24 * b + lag + AT["wo"]
        yield at, ("wo", b)
        yield at, ("st", 1, b)
        at = AT["FFN_LAST"] if b == B - 1 else AT["FFN"] + b * AT["FFN_STEP"]
        for name, step in (("ln1", ("ln", 1, b)), ("xf", ("xf", b)), ("mix", ("mix", b)), ("mixl", ("mixl", b)),
                           ("r", ("r", b)), ("fk", ("fk", b)), ("fkl", ("fkl", b)), ("kv", ("kv", b)),
                           ("kv", ("st", 2, b))):
            yield at + AT[name], step
        at = AT["LAYER1"] + b * AT["LAYER1_STEP"]
        for name, step in (("ln2", ("ln", 2, b)), ("xt2", ("xt", 2, b)), ("q1", ("q1", b)), ("q1", ("k1", b)),
                           ("v1", ("v1", b)), ("v1", ("sq", b)), ("ke", ("ke", b)), ("ke", ("qe", b)),
                           ("kT", ("kT", b)), ("z", ("z", b)), ("kvm", ("kvm", b)), ("zn", ("zn", b)),
                           ("o", ("o", b)), ("o", ("o1split", b)), ("o1l", ("o1l", b)), ("wo1", ("wo1", b)),
                           ("wo1", ("st", 3, b)), ("ln3", ("ln", 3, b)), ("xt3", ("xt", 3, b)), ("xt3", ("xx", b)),
                           ("gl", ("gl", b)), ("gate", ("gate", b)), ("cwT", ("cwT", b))):
            yield at + AT[name], step
    for p in range(2, 6):
        yield AT[f"W{p}"], ("split", p)
    for e in range(4):
        yield AT[f"E{e}"], ("split", 6 + e)


def walk():
    for _, step in sorted(timetable(), key=lambda entry: entry[0]):
        yield step
    for b in range(B):
        for e in range(NE + 1):
            yield ("expert", b, e)
            if b == 0 and e + 4 <= NE:
                yield ("split", 10 + e)


V_STEPS = {"tok", "xt", "lat", "p1", "mT", "pv", "wo", "fk", "kv", "v1", "kvm", "z", "o", "wo1", "gate", "cwT"}
A_STEPS = {"q", "k", "v", "p2", "xf", "r", "q1", "k1", "qe", "ke", "kT", "xx", "gl"}
LAST = {s for s in walk() if s[0] != "pv" or s[3] == NC - 1}
V_NO = {s: n for n, s in enumerate(s for s in walk() if s[0] in V_STEPS and s in LAST)}
A_NO = {s: n for n, s in enumerate(s for s in walk() if s[0] in A_STEPS)}
SMALL = {"lat", "mT", "pv", "gate", "cwT"}
RINGS = ([s for s in walk() if s[0] in V_STEPS | A_STEPS and s[0] not in SMALL],
         [s[0:3] for s in walk() if s[0] in SMALL and (s[0] != "pv" or s[3] == 0)])
RING_NO = {s: (ring, n) for ring in range(2) for n, s in enumerate(RINGS[ring])}


FREE_NO = {("pv",) + s[1:] if s[0] == "pvn" else s: n for n, s in enumerate(
    s for s in walk() if s[0] == "pvn" or s[0] in V_STEPS - {"pv"})}
ST_NO = {s: n for n, s in enumerate(s for s in walk() if s[0] in ("tok", "st"))}
XT_NO = {s: n for n, s in enumerate(s for s in walk() if s[0] == "xt")}
LN_NO = {s: n for n, s in enumerate(s for s in walk() if s[0] == "ln")}


def ln_before(step):
    same = [s for s in LN_NO if s[2] % 2 == step[2] % 2]
    n = same.index(step)
    return same[n - 1] if n else None


def transposed(ln):
    return ("xf", ln[2]) if ln[1] == 1 else ("xt",) + ln[1:]


def tower(nc, xp, w_tok, rows, cls_rows, consts, weights, experts, out):
    ctx = ExitStack()

    def sb(where, name, shape, dt=F32):
        return where.enter_context(nc.sbuf_tensor(name, shape, dt))

    stage = sb(ctx, "stage", [128, 2, EXPERT])
    cst = sb(ctx, "cst", [128, C_TOTAL])
    row = sb(ctx, "row", [TC, R_TOTAL])
    cls = sb(ctx, "cls", [TC, D])
    neg = sb(ctx, "neg", [128, 128])
    rbd = sb(ctx, "rbd", [128, 128])
    eps = sb(ctx, "eps", [128, 1])
    st = sb(ctx, "st", [TC, NC, 6])
    mv = sb(ctx, "mv", [TC, len(ST_NO), NC, 2])
    lnv = sb(ctx, "lnv", [TC, len(ST_NO), NC])
    rst0 = sb(ctx, "rst0", [TC, len(ST_NO), NC])
    nwt = sb(ctx, "nwt", [TC, len(ST_NO), NC])
    rstd = sb(ctx, "rstd", [TC, len(ST_NO), NC])
    mrs = sb(ctx, "mrs", [TC, len(ST_NO), NC])
    tiny = sb(ctx, "tiny", [128, 1])
    g0 = ExitStack()
    X = sb(g0, "X", [TC, B, NC, D])
    xn = sb(g0, "xn", [TC, 2, NC, D])
    XTh = sb(g0, "XTh", [128, 2, 2, TP], F32R)
    XTl = sb(g0, "XTl", [128, 2, 2, TP], F32R)
    size0 = B * NC * D + 2 * NC * D + 8 * TP
    g0.close()
    g0 = ExitStack()
    es = sb(g0, "es", [128, 2, 2, TP])
    eg = sb(g0, "eg", [128, 2, TP])
    ehf = sb(g0, "ehf", [128, 2, TP])
    ehh = sb(g0, "ehh", [128, 2, 2, TP], F32R)
    ehl = sb(g0, "ehl", [128, 2, 2, TP], F32R)
    outb = sb(g0, "outb", [128, 2, 2, TP])
    g0.close()
    assert size0 >= 20 * TP
    sb(ctx, "room0", [128, size0])

    g1 = ExitStack()
    n_w0 = W_COLS["o0"][0]
    W0h = sb(g1, "W0h", [128, n_w0], F32R)
    W0l = sb(g1, "W0l", [128, n_w0], F32R)
    lath = sb(g1, "lath", [128, 2, TP], F32R)
    latl = sb(g1, "latl", [128, 2, TP], F32R)
    qf = sb(g1, "qf", [128, 2, 2, TP])
    wcos = sb(g1, "wcos", [128, 3, D])
    wsin = sb(g1, "wsin", [128, 3, D])
    mid0 = W_COLS["r"][0]
    n_mid = W_COLS["eb"][0] - mid0
    size1 = 2 * n_w0 + 8 * TP + 6 * D
    if size1 < 2 * n_mid:
        sb(g1, "room_mid", [128, 2 * n_mid - size1])
        size1 = 2 * n_mid
    g1.close()
    gm_ = ExitStack()
    at_q1 = W_COLS["q1"][0]
    n_f, n_1 = at_q1 - mid0, W_COLS["eb"][0] - at_q1
    Wfh = sb(gm_, "Wfh", [128, n_f], F32R)
    Wfl = sb(gm_, "Wfl", [128, n_f], F32R)
    Wqh = sb(gm_, "Wqh", [128, n_1], F32R)
    Wql = sb(gm_, "Wql", [128, n_1], F32R)
    if size1 > 2 * n_mid:
        sb(gm_, "room1", [128, size1 - 2 * n_mid])
    g2 = ExitStack()
    qh = sb(g2, "qh", [128, 2, 2, TP], F32R)
    ql = sb(g2, "ql", [128, 2, 2, TP], F32R)
    Qst2 = sb(g2, "Qst2", [128, 8, TP], F32R)
    Kst2 = sb(g2, "Kst2", [128, 8, TP], F32R)
    sb(g2, "pad", [128, 64])
    Vt0 = sb(g2, "Vt0", [TC, NC, NH, 32])
    g2.close()
    g3 = ExitStack()
    xf = sb(g3, "xf", [128, 2, TP + 1])
    dx = sb(g3, "dx", [128, 2, TP])
    xm = sb(g3, "xm", [128, 2, 2, TP])
    xmh = sb(g3, "xmh", [128, 2, 2, TP], F32R)
    xml = sb(g3, "xml", [128, 2, 2, TP], F32R)
    kr = sb(g3, "kr", [128, 2, TP])
    ka = sb(g3, "ka", [128, 2, TP])
    kah = sb(g3, "kah", [128, 2, TP], F32R)
    kal = sb(g3, "kal", [128, 2, TP], F32R)
    er = sb(g3, "er", [TC, NC, D])
    sig = sb(g3, "sig", [TC, NC, D])
    sizeA = 24 * TP + 96 + 2 * NC * D
    g3.close()
    roomA = ExitStack()
    sb(roomA, "roomA", [128, sizeA])
    g2 = ExitStack()
    Woh = sb(g2, "Woh", [128, 4 * D], F32R)
    Wol = sb(g2, "Wol", [128, 4 * D], F32R)
    Qst = [sb(g2, f"Qst{n}", [128, 8, TP], F32R) for n in range(2)] + [Qst2]
    Kst = [sb(g2, f"Kst{n}", [128, 8, TP], F32R) for n in range(2)] + [Kst2]
    Vt = [Vt0, sb(g2, "Vt1", [TC, NC, NH, 32])]
    mx = sb(g2, "mx", [TC, 2, NC, 8])
    nm = sb(g2, "nm", [8, 2, 2, TP], F32R)
    den = sb(g2, "den", [128, TP])
    dln = sb(g2, "dln", [128, TP])
    rec = sb(g2, "rec", [128, TP])
    dre = sb(g2, "dre", [128, TP])
    of = sb(g2, "of", [128, 2, TP])
    oh = sb(g2, "oh", [128, 4, TP], F32R)
    ol = sb(g2, "ol", [128, 4, TP], F32R)
    gp_ = ExitStack()
    P = sb(gp_, "P", [TC, 2, 12, TP])
    gp_.close()
    xps = sb(gp_, "xps", [KP, NC, B, TP])
    wts = sb(gp_, "wts", [KP, NC, D])
    gp_.close()
    g2.close()
    g3 = ExitStack()
    q1f = sb(g3, "q1f", [128, 2, 2, 2, TP])
    q1s = sb(g3, "q1s", [128, 2, 2, TP])
    q1e = sb(g3, "q1e", [128, 2, 2, 2, TP])
    v1t = sb(g3, "v1t", [TC, NC, D])
    k1t = sb(g3, "k1t", [TC, NC, D])
    kvb = sb(g3, "kvb", [128, 2, 128])
    zz = sb(g3, "zz", [128, 2, TP])
    zl = sb(g3, "zl", [128, 2, TP])
    zr = sb(g3, "zr", [128, 2, TP])
    o1f = sb(g3, "o1f", [128, 2, TP])
    o1h = sb(g3, "o1h", [128, 2, 2, TP], F32R)
    o1l = sb(g3, "o1l", [128, 2, 2, TP], F32R)
    size3 = sizeA + 36 * TP + 2 * NC * D + 256 + 128
    g3.close()
    roomA.close()
    gm_.close()
    def parts(n):
        for _ in range(n):
            part.append(sb(ctx, f"We{len(part)}", [128, EXPERT], F32R))

    part = []
    assert n_f == EXPERT
    parts(2)
    n = (size1 - 2 * n_f + sizeA - 4 * EXPERT) // EXPERT
    parts(n)
    sb(ctx, "room_a", [128, size1 - 2 * n_f + sizeA - (n + 4) * EXPERT])
    parts(4)
    parts(2 * NE - 6 - n)
    sb(ctx, "room_b", [128, size3 - sizeA - (2 * NE - 6 - n) * EXPERT])
    order = [0, 1] + list(range(2 + n, 6 + n)) + list(range(2, 2 + n)) + list(range(6 + n, 2 * NE))
    We = [(sb(ctx, "Wsh", [128, EXPERT], F32R), sb(ctx, "Wsl", [128, EXPERT], F32R))]
    We += [(part[order[2 * e]], part[order[2 * e + 1]]) for e in range(NE)]
    n_eb = W_COLS["sel"][0] - W_COLS["eb"][0]
    Ebh = sb(ctx, "Ebh", [128, W_TOTAL - W_COLS["eb"][0]], F32R)
    Ebl = sb(ctx, "Ebl", [128, n_eb], F32R)
    XMh = sb(ctx, "XMh", [128, B, 2, TP], F32R)
    XMl = sb(ctx, "XMl", [128, B, 2, TP], F32R)
    XF = sb(ctx, "XF", [128, B, 2, TP])
    cwx = sb(ctx, "cwx", [128, B, TP], F32R)
    glf = sb(ctx, "glf", [NE, TP])
    glog = sb(ctx, "glog", [TC, NC, NE])
    gm = sb(ctx, "gm", [TC, NC])
    gs = sb(ctx, "gs", [TC, NC])
    gr = sb(ctx, "gr", [TC, NC])
    rank = sb(ctx, "rank", [TC, NC, NE])
    ge = sb(ctx, "ge", [TC, 2, NC, NE])
    gp = sb(ctx, "gp", [TC, NC, NE])
    gt = sb(ctx, "gt", [TC, NC, NE * NE])
    gq = sb(ctx, "gq", [TC, NC, NE * NE])
    cw = sb(ctx, "cw", [TC, 2, NC, NE])

    psum = [ctx.enter_context(nc.psum_tensor(f"unit{n}", [128, 2, 512], F32)) for n in range(4)]

    def unit_of(step):
        ring, n = RING_NO[step[0:3] if step[0] == "pv" else step]
        return psum[3][:, n % 2:n % 2 + 1, :] if ring else psum[n % 3]

    ACC, UP_A, UP_B, CWB = psum

    scratch = nc.dram_tensor("qk_scratch", [B, 2, 2, D, TP], F32, kind="Internal").ap()

    def sem(name):
        return ctx.enter_context(nc.semaphore(name))

    s_xp = [sem(f"patches_in{b}") for b in range(B)]
    s_cst, s_wt = sem("constants_in"), sem("token_weights_in")
    s_stage = [sem(f"stage_in{n}") for n in range(2)]
    s_set = sem("constants_made")
    s_fill = sem("stack_rows_made")
    v_full, v_free = sem("v_full"), sem("v_free")
    a_full, a_free = sem("a_full"), sem("a_free")
    w_hi, w_lo = sem("weights_high"), sem("weights_low")
    stats, rstd_ok, xn_ok = sem("stats_ready"), sem("rstd_ready"), sem("normalised")
    lnv_ok, rst0_ok, newton = sem("log_var_ready"), sem("rstd_estimate"), sem("newton_step")
    rot_ok, q_hi, q_lo = sem("weights_rotated"), sem("qk_high"), sem("qk_low")
    s_scr = [sem(f"qk_in_scratch{n}") for n in range(2)]
    s_stk = [sem(f"stack_in{n}") for n in range(3)]
    s_mrow = [sem(f"max_rows_in{n}") for n in range(3)]
    o_hi, o_lo = sem("heads_high"), sem("heads_low")
    mix_ok, mix_hi, mix_lo = sem("mixed"), sem("mixed_high"), sem("mixed_low")
    ka_hi, ka_lo = sem("square_high"), sem("square_low")
    bo_ok = sem("out_bias_added")
    o1_hi, o1_lo = sem("heads1_high"), sem("heads1_low")
    xt_hi, den_ok, ln_ok, rec_ok, dre_ok = (sem("transposed_high"), sem("sums_ready"), sem("log_ready"),
                                            sem("reciprocal_estimate"), sem("sum_times_estimate"))
    zl_ok, zr_ok = sem("z_log"), sem("z_estimate")
    ge_ok, cw_ok = sem("gate_exp"), sem("expert_weights")
    dve_step = sem("vector_step")
    ma_full, ma_free = sem("up_a_full"), sem("up_a_free")
    mb_full, mb_free = sem("up_b_full"), sem("up_b_free")
    mc_full, mc_free = sem("token_weights_full"), sem("token_weights_free")
    h_ok, down_done, acc_free = sem("hidden_ready"), sem("down_done"), sem("out_ready")
    s_out = [sem(f"out_written{n}") for n in range(2)]
    block = ctx.enter_context(nc.Block())

    def cc(name):
        a, n = C_COLS[name]
        return cst[:, a:a + n]

    def rr(name):
        a, n = R_COLS[name]
        return row[:, a:a + n]

    def piece(p):
        if p < len(PIECES):
            a, (z, n) = W_COLS[PIECES[p][0]][0], W_COLS[PIECES[p][1]]
            n = z + n - a
            if p == 0:
                return n, W0h[:, a:a + n], W0l[:, a:a + n], n
            if p == 1:
                return n, Woh[:, :], Wol[:, :], n
            if p < 5:
                if p == 2:
                    return n, Wfh[:, a - mid0:a - mid0 + n], Wfl[:, a - mid0:a - mid0 + n], n
                return n, Wqh[:, a - at_q1:a - at_q1 + n], Wql[:, a - at_q1:a - at_q1 + n], n
            return n, Ebh[:, :], Ebl[:, :], n_eb
        h, l = We[p - len(PIECES)]
        return EXPERT, h[:, :], l[:, :], EXPERT

    @block.sync
    def _(sp):
        def load_piece(p):
            if p >= 2:
                sp.wait_ge(w_lo, p - 1)
            n = piece(p)[0]
            if p < len(PIECES):
                a = W_COLS[PIECES[p][0]][0]
                src = weights[:, a:a + n]
            else:
                src = experts[p - len(PIECES)]
            sp.dma_start(stage[:, p % 2, 0:n], src).then_inc(s_stage[p % 2], 16)

        def store_qk(r):
            b, k = r // 2, r % 2
            sp.wait_ge(q_lo, r + 1)
            for part, src in ((0, qh), (1, ql)):
                sp.dma_start(scratch[b, k, part].rearrange("(c p) t -> p c t", p=128),
                             src[:, r % 2].bitcast(F32)).then_inc(s_scr[k], 16)

        def load_stacks(i):
            b, c, s = i // 2, i % 2, i % 3
            for k in range(2):
                sp.wait_ge(s_scr[k], 32 * (b + 1))
            if i >= 3:
                sp.wait_ge(a_full, A_NO["p2", i - 3, 11] + 1)
                sp.dma_start(Qst[s][96:98].bitcast(F32), Qst[s][64:66].bitcast(F32)).then_inc(s_stk[s], 16)
            for k, dst, parts in ((0, Qst, (0, 1, 0, 1)), (1, Kst, (0, 0, 1, 1))):
                for g, part in enumerate(parts):
                    src = scratch[b, k, part, 128 * c:128 * c + 128].rearrange("(h d) t -> d h t", d=HD)
                    sp.dma_start(dst[s][HD * g:HD * g + HD].bitcast(F32), src).then_inc(s_stk[s], 16)

        def move_max(i):
            sp.wait_ge(v_free, FREE_NO["mT", i] + 1)
            for part in range(2):
                sp.dma_start(Qst[i % 3][96 + part:97 + part].bitcast(F32),
                             nm[:, i % 2, part].bitcast(F32)).then_inc(s_mrow[i % 3], 16)

        sp.dma_start(wts[:, :, :], w_tok).then_inc(s_wt, 16)
        sp.dma_start(xps[:, :, 0, :], xp[:, :, 0, :]).then_inc(s_xp[0], 16)
        sp.dma_start(cst[:, :], consts).then_inc(s_cst, 16)
        sp.dma_start(row[:, :], rows.partition_broadcast(TC)).then_inc(s_cst, 16)
        sp.dma_start(cls[:, :], cls_rows).then_inc(s_cst, 16)
        load_piece(0)
        for b in range(1, B):
            sp.dma_start(xps[:, :, b, :], xp[:, :, b, :]).then_inc(s_xp[b], 16)
        load_piece(1)
        n_pieces = len(PIECES) + NE + 1
        loaded = 2
        for step in walk():
            kind = step[0]
            if kind == "qsplit":
                store_qk(step[1])
            elif kind == "stk":
                load_stacks(step[1])
            elif kind == "mT":
                move_max(step[1])
            elif kind == "split" and loaded < n_pieces:
                load_piece(loaded)
                loaded += 1
        for b in range(B):
            sp.wait_ge(acc_free, b + 1)
            sp.dma_start(out[b].rearrange("(c p) t -> p c t", p=128), outb[:, b % 2]).then_inc(s_out[b % 2], 16)
        for n in range(2):
            sp.wait_ge(s_out[n], 16 * (B // 2))

    @block.tensor
    def _(pe):
        def unit(step):
            ring, n = RING_NO[step[0:3] if step[0] == "pv" else step]
            before = n - (2 if ring else 3)
            if before >= 0:
                last = RINGS[ring][before]
                if last[0] in V_STEPS:
                    pe.wait_ge(v_free, FREE_NO[last] + 1)
                else:
                    pe.wait_ge(a_free, A_NO[last] + 1)
            return unit_of(step)

        def exact(dst, lh, ll, rh, rl, first, last):
            pe.matmul(dst, lh, rh, start=first, stop=False)
            pe.matmul(dst, lh, rl, start=False, stop=False)
            return pe.matmul(dst, ll, rh, start=False, stop=last)

        def w(name, c, m=None):
            a, n = W_COLS[name]
            for h, l, start in ((Ebh, Ebl, W_COLS["eb"][0]), (Wqh, Wql, at_q1), (Wfh, Wfl, mid0), (Woh, Wol, n_w0), (W0h, W0l, 0)):
                if a >= start:
                    break
            a -= start
            width = {"lat": 128, "gate": NE}.get(name, D)
            a += c * width
            if m is not None:
                a, width = a + 128 * m, 128
            return h[:, a:a + width], l[:, a:a + width]

        def tok(t):
            return slice(TC * t, TC * t + TC)

        def flat(u):
            return u[:, :, :].rearrange("p b n -> p (b n)")

        def transposes(u, src, step=None):
            for c in range(2):
                for t in range(NC):
                    ins = pe.transpose(u[:, c, tok(t)], src[:, t, 128 * c:128 * c + 128], cc("ident")[0:TC, 0:TC])
            return ins

        def token_major(u, lh, ll, name, halves=2):
            for t in range(NC):
                for c in range(halves):
                    ins = exact(flat(u)[0:TC, D * t:D * t + D], lh[:, c, tok(t)], ll[:, c, tok(t)],
                                *w(name, c), c == 0, c == halves - 1)
            return ins

        def feature_major(u, name, xh, xl, halves=2):
            for m in range(2):
                for c in range(halves):
                    ins = exact(u[:, m, 0:TP], *w(name, c, m), xh[:, c], xl[:, c], c == 0, c == halves - 1)
            return ins

        pe.wait_ge(s_wt, 16)
        for step in walk():
            kind = step[0]
            if kind == "tok":
                b = step[1]
                pe.wait_ge(s_xp[b], 16)
                u = unit(step)
                for t in range(NC):
                    for k in range(NC):
                        ins = pe.matmul(flat(u)[0:TC, D * t:D * t + D], xps[:, k, b, tok(t)], wts[:, k, :],
                                        start=k == 0, stop=k == NC - 1)
                ins.then_inc(v_full, 1)
            elif kind in ("xt", "xf"):
                s, b = step[1:] if kind == "xt" else (1, step[1])
                if LN_NO["ln", s, b] == 0:
                    pe.wait_ge(s_cst, 48)
                pe.wait_ge(xn_ok, LN_NO["ln", s, b] + 1)
                u = unit(step)
                transposes(u, xn[:, b % 2]).then_inc(v_full if kind == "xt" else a_full, 1)
            elif kind == "lat":
                b = step[1]
                u = unit(step)
                for c in range(2):
                    ins = exact(u[:, 0, 0:TP], *w("lat", c, 0), XTh[:, b % 2, c], XTl[:, b % 2, c], c == 0, c == 1)
                ins.then_inc(v_full, 1)
            elif kind == "q":
                b = step[1]
                if b == 0:
                    pe.wait_ge(w_lo, 1)
                pe.wait_ge(v_free, FREE_NO["xt", 0, b] + 1)
                u = unit(step)
                feature_major(u, "q0", XTh[:, b % 2], XTl[:, b % 2]).then_inc(a_full, 1)
            elif kind == "k":
                b = step[1]
                pe.wait_ge(v_free, FREE_NO["lat", b] + 1)
                u = unit(step)
                feature_major(u, "k0", lath[:, b % 2:b % 2 + 1], latl[:, b % 2:b % 2 + 1], 1).then_inc(a_full, 1)
            elif kind == "v":
                b = step[1]
                u = unit(step)
                token_major(u, lath[:, b % 2:b % 2 + 1], latl[:, b % 2:b % 2 + 1], "v0", 1).then_inc(a_full, 1)
            elif kind == "p1":
                _, i, n = step
                if n == 0:
                    pe.wait_ge(s_stk[i % 3], 128 * (i // 3 + 1) + 16 * (i // 3))
                    if i < 3:
                        pe.wait_ge(s_set, 5)
                        pe.wait_ge(s_fill, 2)
                u = unit(step)
                for j in range(2):
                    h = 2 * (n % 4) + j
                    ins = pe.matmul(u[0:TC, j, 0:TP], Qst[i % 3][:, h, tok(n // 4)], Kst[i % 3][:, h, :],
                                    start=True, stop=True)
                ins.then_inc(v_full, 1)
            elif kind == "mT":
                i = step[1]
                pe.wait_ge(v_free, FREE_NO["p1", i, 11] + 1)
                u = unit(step)
                for t in range(NC):
                    ins = pe.transpose(u[0:8, 0, tok(t)], mx[:, i % 2, t, :], cc("ident")[0:TC, 0:TC])
                ins.then_inc(v_full, 1)
            elif kind == "p2":
                _, i, n = step
                if n == 0:
                    pe.wait_ge(s_mrow[i % 3], 32 * (i // 3 + 1))
                u = unit(step)
                for j in range(2):
                    t, h = n % 6 // 2, 4 * (n // 6) + 2 * (n % 2) + j
                    ins = pe.matmul(u[0:TC, j, 0:TP], Kst[i % 3][:, h, tok(t)], Qst[i % 3][:, h, :],
                                    start=True, stop=True)
                ins.then_inc(a_full, 1)
            elif kind == "pv":
                _, i, g, t = step
                b = i // 2
                pe.wait_ge(a_free, A_NO["p2", i, 6 * g + 2 * t + 1] + 1)
                u = unit(step) if t == 0 else unit_of(step)
                kn = TC - (t == NC - 1)
                for j in range(4):
                    ins = pe.matmul(u[32 * j:32 * j + 32, 0, 0:TP], Vt[b % 2][0:kn, t, 8 * (i % 2) + 4 * g + j, :],
                                    P[0:kn, g, 4 * t + j, :], start=t == 0, stop=t == NC - 1,
                                    tile_position=(0, 32 * j))
                if t == NC - 1:
                    ins.then_inc(v_full, 1)
            elif kind == "wo":
                b = step[1]
                pe.wait_ge(o_lo, 4 * b + 4)
                u = unit(step)
                token_major(u, oh, ol, "o0", 4).then_inc(v_full, 1)
            elif kind in ("r", "fk"):
                b = step[1]
                if kind == "r":
                    if b == 0:
                        pe.wait_ge(w_lo, 3)
                    pe.wait_ge(mix_lo, b + 1)
                u = unit(step)
                if kind == "r":
                    ins = token_major(u, xmh[:, 0], xml[:, 0], "r")
                else:
                    ins = feature_major(u, "fk", xmh[:, 1], xml[:, 1])
                ins.then_inc(a_full if kind == "r" else v_full, 1)
            elif kind == "kv":
                b = step[1]
                pe.wait_ge(ka_lo, b + 1)
                u = unit(step)
                token_major(u, kah, kal, "fv").then_inc(v_full, 1)
            elif kind in ("q1", "k1", "v1"):
                b = step[1]
                if kind == "q1":
                    if b == 0:
                        pe.wait_ge(w_lo, 5)
                    pe.wait_ge(v_free, FREE_NO["xt", 2, b] + 1)
                u = unit(step)
                if kind == "v1":
                    token_major(u, XTh[:, b % 2], XTl[:, b % 2], kind).then_inc(v_full, 1)
                else:
                    feature_major(u, kind, XTh[:, b % 2], XTl[:, b % 2]).then_inc(a_full, 1)
            elif kind in ("qe", "ke"):
                b, n = step[1], int(kind == "ke")
                if b == 0:
                    pe.wait_ge(s_set, 6)
                if kind == "ke":
                    pe.wait_ge(a_free, A_NO["k1", b] + 1)
                u = unit(step)
                for c in range(2):
                    pe.matmul(u[:, c, 0:TP], rbd[:, :], q1f[:, b % 2, n, c], start=True, stop=False)
                    ins = pe.matmul(u[:, c, 0:TP], neg[:, :], q1s[:, n, c], start=False, stop=True)
                ins.then_inc(a_full, 1)
            elif kind == "kT":
                b = step[1]
                pe.wait_ge(a_free, A_NO["ke", b] + 1)
                u = unit(step)
                for t in range(NC):
                    for c in range(2):
                        ins = pe.transpose(flat(u)[0:TC, D * t + 128 * c:D * t + 128 * c + 128],
                                           q1e[:, b % 2, 1, c, tok(t)], cc("ident"))
                ins.then_inc(a_full, 1)
            elif kind == "kvm":
                b = step[1]
                pe.wait_ge(a_free, A_NO["kT", b] + 1)
                u = unit(step)
                for c in range(2):
                    for t in range(NC):
                        kn = TC - (t == NC - 1)
                        ins = pe.matmul(u[:, c, 0:128], k1t[0:kn, t, 128 * c:128 * c + 128],
                                        v1t[0:kn, t, 128 * c:128 * c + 128], start=t == 0, stop=t == NC - 1)
                ins.then_inc(v_full, 1)
            elif kind == "z":
                b = step[1]
                pe.wait_ge(a_free, A_NO["qe", b] + 1)
                u = unit(step)
                for c in range(2):
                    ins = pe.matmul(u[:, c, 0:TP], cc("mask"), q1e[:, b % 2, 0, c], start=True, stop=True)
                ins.then_inc(v_full, 1)
            elif kind == "o":
                b = step[1]
                pe.wait_ge(v_free, FREE_NO["kvm", b] + 1)
                u = unit(step)
                for c in range(2):
                    ins = pe.matmul(u[:, c, 0:TP], kvb[:, c], q1e[:, b % 2, 0, c], start=True, stop=True)
                ins.then_inc(v_full, 1)
            elif kind == "wo1":
                b = step[1]
                pe.wait_ge(o1_lo, b + 1)
                u = unit(step)
                token_major(u, o1h[:, b % 2], o1l[:, b % 2], "o1").then_inc(v_full, 1)
            elif kind == "xx":
                b = step[1]
                pe.wait_ge(v_free, FREE_NO["wo1", b] + 1)
                u = unit(step)
                transposes(u, X[:, b]).then_inc(a_full, 1)
            elif kind == "gl":
                b = step[1]
                if b == 0:
                    pe.wait_ge(w_lo, 6)
                pe.wait_ge(v_free, FREE_NO["xt", 3, b] + 1)
                u = unit(step)
                for c in range(2):
                    ins = exact(u[0:NE, 0, 0:TP], *w("gate", c), XMh[:, b, c], XMl[:, b, c], c == 0, c == 1)
                ins.then_inc(a_full, 1)
            elif kind == "gate":
                b = step[1]
                pe.wait_ge(a_free, A_NO["gl", b] + 1)
                u = unit(step)
                for t in range(NC):
                    ins = pe.transpose(u[0:TC, 0, NE * t:NE * t + NE], glf[:, tok(t)], cc("ident")[0:NE, 0:NE])
                ins.then_inc(v_full, 1)
            elif kind == "cwT":
                b = step[1]
                pe.wait_ge(cw_ok, b + 1)
                u = unit(step)
                for t in range(NC):
                    ins = pe.transpose(u[0:NE, 0, tok(t)], cw[:, b % 2, t, :], cc("ident")[0:TC, 0:TC])
                ins.then_inc(v_full, 1)
            elif kind == "expert":
                _, b, e = step
                n = (NE + 1) * b + e

                def down(b, e):
                    n = (NE + 1) * b + e
                    wh, wl = We[e]
                    if e == 0:
                        if b:
                            pe.wait_ge(acc_free, b)
                        for m in range(2):
                            bias_h, bias_l = w("eb", 0, m)
                            pe.matmul(ACC[:, m, 0:TP], bias_h, cwx[:, b, :], start=True, stop=False)
                            pe.matmul(ACC[:, m, 0:TP], bias_l, cwx[:, b, :], start=False, stop=False)
                    pe.wait_ge(h_ok, n + 1)
                    for m in range(2):
                        for c in range(2):
                            a = 4 * D + D * c + 128 * m
                            ins = exact(ACC[:, m, 0:TP], wh[:, a:a + 128], wl[:, a:a + 128],
                                        ehh[:, n % 2, c], ehl[:, n % 2, c], False, e == NE and c == 1)
                    ins.then_inc(down_done, 1)

                wh, wl = We[e]
                if n == 0:
                    pe.wait_ge(v_free, len(V_NO))
                    pe.wait_ge(a_free, len(A_NO))
                if b == 0:
                    pe.wait_ge(w_lo, len(PIECES) + e + 1)
                for up, full, free, at in ((UP_A, ma_full, ma_free, 0), (UP_B, mb_full, mb_free, D)):
                    if n:
                        pe.wait_ge(free, n)
                    for m in range(2):
                        for c in range(2):
                            a = 2 * D * c + at + 128 * m
                            ins = exact(up[:, m, 0:TP], wh[:, a:a + 128], wl[:, a:a + 128],
                                        XMh[:, b, c], XMl[:, b, c], c == 0, c == 1)
                    ins.then_inc(full, 1)
                if e:
                    nc_ = NE * b + e - 1
                    if nc_:
                        pe.wait_ge(mc_free, nc_)
                    a = W_COLS["sel"][0] - W_COLS["eb"][0] + 128 * (e - 1)
                    pe.matmul(CWB[:, 0, 0:TP], Ebh[:, a:a + 128], cwx[:, b, :], start=True, stop=True).then_inc(mc_full, 1)
                if n:
                    down((n - 1) // (NE + 1), (n - 1) % (NE + 1))
                if n == B * (NE + 1) - 1:
                    down(b, e)

    @block.scalar
    def _(act):
        def full(step):
            act.wait_ge(a_full, A_NO[step] + 1)
            return unit_of(step)

        def flat(u):
            return u[:, :, :].rearrange("p b n -> p (b n)")

        act.preload_act_table_set("natural_log_exp_and_others")
        act.wait_ge(s_set, 1)
        for step in walk():
            kind = step[0]
            if kind == "split":
                p = step[1]
                n, hi, _, _ = piece(p)
                act.wait_ge(s_stage[p % 2], 16 * (p // 2 + 1))
                if p == 0:
                    act.wait_ge(rot_ok, 1)
                if p == 2:
                    act.wait_ge(a_full, A_NO["v", B - 1] + 1)
                    act.wait_ge(q_lo, 2 * B)
                if p == 5:
                    act.wait_ge(v_free, FREE_NO["wo", B - 1] + 1)
                if p == len(PIECES) + 1:
                    act.wait_ge(stats, ST_NO["st", 2, B - 1] + 1)
                if p == len(PIECES) + 4:
                    act.wait_ge(v_free, FREE_NO["wo1", B - 1] + 1)
                act.activation(hi, stage[:, p % 2, 0:n], ACT.Copy).then_inc(w_hi, 1)
            elif kind in ("tok", "st"):
                n = ST_NO[step]
                act.wait_ge(stats, n + 1)
                act.activation(lnv[:, n, :], mv[:, n, :, 1], ACT.Ln, bias=eps[0:TC, :]).then_inc(lnv_ok, 1)
                act.wait_ge(lnv_ok, n + 1)
                act.activation(rst0[:, n, :], lnv[:, n, :], ACT.Exp, scale=-0.5).then_inc(rst0_ok, 1)
            elif kind == "ln":
                _, s, b = step
                n = ST_NO["st", s, b]
                if ln_before(step):
                    last = transposed(ln_before(step))
                    if last[0] == "xt":
                        act.wait_ge(v_full, V_NO[last] + 1)
                    else:
                        act.wait_ge(a_full, A_NO[last] + 1)
                act.wait_ge(rstd_ok, n + 1)
                for t in range(NC):
                    ins = act.activation(xn[:, b % 2, t, :], X[:, b, t, :], ACT.Identity,
                                         bias=mrs[:, n, t:t + 1], scale=rstd[:, n, t:t + 1])
                ins.then_inc(xn_ok, 1)
            elif kind == "xt":
                _, s, b = step
                act.wait_ge(v_full, V_NO[step] + 1)
                if s == 0 and b >= 2:
                    act.wait_ge(a_full, A_NO["q", b - 2] + 1)
                    act.wait_ge(v_full, V_NO["lat", b - 2] + 1)
                if s == 2 and b >= 2:
                    act.wait_ge(v_full, V_NO["v1", b - 2] + 1)
                    act.wait_ge(a_full, A_NO["k1", b - 2] + 1)
                hi = XMh[:, b] if s == 3 else XTh[:, b % 2]
                act.activation(hi, unit_of(step)[:, :, 0:TP], ACT.Copy).then_inc(xt_hi, 1)
            elif kind == "xf":
                b = step[1]
                u = full(step)
                if b:
                    act.wait_ge(mix_ok, b)
                else:
                    act.wait_ge(a_full, A_NO["p2", 5, 11] + 1)
                    act.wait_ge(s_scr[0], 32 * B)
                    act.wait_ge(s_scr[1], 32 * B)
                act.activation(xf[:, :, 1:TP + 1], u[:, :, 0:TP], ACT.Copy).then_inc(a_free, 1)
            elif kind == "pv" and step in LAST:
                _, i, g, _ = step
                q = 2 * i + g
                act.wait_ge(den_ok, q + 1)
                if q:
                    act.wait_ge(v_free, FREE_NO["pv", (q - 1) // 2, (q - 1) % 2] + 1)
                act.activation(dln[:, :], den[:, :], ACT.Ln, bias=tiny[:, :]).then_inc(ln_ok, 1)
                act.wait_ge(ln_ok, q + 1)
                act.activation(rec[:, :], dln[:, :], ACT.Exp, scale=-1.0).then_inc(rec_ok, 1)
            elif kind == "z":
                b = step[1]
                act.wait_ge(v_free, FREE_NO[step] + 1)
                act.activation(zl[:, :, :], zz[:, :, :], ACT.Ln, bias=tiny[:, :]).then_inc(zl_ok, 1)
                act.wait_ge(zl_ok, b + 1)
                if b:
                    act.wait_ge(v_free, FREE_NO["o", b - 1] + 1)
                act.activation(zr[:, :, :], zl[:, :, :], ACT.Exp, scale=-1.0).then_inc(zr_ok, 1)
            elif kind == "kT":
                b = step[1]
                u = full(step)
                if b:
                    act.wait_ge(v_full, V_NO["kvm", b - 1] + 1)
                act.activation(k1t[:, :, :].rearrange("p t d -> p (t d)"), flat(u)[0:TC, 0:NC * D], ACT.Copy).then_inc(a_free, 1)
            elif kind == "gl":
                b = step[1]
                u = full(step)
                if b:
                    act.wait_ge(v_full, V_NO["gate", b - 1] + 1)
                act.activation(glf[:, :], u[0:NE, 0, 0:TP], ACT.Copy).then_inc(a_free, 1)
            elif kind in ("q", "k"):
                b, r = step[1], 2 * step[1] + (kind == "k")
                u = full(step)
                if r >= 2:
                    act.wait_ge(q_lo, r - 1)
                act.activation(qf[:, r % 2], u[:, :, 0:TP], ACT.Copy).then_inc(a_free, 1)
            elif kind == "v":
                b = step[1]
                u = full(step)
                if b == 0:
                    act.wait_ge(s_set, 3)
                if b >= 2:
                    act.wait_ge(v_full, V_NO["pv", 2 * b - 3, 1, NC - 1] + 1)
                for t in range(NC):
                    ins = act.activation(Vt[b % 2][:, t, :, 0:HD],
                                         flat(u)[0:TC, D * t:D * t + D].rearrange("p (h d) -> p h d", d=HD), ACT.Copy)
                ins.then_inc(a_free, 1)
            elif kind == "qsplit":
                r = step[1]
                act.wait_ge(a_free, A_NO["qk"[r % 2], r // 2] + 1)
                if r >= 2:
                    act.wait_ge(s_scr[r % 2], 32 * (r // 2))
                act.activation(qh[:, r % 2], qf[:, r % 2], ACT.Copy).then_inc(q_hi, 1)
            elif kind == "p2":
                _, i, n = step
                g = n // 6
                u = full(step)
                if i == 0 and n == 0:
                    act.wait_ge(v_full, V_NO["tok", B - 1] + 1)
                if i and n % 6 == 0:
                    act.wait_ge(v_full, V_NO["pv", i - 1, g, NC - 1] + 1)
                k = 2 * n - 12 * g
                act.activation(P[:, g, k:k + 2, :], u[0:TC, :, 0:TP], ACT.Exp, scale=HD ** -0.5).then_inc(a_free, 1)
            elif kind == "osplit":
                _, i, g = step
                q = 2 * i + g
                act.wait_ge(v_free, FREE_NO["pv", i, g] + 1)
                if q % 4 == 0 and q:
                    act.wait_ge(v_full, V_NO["wo", i // 2 - 1] + 1)
                act.activation(oh[:, q % 4, :], of[:, q % 2, :], ACT.Copy).then_inc(o_hi, 1)
            elif kind == "mix":
                b = step[1]
                act.wait_ge(mix_ok, b + 1)
                if b:
                    act.wait_ge(v_full, V_NO["fk", b - 1] + 1)
                act.activation(xmh[:, :, :, :].rearrange("p a c t -> p (a c t)"),
                               xm[:, :, :, :].rearrange("p a c t -> p (a c t)"), ACT.Copy).then_inc(mix_hi, 1)
            elif kind == "r":
                b = step[1]
                u = full(step)
                if b:
                    act.wait_ge(v_free, FREE_NO["kv", b - 1] + 1)
                else:
                    act.wait_ge(v_full, V_NO["pv", 5, 1, NC - 1] + 1)
                act.activation(er[:, :, :].rearrange("p t d -> p (t d)"), flat(u)[0:TC, 0:NC * D],
                               ACT.Sigmoid).then_inc(a_free, 1)
                act.preload_act_table_set("natural_log_exp_and_others")
            elif kind == "fk":
                b = step[1]
                act.wait_ge(v_free, FREE_NO[step] + 1)
                if b:
                    act.wait_ge(v_full, V_NO["kv", b - 1] + 1)
                act.activation(kah[:, :, :], ka[:, :, :], ACT.Copy).then_inc(ka_hi, 1)
            elif kind in ("q1", "k1"):
                b, n = step[1], int(kind == "k1")
                u = full(step)
                if b:
                    act.wait_ge(a_full, A_NO["qe", b - 1] + 1)
                for c in range(2):
                    bias = cc("bk" if n else "bq")[:, c:c + 1]
                    act.activation(q1f[:, b % 2, n, c], u[:, c, 0:TP], ACT.Identity, bias=bias)
                    ins = act.activation(q1s[:, n, c], u[:, c, 0:TP], ACT.Square, bias=bias)
                ins.then_inc(a_free, 1)
            elif kind in ("qe", "ke"):
                b, n = step[1], int(kind == "ke")
                u = full(step)
                if b >= 2:
                    act.wait_ge(v_full, V_NO["o" if n == 0 else "kvm", b - 2] + 1)
                act.activation(q1e[:, b % 2, n], u[:, :, 0:TP], ACT.Exp).then_inc(a_free, 1)
            elif kind == "o1split":
                b = step[1]
                act.wait_ge(v_free, FREE_NO["o", b] + 1)
                if b >= 2:
                    act.wait_ge(v_full, V_NO["wo1", b - 2] + 1)
                act.activation(o1h[:, b % 2], o1f[:, :, :], ACT.Copy).then_inc(o1_hi, 1)
            elif kind == "xx":
                b = step[1]
                u = full(step)
                act.activation(XF[:, b], u[:, :, 0:TP], ACT.Copy).then_inc(a_free, 1)
            elif kind == "gate":
                b = step[1]
                act.wait_ge(v_free, FREE_NO[step] + 1)
                act.activation(ge[:, b % 2], glog[:, :, :], ACT.Exp).then_inc(ge_ok, 1)
            elif kind == "expert":
                _, b, e = step
                n = (NE + 1) * b + e
                if n == 0:
                    act.wait_ge(v_full, len(V_NO))
                    act.wait_ge(a_full, len(A_NO))
                act.wait_ge(ma_full, n + 1)
                if n >= 2:
                    act.wait_ge(mb_free, n - 1)
                for m in range(2):
                    a = C_COLS["b1"][0] + 4 * e + m
                    ins = act.activation(es[:, n % 2, m], UP_A[:, m, 0:TP], ACT.Silu, bias=cst[:, a:a + 1])
                ins.then_inc(ma_free, 1)

    @block.gpsimd
    def _(pool):
        pool.memset(tiny[:, :], 0.0)
        pool.memset(eps[:, :], EPS).then_inc(s_set, 1)
        for n in range(2):
            ins = pool.memset(Vt[n][:, :, :, HD:32], 0.0)
        ins.then_inc(s_set, 1)
        pool.wait_ge(s_set, 2)
        for n in range(2):
            ins = pool.memset(Vt[n][:, :, :, HD:HD + 1], 1.0)
        ins.then_inc(s_set, 1)
        pool.wait_ge(s_set, 3)
        for n in (1, 2):
            pool.memset(Qst[n][64:128].bitcast(F32), 0.0)
            ins = pool.memset(Kst[n][64:128].bitcast(F32), 0.0)
        ins.then_inc(s_set, 1)
        pool.wait_ge(s_set, 4)
        for n in (1, 2):
            ins = pool.memset(Kst[n][96:98].bitcast(F32), 1.0)
        ins.then_inc(s_set, 1)
        pool.wait_ge(s_set, 5)
        for step in walk():
            kind = step[0]
            if step == ("split", 0):
                pool.wait_ge(s_cst, 48)
            if kind in ("tok", "st"):
                n = ST_NO[step]
                pool.wait_ge(rst0_ok, n + 1)
                r0, t = rst0[:, n, :], nwt[:, n, :]
                pool.tensor_tensor(t, r0, r0, ALU.mult).then_inc(newton, 1)
                pool.wait_ge(newton, 5 * n + 1)
                pool.tensor_scalar(lnv[:, n, :], mv[:, n, :, 1], EPS, -0.5, ALU.add, ALU.mult).then_inc(newton, 1)
                pool.wait_ge(newton, 5 * n + 2)
                pool.tensor_tensor(t, t, lnv[:, n, :], ALU.mult).then_inc(newton, 1)
                pool.wait_ge(newton, 5 * n + 3)
                pool.tensor_scalar(t, t, 1.5, None, ALU.add).then_inc(newton, 1)
                pool.wait_ge(newton, 5 * n + 4)
                pool.tensor_tensor(rstd[:, n, :], t, r0, ALU.mult)
                pool.tensor_scalar(mrs[:, n, :], mv[:, n, :, 0], -1.0, None, ALU.mult).then_inc(newton, 1)
                pool.wait_ge(newton, 5 * n + 5)
                pool.tensor_tensor(mrs[:, n, :], mrs[:, n, :], rstd[:, n, :], ALU.mult).then_inc(rstd_ok, 1)
            elif kind == "split":
                p = step[1]
                _, hi, lo, n = piece(p)
                pool.wait_ge(w_hi, p + 1)
                pool.tensor_tensor(lo, stage[:, p % 2, 0:n], hi[:, 0:n].bitcast(F32), ALU.subtract).then_inc(w_lo, 1)
                if p == 1:
                    pool.tensor_scalar(neg[:, :], cc("mask"), -0.5 / HD, None, ALU.mult)
                    pool.tensor_scalar(rbd[:, :], cc("rbd"), HD ** -0.5, None, ALU.mult).then_inc(s_set, 1)
                if p == 5:
                    pool.wait_ge(s_set, 6)
                    pool.memset(cwx[:, :, :].bitcast(F32), 0.0).then_inc(s_set, 1)
                    pool.wait_ge(s_set, 7)
                    pool.memset(cwx[32:33, :, :].bitcast(F32), 1.0).then_inc(s_set, 1)
                    pool.wait_ge(s_set, 8)
            elif kind == "pv" and step in LAST:
                _, i, g, _ = step
                pool.wait_ge(rec_ok, 2 * i + g + 1)
                pool.tensor_tensor(dre[:, :], den[:, :], rec[:, :], ALU.mult).then_inc(dre_ok, 1)
            elif kind == "qsplit":
                r = step[1]
                pool.wait_ge(q_hi, r + 1)
                pool.tensor_tensor(ql[:, r % 2], qf[:, r % 2], qh[:, r % 2].bitcast(F32),
                                   ALU.subtract).then_inc(q_lo, 1)
            elif kind == "osplit":
                _, i, g = step
                q = 2 * i + g
                pool.wait_ge(o_hi, q + 1)
                pool.tensor_tensor(ol[:, q % 4, :], of[:, q % 2, :], oh[:, q % 4, :].bitcast(F32),
                                   ALU.subtract).then_inc(o_lo, 1)
            elif kind == "sq":
                b = step[1]
                pool.wait_ge(xn_ok, LN_NO["ln", 2, b] + 1)
                pool.tensor_tensor(X[:, b], X[:, b], rr("bo").unsqueeze(1).broadcast_to([TC, NC, D]),
                                   ALU.add).then_inc(bo_ok, 1)

    @block.vector
    def _(dve):
        steps = [0]

        def link(ins):
            steps[0] += 1
            ins.then_inc(dve_step, 1)
            dve.wait_ge(dve_step, steps[0])

        def full(step):
            dve.wait_ge(v_full, V_NO[step] + 1)
            return unit_of(step)

        def flat(u):
            return u[:, :, :].rearrange("p b n -> p (b n)")

        def statistics(src, n):
            for t in range(NC):
                ins = dve.bn_stats(st[:, t, :], src[:, t])
            link(ins)
            for t in range(NC):
                ins = dve.bn_aggr(mv[:, n, t, :], st[:, t, :])
            ins.then_inc(stats, 1)
            dve.wait_ge(stats, n + 1)

        def split(hi, lo, src, semaphore):
            link(dve.tensor_copy(hi, src))
            dve.tensor_tensor(lo, src, hi.bitcast(F32), ALU.subtract).then_inc(semaphore, 1)

        def finish(b):
            dve.wait_ge(down_done, (NE + 1) * (b + 1))
            if b >= 2:
                dve.wait_ge(s_out[b % 2], 16 * (b // 2))
            dve.tensor_tensor(outb[:, b % 2], ACC[:, :, 0:TP], XF[:, b], ALU.add).then_inc(acc_free, 1)

        dve.memset(Qst[0][64:128].bitcast(F32), 0.0)
        dve.memset(Kst[0][64:128].bitcast(F32), 0.0).then_inc(s_fill, 1)
        dve.wait_ge(s_fill, 1)
        dve.memset(Kst[0][96:98].bitcast(F32), 1.0).then_inc(s_fill, 1)
        dve.wait_ge(s_cst, 48)
        dve.wait_ge(s_stage[0], 16)
        a = W_COLS["q0"][0]
        wqk = stage[:, 0, a:a + 3 * D].rearrange("p (n d) -> p n d", d=D)
        cos3, sin3 = (cc(name).unsqueeze(1).broadcast_to([128, 3, D]) for name in ("cos", "sin"))
        dve.tensor_tensor(wcos[:, :, :], wqk, cos3, ALU.mult)
        for even in range(2):
            ins = dve.tensor_tensor(wsin[:, :, even::2], wqk[:, :, 1 - even::2], sin3[:, :, even::2], ALU.mult)
        link(ins)
        dve.tensor_tensor(wqk, wcos[:, :, :], wsin[:, :, :], ALU.add).then_inc(rot_ok, 1)
        for step in walk():
            kind = step[0]
            if kind == "tok":
                b, n = step[1], ST_NO[step]
                u = full(step)
                uu = flat(u)[0:TC, 0:NC * D].rearrange("p (t d) -> p t d", d=D)
                statistics(uu, n)
                for t in range(NC):
                    ins = dve.scalar_tensor_tensor(X[:, b, t, :], uu[:, t, :], mv[:, n, t, 0:1], rr("gamma"),
                                                   ALU.subtract, ALU.mult)
                ins.then_inc(v_free, 1)
                dve.wait_ge(v_free, FREE_NO[step] + 1)
            elif kind == "tokn":
                b, n = step[1], ST_NO["tok", step[1]]
                dve.wait_ge(rstd_ok, n + 1)
                dve.scalar_tensor_tensor(X[:, b, 0, :], X[:, b, 0, :], rstd[:, n, 0:1], cls[:, :], ALU.mult, ALU.add)
                for t in range(1, NC):
                    ins = dve.tensor_scalar(X[:, b, t, :], X[:, b, t, :], rstd[:, n, t:t + 1], None, ALU.mult)
                link(ins)
            elif kind == "st":
                _, s, b = step
                statistics(X[:, b], ST_NO[step])
            elif kind == "xt":
                _, s, b = step
                u = full(step)
                dve.wait_ge(xt_hi, XT_NO[step] + 1)
                hi, lo = (XMh[:, b], XMl[:, b]) if s == 3 else (XTh[:, b % 2], XTl[:, b % 2])
                dve.tensor_tensor(lo, u[:, :, 0:TP], hi.bitcast(F32), ALU.subtract).then_inc(v_free, 1)
            elif kind == "lat":
                b = step[1]
                if b >= 2:
                    dve.wait_ge(a_full, A_NO["v", b - 2] + 1)
                u = full(step)
                split(lath[:, b % 2], latl[:, b % 2], u[:, 0, 0:TP], v_free)
            elif kind == "p1":
                _, i, n = step
                u = full(step)
                if n == 0 and i >= 2:
                    dve.wait_ge(v_full, V_NO["mT", i - 2] + 1)
                a = 2 * (n % 4)
                dve.tensor_reduce(mx[:, i % 2, n // 4, a:a + 2], u[0:TC, :, 0:T], AX, ALU.max).then_inc(v_free, 1)
            elif kind == "mT":
                i = step[1]
                u = full(step)
                if i >= 2:
                    dve.wait_ge(s_mrow[(i - 2) % 3], 32 * ((i - 2) // 3 + 1))
                link(dve.tensor_scalar(nm[:, i % 2, 0, :], u[0:8, 0, 0:TP], -1.0, None, ALU.mult))
                dve.scalar_tensor_tensor(nm[:, i % 2, 1, :], u[0:8, 0, 0:TP], -1.0, nm[:, i % 2, 0, :].bitcast(F32),
                                         ALU.mult, ALU.subtract).then_inc(v_free, 1)
            elif kind == "pv" and step in LAST:
                _, i, g, _ = step
                u = full(step)
                dve.stream_shuffle(den[:, :], u[:, 0, 0:TP], [HD] * 32).then_inc(den_ok, 1)
            elif kind == "pvn":
                _, i, g = step
                q = 2 * i + g
                u = unit_of(("pv", i, g, 0))
                dve.wait_ge(dre_ok, q + 1)
                link(dve.scalar_tensor_tensor(dre[:, :], dre[:, :], 2.0, rec[:, :], ALU.subtract, ALU.mult))
                if q >= 2:
                    dve.wait_ge(o_lo, q - 1)
                dve.scalar_tensor_tensor(of[:, q % 2, :], u[:, 0, 0:TP], -1.0, dre[:, :], ALU.mult,
                                         ALU.mult).then_inc(v_free, 1)
                dve.wait_ge(v_free, FREE_NO["pv", i, g] + 1)
            elif kind in ("wo", "wo1"):
                b = step[1]
                if kind == "wo1":
                    dve.wait_ge(bo_ok, b + 1)
                u = full(step)
                xb = X[:, b].rearrange("p t d -> p (t d)")
                dve.tensor_tensor(xb, xb, flat(u)[0:TC, 0:NC * D], ALU.add).then_inc(v_free, 1)
                dve.wait_ge(v_free, FREE_NO[step] + 1)
            elif kind == "mix":
                b = step[1]
                dve.wait_ge(a_free, A_NO["xf", b] + 1)
                if b == 0:
                    link(dve.memset(xf[:, :, 0:1], 0.0))
                link(dve.tensor_tensor(dx[:, :, :], xf[:, :, 1:TP + 1], xf[:, :, 0:TP], ALU.subtract))
                if b:
                    dve.wait_ge(mix_lo, b)
                for k, name in enumerate(("mu_r", "mu_k")):
                    for c in range(2):
                        ins = dve.scalar_tensor_tensor(xm[:, k, c], dx[:, c], cc(name)[:, c:c + 1], xf[:, c, 0:TP],
                                                       ALU.mult, ALU.add)
                ins.then_inc(mix_ok, 1)
                dve.wait_ge(mix_ok, b + 1)
            elif kind == "mixl":
                b = step[1]
                dve.wait_ge(mix_hi, b + 1)
                dve.tensor_tensor(xml[:, :, :, :].rearrange("p a c t -> p (a c t)"),
                                  xm[:, :, :, :].rearrange("p a c t -> p (a c t)"),
                                  xmh[:, :, :, :].bitcast(F32).rearrange("p a c t -> p (a c t)"),
                                  ALU.subtract).then_inc(mix_lo, 1)
            elif kind == "fk":
                b = step[1]
                u = full(step)
                link(dve.tensor_scalar(kr[:, :, :], u[:, :, 0:TP], 0.0, None, ALU.max))
                if b:
                    dve.wait_ge(ka_lo, b)
                dve.tensor_tensor(ka[:, :, :], kr[:, :, :], kr[:, :, :], ALU.mult).then_inc(v_free, 1)
            elif kind == "fkl":
                b = step[1]
                dve.wait_ge(ka_hi, b + 1)
                dve.tensor_tensor(kal[:, :, :], ka[:, :, :], kah[:, :, :].bitcast(F32), ALU.subtract).then_inc(ka_lo, 1)
            elif kind == "o1l":
                b = step[1]
                dve.wait_ge(o1_hi, b + 1)
                dve.tensor_tensor(o1l[:, b % 2], o1f[:, :, :], o1h[:, b % 2].bitcast(F32), ALU.subtract).then_inc(o1_lo, 1)
            elif kind == "kv":
                b = step[1]
                dve.wait_ge(a_free, A_NO["r", b] + 1)
                u = full(step)
                ee = er[:, :, :].rearrange("p t d -> p (t d)")
                dve.tensor_tensor(sig[:, :, :].rearrange("p t d -> p (t d)"), flat(u)[0:TC, 0:NC * D], ee,
                                  ALU.mult).then_inc(v_free, 1)
                dve.wait_ge(v_free, FREE_NO[step] + 1)
                link(dve.tensor_tensor(X[:, b], X[:, b], sig[:, :, :], ALU.add))
            elif kind == "v1":
                b = step[1]
                u = full(step)
                if b:
                    dve.wait_ge(v_full, V_NO["kvm", b - 1] + 1)
                dve.tensor_tensor(v1t[:, :, :], flat(u)[0:TC, 0:NC * D].rearrange("p (t d) -> p t d", d=D),
                                  rr("bv").unsqueeze(1).broadcast_to([TC, NC, D]), ALU.add).then_inc(v_free, 1)
            elif kind == "kvm":
                b = step[1]
                u = full(step)
                if b:
                    dve.wait_ge(v_full, V_NO["o", b - 1] + 1)
                dve.tensor_tensor(kvb[:, :, :], u[:, :, 0:128], cc("mask").unsqueeze(1).broadcast_to([128, 2, 128]),
                                  ALU.mult).then_inc(v_free, 1)
            elif kind == "z":
                b = step[1]
                u = full(step)
                dve.tensor_scalar(zz[:, :, :], u[:, :, 0:TP], 1e-8, None, ALU.add).then_inc(v_free, 1)
            elif kind == "zn":
                b = step[1]
                dve.wait_ge(zr_ok, b + 1)
                link(dve.tensor_tensor(zl[:, :, :], zz[:, :, :], zr[:, :, :], ALU.mult))
                link(dve.scalar_tensor_tensor(zz[:, :, :], zl[:, :, :], 2.0, zr[:, :, :], ALU.subtract, ALU.mult))
            elif kind == "o":
                b = step[1]
                u = full(step)
                if b:
                    dve.wait_ge(o1_lo, b)
                dve.scalar_tensor_tensor(o1f[:, :, :], u[:, :, 0:TP], -1.0, zz[:, :, :], ALU.mult,
                                         ALU.mult).then_inc(v_free, 1)
                dve.wait_ge(v_free, FREE_NO[step] + 1)
            elif kind == "gate":
                b = step[1]
                u = full(step)
                lg = u[0:TC, 0, 0:NC * NE].rearrange("p (t e) -> p t e", e=NE)
                bc = [TC, NC, NE]
                if b:
                    dve.wait_ge(cw_ok, b)
                if b:
                    dve.wait_ge(v_free, FREE_NO["gate", b - 1] + 1)
                link(dve.tensor_tensor(gp[:, :, :], lg, rr("gate_b").unsqueeze(1).broadcast_to(bc), ALU.add))
                link(dve.tensor_reduce(gm[:, :], gp[:, :, :], AX, ALU.max))
                if b:
                    dve.wait_ge(ge_ok, b)
                dve.tensor_tensor(glog[:, :, :], gp[:, :, :], gm[:, :].unsqueeze(2).broadcast_to(bc),
                                  ALU.subtract).then_inc(v_free, 1)
            elif kind == "cwT":
                b = step[1]
                bc, b4 = [TC, NC, NE], [TC, NC, NE, NE]
                dve.wait_ge(ge_ok, b + 1)
                dve.wait_ge(v_free, FREE_NO["gate", b] + 1)
                link(dve.tensor_reduce(gs[:, :], ge[:, b % 2], AX, ALU.add))
                link(dve.reciprocal(gr[:, :], gs[:, :]))
                link(dve.tensor_tensor(gp[:, :, :], ge[:, b % 2], gr[:, :].unsqueeze(2).broadcast_to(bc), ALU.mult))
                p_j, p_e = gp[:, :, :].unsqueeze(2).broadcast_to(b4), gp[:, :, :].unsqueeze(3).broadcast_to(b4)
                before = rr("before").rearrange("p (e j) -> p e j", j=NE).unsqueeze(1).broadcast_to(b4)
                gt4, gq4 = (x[:, :, :].rearrange("p t (e j) -> p t e j", j=NE) for x in (gt, gq))
                link(dve.tensor_tensor(gq4, p_j, p_e, ALU.is_equal))
                link(dve.tensor_tensor(gq4, gq4, before, ALU.mult))
                link(dve.tensor_tensor(gt4, p_j, p_e, ALU.is_gt))
                link(dve.tensor_tensor(gt4, gt4, gq4, ALU.add))
                link(dve.tensor_reduce(rank[:, :, :], gt4, AX, ALU.add))
                dve.scalar_tensor_tensor(cw[:, b % 2], rank[:, :, :], 2.0, gp[:, :, :], ALU.is_lt, ALU.mult).then_inc(cw_ok, 1)
                if b == 0:
                    dve.wait_ge(s_set, 8)
                u = full(step)
                link(dve.tensor_copy(cwx[0:NE, b, :], u[0:NE, 0, 0:TP]))
                dve.tensor_tensor(cwx[64:64 + NE, b, :], u[0:NE, 0, 0:TP], cwx[0:NE, b, :].bitcast(F32),
                                  ALU.subtract).then_inc(v_free, 1)
            elif kind == "expert":
                _, b, e = step
                n = (NE + 1) * b + e
                dve.wait_ge(ma_free, n + 1)
                dve.wait_ge(mb_full, n + 1)
                g = eg if e else ehf
                if n:
                    dve.wait_ge(h_ok, n)
                for m in range(2):
                    a = C_COLS["b1"][0] + 4 * e + 2 + m
                    ins = dve.scalar_tensor_tensor(g[:, m], UP_B[:, m, 0:TP], cst[:, a:a + 1], es[:, n % 2, m],
                                                   ALU.add, ALU.mult)
                ins.then_inc(mb_free, 1)
                dve.wait_ge(mb_free, n + 1)
                if e:
                    k = NE * b + e - 1
                    dve.wait_ge(mc_full, k + 1)
                    dve.tensor_tensor(ehf[:, :, :], eg[:, :, :], CWB[:, 0:1, 0:TP].broadcast_to([128, 2, TP]),
                                      ALU.mult).then_inc(mc_free, 1)
                    dve.wait_ge(mc_free, k + 1)
                if n >= 2:
                    dve.wait_ge(down_done, n - 1)
                split(ehh[:, n % 2], ehl[:, n % 2], ehf[:, :, :], h_ok)
                if e == 0 and b:
                    finish(b - 1)
                if n == B * (NE + 1) - 1:
                    finish(b)

    ctx.close()


def _layout(x, cls_tok, w):
    f = np.float32

    def halves(a):
        a = np.asarray(a)
        return np.concatenate([a[0:128], a[128:256]], axis=1)

    patches = np.asarray(x).reshape(B, 5, 16, 8, 16, 8).transpose(1, 3, 5, 0, 2, 4).reshape(320, B, D)
    xp = np.zeros((NC * KP, B, TP), f)
    xp[0:320, :, 1:T] = patches
    xp = np.ascontiguousarray(xp.reshape(NC, KP, B, TP).transpose(1, 0, 2, 3))
    wt = np.zeros((NC * KP, D), f)
    wt[0:320] = w["L0_tok_W"]
    wt = np.ascontiguousarray(wt.reshape(NC, KP, D).transpose(1, 0, 2))

    pack = np.zeros((128, W_TOTAL), f)

    def put(name, a):
        at, n = W_COLS[name]
        assert a.shape[1] == n
        pack[0:a.shape[0], at:at + n] = a

    w = {k: np.asarray(v) for k, v in w.items()}
    put("lat", halves(np.concatenate([w["L0_attn_wk_a"].T, w["L0_attn_wv_a"].T], axis=1)))
    put("q0", halves(w["L0_attn_wq"].T))
    put("k0", w["L0_attn_wk_b"].T)
    put("v0", np.concatenate([np.zeros((64, D), f), w["L0_attn_wv_b"].T]))
    o0 = np.zeros((4, 4, 32, D), f)
    o0[:, :, 0:HD] = w["L0_attn_wo"].T.reshape(4, 4, HD, D)
    put("o0", o0.reshape(4, 128, D).transpose(1, 0, 2).reshape(128, 4 * D))
    for name, key in (("r", "L0_ffn_W_r"), ("fk", "L0_ffn_W_k"), ("fv", "L0_ffn_W_v"), ("q1", "L1_attn_Wq"),
                      ("k1", "L1_attn_Wk"), ("v1", "L1_attn_Wv"), ("o1", "L1_attn_Wo")):
        put(name, halves(w[key].T))
    eb = np.zeros((128, D), f)
    eb[0:NE] = eb[64:64 + NE] = w["L1_ffn_rb2"]
    eb[32] = w["L1_ffn_sb2"][0]
    put("eb", eb)
    put("gate", halves(w["L1_ffn_gate_w"]))
    sel = np.zeros((128, NE, 128), f)
    for e in range(NE):
        sel[e, e] = sel[64 + e, e] = 1.0
    put("sel", sel.reshape(128, NE * 128))

    experts = np.zeros((NE + 1, 128, EXPERT), f)
    w1 = np.concatenate([w["L1_ffn_sw1"], w["L1_ffn_rw1"]])
    w2 = np.concatenate([w["L1_ffn_sw2"], w["L1_ffn_rw2"]])
    b1 = np.concatenate([w["L1_ffn_sb1"], w["L1_ffn_rb1"]])
    for e in range(NE + 1):
        experts[e, :, 0:4 * D] = halves(w1[e])
        experts[e, :, 4 * D:] = halves(w2[e])

    con = np.zeros((128, C_TOTAL), f)

    def const(name, a):
        at, n = C_COLS[name]
        con[:, at:at + n] = np.asarray(a).reshape(128, n)

    inv = (1.0 / 10000.0 ** (np.arange(0, HD, 2, dtype=f) / f(HD))).astype(f)
    angle = np.repeat(np.arange(NH, dtype=f)[:, None] * inv[None, :], 2, axis=1).reshape(1, D)
    sign = np.where(np.arange(D) % 2 == 0, f(-1), f(1))
    const("cos", np.repeat(np.cos(angle), 128, axis=0))
    const("sin", np.repeat(np.sin(angle) * sign, 128, axis=0))
    block = np.arange(128) // HD
    const("mask", (block[:, None] == block[None, :]).astype(f))
    rbd = np.zeros((128, 128), f)
    for h in range(8):
        rbd[HD * h:HD * h + HD, HD * h:HD * h + HD] = w["L1_attn_R"]
    const("rbd", rbd)
    const("ident", np.eye(128, dtype=f))
    for name, key in (("mu_r", "L0_ffn_mu_r"), ("mu_k", "L0_ffn_mu_k"), ("bq", "L1_attn_bq"), ("bk", "L1_attn_bk")):
        const(name, w[key].reshape(2, 128).T)
    const("b1", b1.reshape(NE + 1, 4, 128).transpose(2, 0, 1).reshape(128, -1))

    rows = np.zeros((1, R_TOTAL), f)
    before = (np.arange(NE)[None, :] < np.arange(NE)[:, None]).astype(f)
    for name, a in (("gamma", w["L0_tok_gamma"]), ("bv", w["L1_attn_bv"]), ("bo", w["L1_attn_bo"]),
                    ("gate_b", w["L1_ffn_gate_b"]), ("before", before)):
        at, n = R_COLS[name]
        rows[0, at:at + n] = a.reshape(n)
    cls_rows = np.zeros((TC, D), f)
    cls_rows[0] = np.asarray(cls_tok).reshape(D)
    return {"patches": xp, "w_tok": wt, "rows": rows, "cls_rows": cls_rows, "consts": con,
            "weights": pack, "experts": experts}


def kernel(x, cls_tok, **w):
    import concourse.bacc as bacc
    from concourse.bass_utils import run_bass_kernel_spmd

    nc = bacc.Bacc("TRN2", target_bir_lowering=False, num_devices=1)
    arrays = _layout(x, cls_tok, w)
    args = [nc.dram_tensor(name, a.shape, F32, kind="ExternalInput").ap() for name, a in arrays.items()]
    out = nc.dram_tensor("tower_out", (B, D, TP), F32, kind="ExternalOutput").ap()
    tower(nc, *args, out)
    got = run_bass_kernel_spmd(nc, [arrays], core_ids=[0]).results[0]["tower_out"]
    return np.ascontiguousarray(got.transpose(0, 2, 1)[:, 0:T, :])
```
